# Optimizing a Trainium2 kernel written in Bass

```python
import numpy as np
import jax
import jax.numpy as jnp

def _softmax(x, axis=-1):
    return jax.nn.softmax(x, axis=axis)

def _gelu(x):
    return jax.nn.gelu(x, approximate=True)

def _silu(x):
    return jax.nn.silu(x)

def _sigmoid(x):
    return jax.nn.sigmoid(x)

def _layernorm(x, axis=-1, eps=1e-05):
    m = jnp.mean(x, axis=axis, keepdims=True)
    v = jnp.var(x, axis=axis, keepdims=True)
    return (x - m) / jnp.sqrt(v + eps)

def _scatter_add(tgt, idx, src, axis=0):
    return tgt.at[idx].add(src)

def _segment_sum(src, seg, n):
    return jax.ops.segment_sum(src, seg, n)
kernel_name = 'mk_seq_preln_d1_jaxref_r8_ece8f1'

def setup_inputs(seed: int=0):
    np.random.seed(seed)
    _w = jnp.asarray

    def _L0_attn_setup():
        import jax, jax.numpy as jnp
        import numpy as np
        import math
        N_HEAD = 16
        V_HEAD = 32
        NOPE = 32
        ROPE_D = 64
        KEEP = 32
        EPS = 1e-06

        def _freqs(T, dim=ROPE_D, theta=10000.0):
            f = 1.0 / theta ** (jnp.arange(0, dim, 2, dtype=jnp.float32) / dim)
            t = jnp.arange(T, dtype=jnp.float32)
            a = jnp.outer(t, f)
            return (jnp.cos(a), jnp.sin(a))

        def _rope(x, cos, sin):
            S = x.shape[-2]
            c = cos[:S][None, None]
            s = sin[:S][None, None]
            x1, x2 = jnp.split(x, 2, axis=-1)
            return jnp.concatenate([x1 * c - x2 * s, x1 * s + x2 * c], axis=-1)

        def _rms(x, g, eps=EPS):
            return x * jax.lax.rsqrt(jnp.mean(x * x, axis=-1, keepdims=True) + eps) * g

        def _attn(q, k, v, causal):
            scale = 1.0 / math.sqrt(q.shape[-1])
            s = jnp.einsum('bhqd,bhkd->bhqk', q, k) * scale
            if causal:
                Tq, Tk = (s.shape[-2], s.shape[-1])
                mask = jnp.tril(jnp.ones((Tq, Tk), dtype=bool))
                s = jnp.where(mask, s, jnp.finfo(s.dtype).min)
            return jnp.einsum('bhqk,bhkd->bhqd', jax.nn.softmax(s, axis=-1), v)

        def _forward(x, w_cq, g_qnorm, w_dq_nope, w_dq_rope, w_ckv, g_kvnorm, w_dk_nope, w_dv, w_krope, w_imp, w_selk, w_selv, w_wink, w_winv, w_gate, w_proj):
            B, T, C = x.shape
            cos, sin = _freqs(T)
            nq = _rms(x @ w_cq, g_qnorm)
            q_nope = (nq @ w_dq_nope).reshape(B, T, N_HEAD, NOPE).transpose(0, 2, 1, 3)
            q_rope = (nq @ w_dq_rope).reshape(B, T, N_HEAD, ROPE_D).transpose(0, 2, 1, 3)
            q_rope = _rope(q_rope, cos, sin)
            q = jnp.concatenate([q_nope, q_rope], axis=-1)
            gate = jax.nn.softmax((x @ w_gate).mean(axis=1), axis=-1)
            ckv = _rms(x @ w_ckv, g_kvnorm)
            k_nope = (ckv @ w_dk_nope).reshape(B, T, N_HEAD, NOPE).transpose(0, 2, 1, 3)
            v1 = (ckv @ w_dv).reshape(B, T, N_HEAD, V_HEAD).transpose(0, 2, 1, 3)
            k_rope = (x @ w_krope).reshape(B, T, 1, ROPE_D).transpose(0, 2, 1, 3) / N_HEAD
            k_rope = _rope(k_rope, cos, sin)
            k1 = jnp.concatenate([k_nope, jnp.broadcast_to(k_rope, (B, N_HEAD, T, ROPE_D))], axis=-1)
            scores = (x @ w_imp)[..., 0]
            _, idx = jax.lax.top_k(scores, KEEP)
            idx = jnp.sort(idx, axis=1)
            sel = jnp.take_along_axis(x, idx[:, :, None], axis=1)
            ks = (sel @ w_selk).reshape(B, KEEP, N_HEAD, NOPE + ROPE_D).transpose(0, 2, 1, 3)
            vs = (sel @ w_selv).reshape(B, KEEP, N_HEAD, V_HEAD).transpose(0, 2, 1, 3)
            ks = jnp.concatenate([ks[..., :NOPE], _rope(ks[..., NOPE:], cos, sin)], axis=-1)
            kw = (x @ w_wink).reshape(B, T, N_HEAD, NOPE + ROPE_D).transpose(0, 2, 1, 3)
            vw = (x @ w_winv).reshape(B, T, N_HEAD, V_HEAD).transpose(0, 2, 1, 3)
            kw = jnp.concatenate([kw[..., :NOPE], _rope(kw[..., NOPE:], cos, sin)], axis=-1)
            a1 = _attn(q, k1, v1, causal=True)
            a2 = _attn(q, ks, vs, causal=False)
            a3 = _attn(q, kw, vw, causal=True)
            g = gate[:, :, None, None, None]
            out = g[:, 0] * a1 + g[:, 1] * a2 + g[:, 2] * a3
            out = out.transpose(0, 2, 1, 3).reshape(B, T, N_HEAD * V_HEAD)
            return out @ w_proj
        key = jax.random.key(seed)
        ks = jax.random.split(key, 20)
        B, T, C = (2, 128, 128)
        q_lora, kv_lora = (96, 32)
        std = 0.02

        def w(k, shape):
            return jax.random.normal(k, shape, dtype=jnp.float32) * std
        return {'x': jax.random.normal(ks[0], (B, T, C), dtype=jnp.float32), 'w_cq': w(ks[1], (C, q_lora)), 'g_qnorm': jnp.ones((q_lora,), jnp.float32), 'w_dq_nope': w(ks[2], (q_lora, N_HEAD * NOPE)), 'w_dq_rope': w(ks[3], (q_lora, N_HEAD * ROPE_D)), 'w_ckv': w(ks[4], (C, kv_lora)), 'g_kvnorm': jnp.ones((kv_lora,), jnp.float32), 'w_dk_nope': w(ks[5], (kv_lora, N_HEAD * NOPE)), 'w_dv': w(ks[6], (kv_lora, N_HEAD * V_HEAD)), 'w_krope': w(ks[7], (C, ROPE_D)), 'w_imp': w(ks[8], (C, 1)), 'w_selk': w(ks[9], (C, N_HEAD * (NOPE + ROPE_D))), 'w_selv': w(ks[10], (C, N_HEAD * V_HEAD)), 'w_wink': w(ks[11], (C, N_HEAD * (NOPE + ROPE_D))), 'w_winv': w(ks[12], (C, N_HEAD * V_HEAD)), 'w_gate': w(ks[13], (C, 3)), 'w_proj': w(ks[14], (N_HEAD * V_HEAD, C))}
    _L0_attn_in = _L0_attn_setup()

    def _L0_ffn_setup():
        import jax, jax.numpy as jnp
        import numpy as np
        B, L, D = (1, 256, 128)
        E, H, G, K = (64, 32, 64, 16)

        def _grouped_routing_scores(router_scores):
            T, En = router_scores.shape
            Tq = T // G
            budget = Tq * K
            order = jnp.argsort(-router_scores, axis=0)
            sorted_vals = jnp.take_along_axis(router_scores, order, axis=0)
            group_score = sorted_vals.reshape(Tq, G, En).sum(axis=1)
            _, top_flat = jax.lax.top_k(group_score.reshape(-1), budget)
            gmask = jnp.zeros((Tq * En,), bool).at[top_flat].set(True).reshape(Tq, En)
            mask_sorted = jnp.broadcast_to(gmask[:, None, :], (Tq, G, En)).reshape(T, En)
            mask = jnp.zeros((T, En), bool).at[order, jnp.arange(En)[None, :]].set(mask_sorted)
            fs = jnp.where(mask, router_scores, 0.0)
            return fs / (fs.sum(axis=-1, keepdims=True) + 1e-06)
        key = jax.random.key(seed)
        ks = jax.random.split(key, 6)
        s = lambda k, shape, scale: jax.random.normal(k, shape, jnp.float32) * scale
        return {'x': jax.random.normal(ks[0], (B, L, D), jnp.float32), 'Wr': s(ks[1], (D, E), D ** (-0.5)), 'br': jnp.zeros((E,), jnp.float32), 'Wup': s(ks[2], (E, D, H), D ** (-0.5)), 'bup': jnp.zeros((E, H), jnp.float32), 'Wgate': s(ks[3], (E, D, H), D ** (-0.5)), 'bgate': jnp.zeros((E, H), jnp.float32), 'Wdown': s(ks[4], (E, H, D), H ** (-0.5)), 'bdown': jnp.zeros((E, D), jnp.float32)}
    _L0_ffn_in = _L0_ffn_setup()
    _d = {'L0_attn_x': _L0_attn_in['x'], 'L0_attn_w_cq': _L0_attn_in['w_cq'], 'L0_attn_g_qnorm': _L0_attn_in['g_qnorm'], 'L0_attn_w_dq_nope': _L0_attn_in['w_dq_nope'], 'L0_attn_w_dq_rope': _L0_attn_in['w_dq_rope'], 'L0_attn_w_ckv': _L0_attn_in['w_ckv'], 'L0_attn_g_kvnorm': _L0_attn_in['g_kvnorm'], 'L0_attn_w_dk_nope': _L0_attn_in['w_dk_nope'], 'L0_attn_w_dv': _L0_attn_in['w_dv'], 'L0_attn_w_krope': _L0_attn_in['w_krope'], 'L0_attn_w_imp': _L0_attn_in['w_imp'], 'L0_attn_w_selk': _L0_attn_in['w_selk'], 'L0_attn_w_selv': _L0_attn_in['w_selv'], 'L0_attn_w_wink': _L0_attn_in['w_wink'], 'L0_attn_w_winv': _L0_attn_in['w_winv'], 'L0_attn_w_gate': _L0_attn_in['w_gate'], 'L0_attn_w_proj': _L0_attn_in['w_proj'], 'L0_ffn_Wr': _L0_ffn_in['Wr'], 'L0_ffn_br': _L0_ffn_in['br'], 'L0_ffn_Wup': _L0_ffn_in['Wup'], 'L0_ffn_bup': _L0_ffn_in['bup'], 'L0_ffn_Wgate': _L0_ffn_in['Wgate'], 'L0_ffn_bgate': _L0_ffn_in['bgate'], 'L0_ffn_Wdown': _L0_ffn_in['Wdown'], 'L0_ffn_bdown': _L0_ffn_in['bdown']}
    _x0 = _d['L0_attn_x']
    _d['L0_attn_x'] = jax.random.normal(jax.random.fold_in(jax.random.key(seed), 1), (8, 512, 128), dtype=_x0.dtype)
    del _x0
    return _d

def reference(L0_attn_x, L0_attn_w_cq, L0_attn_g_qnorm, L0_attn_w_dq_nope, L0_attn_w_dq_rope, L0_attn_w_ckv, L0_attn_g_kvnorm, L0_attn_w_dk_nope, L0_attn_w_dv, L0_attn_w_krope, L0_attn_w_imp, L0_attn_w_selk, L0_attn_w_selv, L0_attn_w_wink, L0_attn_w_winv, L0_attn_w_gate, L0_attn_w_proj, L0_ffn_Wr, L0_ffn_br, L0_ffn_Wup, L0_ffn_bup, L0_ffn_Wgate, L0_ffn_bgate, L0_ffn_Wdown, L0_ffn_bdown):

    def _L0_attn_ref(x, w_cq, g_qnorm, w_dq_nope, w_dq_rope, w_ckv, g_kvnorm, w_dk_nope, w_dv, w_krope, w_imp, w_selk, w_selv, w_wink, w_winv, w_gate, w_proj):
        import jax, jax.numpy as jnp
        import numpy as np
        import math
        N_HEAD = 16
        V_HEAD = 32
        NOPE = 32
        ROPE_D = 64
        KEEP = 32
        EPS = 1e-06

        def _freqs(T, dim=ROPE_D, theta=10000.0):
            f = 1.0 / theta ** (jnp.arange(0, dim, 2, dtype=jnp.float32) / dim)
            t = jnp.arange(T, dtype=jnp.float32)
            a = jnp.outer(t, f)
            return (jnp.cos(a), jnp.sin(a))

        def _rope(x, cos, sin):
            S = x.shape[-2]
            c = cos[:S][None, None]
            s = sin[:S][None, None]
            x1, x2 = jnp.split(x, 2, axis=-1)
            return jnp.concatenate([x1 * c - x2 * s, x1 * s + x2 * c], axis=-1)

        def _rms(x, g, eps=EPS):
            return x * jax.lax.rsqrt(jnp.mean(x * x, axis=-1, keepdims=True) + eps) * g

        def _attn(q, k, v, causal):
            scale = 1.0 / math.sqrt(q.shape[-1])
            s = jnp.einsum('bhqd,bhkd->bhqk', q, k) * scale
            if causal:
                Tq, Tk = (s.shape[-2], s.shape[-1])
                mask = jnp.tril(jnp.ones((Tq, Tk), dtype=bool))
                s = jnp.where(mask, s, jnp.finfo(s.dtype).min)
            return jnp.einsum('bhqk,bhkd->bhqd', jax.nn.softmax(s, axis=-1), v)

        def _forward(x, w_cq, g_qnorm, w_dq_nope, w_dq_rope, w_ckv, g_kvnorm, w_dk_nope, w_dv, w_krope, w_imp, w_selk, w_selv, w_wink, w_winv, w_gate, w_proj):
            B, T, C = x.shape
            cos, sin = _freqs(T)
            nq = _rms(x @ w_cq, g_qnorm)
            q_nope = (nq @ w_dq_nope).reshape(B, T, N_HEAD, NOPE).transpose(0, 2, 1, 3)
            q_rope = (nq @ w_dq_rope).reshape(B, T, N_HEAD, ROPE_D).transpose(0, 2, 1, 3)
            q_rope = _rope(q_rope, cos, sin)
            q = jnp.concatenate([q_nope, q_rope], axis=-1)
            gate = jax.nn.softmax((x @ w_gate).mean(axis=1), axis=-1)
            ckv = _rms(x @ w_ckv, g_kvnorm)
            k_nope = (ckv @ w_dk_nope).reshape(B, T, N_HEAD, NOPE).transpose(0, 2, 1, 3)
            v1 = (ckv @ w_dv).reshape(B, T, N_HEAD, V_HEAD).transpose(0, 2, 1, 3)
            k_rope = (x @ w_krope).reshape(B, T, 1, ROPE_D).transpose(0, 2, 1, 3) / N_HEAD
            k_rope = _rope(k_rope, cos, sin)
            k1 = jnp.concatenate([k_nope, jnp.broadcast_to(k_rope, (B, N_HEAD, T, ROPE_D))], axis=-1)
            scores = (x @ w_imp)[..., 0]
            _, idx = jax.lax.top_k(scores, KEEP)
            idx = jnp.sort(idx, axis=1)
            sel = jnp.take_along_axis(x, idx[:, :, None], axis=1)
            ks = (sel @ w_selk).reshape(B, KEEP, N_HEAD, NOPE + ROPE_D).transpose(0, 2, 1, 3)
            vs = (sel @ w_selv).reshape(B, KEEP, N_HEAD, V_HEAD).transpose(0, 2, 1, 3)
            ks = jnp.concatenate([ks[..., :NOPE], _rope(ks[..., NOPE:], cos, sin)], axis=-1)
            kw = (x @ w_wink).reshape(B, T, N_HEAD, NOPE + ROPE_D).transpose(0, 2, 1, 3)
            vw = (x @ w_winv).reshape(B, T, N_HEAD, V_HEAD).transpose(0, 2, 1, 3)
            kw = jnp.concatenate([kw[..., :NOPE], _rope(kw[..., NOPE:], cos, sin)], axis=-1)
            a1 = _attn(q, k1, v1, causal=True)
            a2 = _attn(q, ks, vs, causal=False)
            a3 = _attn(q, kw, vw, causal=True)
            g = gate[:, :, None, None, None]
            out = g[:, 0] * a1 + g[:, 1] * a2 + g[:, 2] * a3
            out = out.transpose(0, 2, 1, 3).reshape(B, T, N_HEAD * V_HEAD)
            return out @ w_proj
        return _forward(x, w_cq, g_qnorm, w_dq_nope, w_dq_rope, w_ckv, g_kvnorm, w_dk_nope, w_dv, w_krope, w_imp, w_selk, w_selv, w_wink, w_winv, w_gate, w_proj)

    def _L0_ffn_ref(x, Wr, br, Wup, bup, Wgate, bgate, Wdown, bdown):
        import jax, jax.numpy as jnp
        import numpy as np
        B, L, D = (1, 256, 128)
        E, H, G, K = (64, 32, 64, 16)

        def _grouped_routing_scores(router_scores):
            T, En = router_scores.shape
            Tq = T // G
            budget = Tq * K
            order = jnp.argsort(-router_scores, axis=0)
            sorted_vals = jnp.take_along_axis(router_scores, order, axis=0)
            group_score = sorted_vals.reshape(Tq, G, En).sum(axis=1)
            _, top_flat = jax.lax.top_k(group_score.reshape(-1), budget)
            gmask = jnp.zeros((Tq * En,), bool).at[top_flat].set(True).reshape(Tq, En)
            mask_sorted = jnp.broadcast_to(gmask[:, None, :], (Tq, G, En)).reshape(T, En)
            mask = jnp.zeros((T, En), bool).at[order, jnp.arange(En)[None, :]].set(mask_sorted)
            fs = jnp.where(mask, router_scores, 0.0)
            return fs / (fs.sum(axis=-1, keepdims=True) + 1e-06)
        Bx, Lx, Dx = x.shape
        xt = x.reshape(-1, Dx)
        router_scores = jax.nn.softmax(xt @ Wr + br, axis=-1)
        fs = _grouped_routing_scores(router_scores)
        up = jnp.einsum('td,edh->teh', xt, Wup) + bup
        gate = jnp.einsum('td,edh->teh', xt, Wgate) + bgate
        h = jax.nn.silu(up) * gate * fs[:, :, None]
        out = jnp.einsum('teh,ehd->td', h, Wdown) + fs @ bdown
        return out.reshape(Bx, Lx, Dx)
    x = L0_attn_x
    x = x + _L0_attn_ref(_layernorm(x, axis=-1), L0_attn_w_cq, L0_attn_g_qnorm, L0_attn_w_dq_nope, L0_attn_w_dq_rope, L0_attn_w_ckv, L0_attn_g_kvnorm, L0_attn_w_dk_nope, L0_attn_w_dv, L0_attn_w_krope, L0_attn_w_imp, L0_attn_w_selk, L0_attn_w_selv, L0_attn_w_wink, L0_attn_w_winv, L0_attn_w_gate, L0_attn_w_proj)
    x = x + _L0_ffn_ref(_layernorm(x, axis=-1), L0_ffn_Wr, L0_ffn_br, L0_ffn_Wup, L0_ffn_bup, L0_ffn_Wgate, L0_ffn_bgate, L0_ffn_Wdown, L0_ffn_bdown)
    return x

_drawn_inputs = setup_inputs


def setup_inputs(seed=0):
    import zlib

    import numpy as np

    out = dict(_drawn_inputs(seed))
    spreads = {'L0_attn_g_qnorm': (1.0, 0.6),
     'L0_attn_g_kvnorm': (1.0, 0.6),
     'L0_ffn_br': (0.0, 0.304),
     'L0_ffn_bup': (0.0, 0.441),
     'L0_ffn_bgate': (0.0, 0.452),
     'L0_ffn_bdown': (0.0, 0.268)}
    factors = {'L0_attn_w_cq': 8.0,
     'L0_attn_w_dq_nope': 8.0,
     'L0_attn_w_dq_rope': 8.0,
     'L0_attn_w_ckv': 8.0,
     'L0_attn_w_dk_nope': 8.0,
     'L0_attn_w_dv': 8.0,
     'L0_attn_w_krope': 22.874,
     'L0_attn_w_imp': 5.418,
     'L0_attn_w_selk': 8.0,
     'L0_attn_w_selv': 4.951,
     'L0_attn_w_wink': 8.0,
     'L0_attn_w_winv': 8.0,
     'L0_attn_w_gate': 8.0,
     'L0_attn_w_proj': 4.631}
    for name, (base, spread) in spreads.items():
        noise = np.random.default_rng([zlib.crc32(name.encode()), seed]).standard_normal(out[name].shape)
        drawn = base * np.exp(spread * noise) if base else spread * noise
        out[name] = jnp.asarray(drawn.astype(out[name].dtype))
    for name, factor in factors.items():
        out[name] = (out[name] * factor).astype(out[name].dtype)
    return out
```

```python
from contextlib import ExitStack

import numpy as np

import concourse.bass as bass
from concourse import mybir

F32 = mybir.dt.float32
BF16 = mybir.dt.bfloat16
I32 = mybir.dt.int32
ALU = mybir.AluOpType
ACT = mybir.ActivationFunctionType
AX = mybir.AxisListType

P = 128
B, T, C = 8, 512, 128
NH, NOPE, ROPE, VD = 16, 32, 64, 32
QL, KVL, KEEP = 96, 32, 32
HD = KVL + ROPE + NOPE
KD = ROPE + NOPE
HPG = 4
NG = NH // HPG
TT = T // P
NU = HPG * TT
VA = VD + 1
EXPERTS, HID, GROUP, TOPK = 64, 32, 64, 16
NTOK = B * T
HALF = NTOK // 2
NGR = HALF // GROUP
BUDGET = NTOK // GROUP * TOPK
HT = EXPERTS * HID // P
EPT = P // HID
NBLK = B // 2
EPS_LN, EPS_RMS, EPS_DEN = 1e-5, 1e-6, 1e-6
MASKED = -1e30
TAKEN = -3.0e38
BIG = 3.0e38
RSQRT_MAGIC = float(0x5F3759DF)
SCORE_ROUNDS = [27, 23, 19, 15, 11, 7, 3, 0]
INDEX_ROUNDS = [9, 5, 1, 0]
CAND = 15

CONST = {}
_at = 0
for _name, _n in (("ident", P), ("mask", P), ("ropeC", TT * ROPE), ("ropeS", TT * ROPE), ("diag", HPG * VD),
                  ("count", KEEP), ("pair", P), ("lower", P), ("ones", P), ("half", 2), ("gidx", NGR),
                  ("irnd", len(INDEX_ROUNDS) * CAND)):
    CONST[_name] = (_at, _at + _n)
    _at += _n
NCONST = _at


ONLY = False


class Flag:

    def __init__(self, sem, per, base=0):
        self.sem, self.per, self.base = sem, per, base

    def at(self, it, n):
        return it * self.per + n + self.base


class Chain:

    def __init__(self, eng, flag, it):
        self.eng, self.flag, self.it, self.n = eng, flag, it, 0

    def __call__(self, ins):
        self.n += 1
        ins.then_inc(self.flag.sem, 1)
        self.eng.wait_ge(self.flag.sem, self.flag.at(self.it, self.n))

    def close(self):
        assert self.n == self.flag.per, (self.n, self.flag.per)


def build(nc, x, w_cat, w_imp, w_gate, g_q, g_kv, w_q, dqn_t, dkn_t, w_dv, w_wink, w_winv, w_selk, w_selv, w_proj,
          w_r, b_r, w_up, b_up, w_gt, b_gt, w_dn, b_dn, consts, bits, select, out, only_attention=False):
    with ExitStack() as ctx:
        def sb(name, shape, dt=F32):
            return ctx.enter_context(nc.sbuf_tensor(name, shape, dt))

        def flag(name, per=1, base=0):
            return Flag(ctx.enter_context(nc.semaphore(name)), per, base)

        banks = ctx.enter_context(nc.psum_tensor("banks", [P, 8, 512], F32))

        def bank(i):
            return banks[:, i, :]

        xres = sb("xres", [P, B * TT, C])
        x2nT = sb("x2nT", [P, NTOK])
        cst = sb("cst", [P, NCONST])
        cbits = sb("cbits", [P, len(SCORE_ROUNDS) * CAND], I32)
        identb = sb("identb", [P, P], BF16)
        maskb = sb("maskb", [P, P], BF16)
        wcat = sb("wcat", [P, QL + KVL + ROPE])
        wimp = sb("wimp", [P, 1])
        wgate = sb("wgate", [P, 3])
        gq = sb("gq", [QL, 1])
        k1s = sb("k1s", [P, 1])
        wide = sb("wide", [P, NH * (HD + 2 * KD + 3 * VD + QL + KVL) + NG * C])
        room = [0]

        def part(rows, cols):
            room[0] += cols
            return wide[0:rows, room[0] - cols:room[0]]

        wq = part(QL, NH * HD)
        wink = part(P, NH * KD)
        winv = part(P, NH * VD)
        wselk = part(P, NH * KD)
        wselv = part(P, NH * VD)
        dqn = part(NOPE, NH * QL)
        dkn = part(NOPE, NH * KVL)
        wdv = part(KVL, NH * VD)
        wproj = part(P, NG * C)
        room[0] = 0
        wup = part(P, HT * P)
        wgt = part(P, HT * P)
        wdn = part(P, HT * C)
        selw = part(P, HT * P).bitcast(BF16).rearrange("p (n c) -> p n c", n=2 * HT)
        wr = sb("wr", [P, EXPERTS])
        brb = sb("brb", [P, EXPERTS])
        bup = sb("bup", [P, HT])
        bgt = sb("bgt", [P, HT])
        bdn = sb("bdn", [P, 2, C])
        rtok = sb("rtok", [P, B * TT, EXPERTS])

        xc = sb("xc", [P, TT, C])
        xn = sb("xn", [P, TT, C])
        sq = sb("sq", [P, TT, C])
        st = sb("st", [P, 64])
        xnT = sb("xnT", [P, T])
        pc = sb("pc", [P, TT, QL + KVL + ROPE])
        nq = sb("nq", [P, TT, QL])
        k1 = sb("k1", [P, TT, HD])
        nqT = sb("nqT", [QL, T])
        k1T = sb("k1T", [P, T])
        top8 = sb("top8", [1, 8])
        carrier = sb("carrier", [1, 2])
        key = sb("key", [P, TT])
        selm = sb("selm", [P, TT, KEEP])
        selT = sb("selT", [P, HPG, KEEP])
        xsb = sb("xsb", [P, P])
        gl = sb("gl", [P, 16])
        g13 = sb("g13", [P, 2])
        g2 = sb("g2", [P, 1])

        qtok = sb("qtok", [P, TT, HPG, HD])
        ktok = sb("ktok", [P, TT, HPG, HD])
        ra = sb("ra", [P, TT, HPG, ROPE])
        rb = sb("rb", [P, TT, HPG, ROPE])
        qT = sb("qT", [P, HPG, T])
        imp = qT[0:1]
        k3T = sb("k3T", [P, HPG, T])
        v13 = sb("v13", [P, 2, TT, HPG, VA])
        kstok = sb("kstok", [KEEP, HPG, HD])
        ksraw = sb("ksraw", [KEEP, HPG, KD])
        ksT = sb("ksT", [P, HPG, KEEP])
        vsd = sb("vsd", [P, HPG * VD])
        prob = sb("prob", [P, 2, 2, T])
        pT = sb("pT", [P, 2, 2, T])
        nmax = sb("nmax", [P, 2, 2])
        p2 = sb("p2", [P, TT * HPG, KEEP])
        p2e = sb("p2e", [P, TT * HPG, KEEP])
        p2T = sb("p2T", [P, T])
        n2 = sb("n2", [P, 4, TT * HPG])
        o2 = sb("o2", [P, TT, HPG, VD])
        rec = sb("rec", [P, 4, TT * 2])
        onum = sb("onum", [P, 2, TT * 2, VD])
        osum = sb("osum", [P, TT, VD])
        att = sb("att", [P, TT, HPG * VD])
        attT = sb("attT", [P, T])

        sortA = qtok[:].rearrange("p a b c -> p (a b c)")
        sortB = ktok[:].rearrange("p a b c -> p (a b c)")
        score = qT[:].rearrange("p a b -> p (a b)")
        rpair = sortB
        routed = k3T[:].rearrange("p a b -> p (a b)")
        above = prob[:].rearrange("p a b c -> p (a b c)")
        equal = pT[:].rearrange("p a b c -> p (a b c)")
        gsum = sb("gsum", [P, NGR])
        glast = sb("glast", [P, NGR])
        gcmp = sb("gcmp", [P, CAND, NGR])
        gkey = sb("gkey", [P, NGR])
        gm = sb("gm", [P, 4, NGR])
        rs = sb("rs", [P, 64])
        cand = sb("cand", [P, CAND])
        cnt = sb("cnt", [P, CAND])
        found = sb("found", [P, CAND + 1])

        fblk = sb("fblk", [P, T])
        siluT = sb("siluT", [P, 2, T])
        gateT = sb("gateT", [P, 2, T])
        hT = sb("hT", [P, 2, T])
        yout = [xc, xn]
        yrec = sb("yrec", [P, 2, TT])
        fpart = sb("fpart", [P, 3, T], BF16)
        frest = [p2[:].rearrange("p a b -> p (a b)"), p2e[:].rearrange("p a b -> p (a b)")]

        rak = siluT[:].rearrange("p s (t h c) -> p (s t) h c", h=HPG, c=ROPE)
        rbk = gateT[:].rearrange("p s (t h c) -> p (s t) h c", h=HPG, c=ROPE)
        ksa = hT[0:KEEP, 0, 0:HPG * ROPE].rearrange("p (h c) -> p h c", h=HPG)
        ksb = hT[0:KEEP, 1, 0:HPG * ROPE].rearrange("p (h c) -> p h c", h=HPG)

        def K(name, rows=slice(0, P)):
            a, b = CONST[name]
            return cst[rows, a:b]

        ident = K("ident")

        ld_x, ld_w, ld_e = flag("ld_x"), flag("ld_w"), flag("ld_e")
        cast_done, zero_done = flag("cast_done"), flag("zero_done")
        pe_abs, act_abs = flag("pe_abs"), flag("act_abs")
        dve_b = flag("dve_b", 50)
        dve_b2 = flag("dve_b2", 22)
        xn_ready, pe_xnT, act_xnT = flag("xn_ready"), flag("pe_xnT"), flag("act_xnT")
        pe_cat, act_cat = flag("pe_cat"), flag("act_cat")
        k1_ready, pe_nk, act_nk = flag("k1_ready"), flag("pe_nk"), flag("act_nk")
        pe_imp, key_row, pe_key, sel_ready = flag("pe_imp"), flag("key_row"), flag("pe_key"), flag("sel_ready")
        pe_selT, selT_ready = flag("pe_selT"), flag("selT_ready")
        gates_ready = flag("gates_ready")
        xsb_ready, pe_gl, gl_ready, act_gl = flag("xsb_ready"), flag("pe_gl"), flag("gl_ready"), flag("act_gl")
        dve_g = flag("dve_g", 12)
        pe_qkv, act_qkv = flag("pe_qkv", TT), flag("act_qkv", TT)
        pe_v1, act_v1, pe_sel, act_sel, vsd_ready = (flag("pe_v1"), flag("act_v1"), flag("pe_sel"), flag("act_sel"),
                                                     flag("vsd_ready"))
        rope_ab, rope_sum = flag("rope_ab", 3), flag("rope_sum", 3)
        pe_turn, act_turn, dve_turn = flag("pe_turn", 2 * HPG), flag("act_turn", HPG), flag("dve_turn", HPG)
        pe_ksT, ksT_ready = flag("pe_ksT"), flag("ksT_ready")
        pe_s2, s2_shift, act_e2, pe_t2, p2T_ready, pe_o2, o2_ready = (
            flag("pe_s2"), flag("s2_shift"), flag("act_e2"), flag("pe_t2"), flag("p2T_ready"), flag("pe_o2"),
            flag("o2_ready"))
        scored, maxed, weighed, turned, pT_ready, summed = (
            flag("scored", NU), flag("maxed", NU), flag("weighed", NU), flag("turned", NU), flag("pT_ready", NU),
            flag("summed", NU))
        onum_ready, osum_done, att_ready = flag("onum_ready", HPG), flag("osum_done", HPG), flag("att_ready", HPG)
        pe_attT, attT_ready, pe_y, x_done = flag("pe_attT"), flag("attT_ready"), flag("pe_y"), flag("x_done", base=1)
        x2_ready, pe_x2T, act_x2T, pool_x2T = flag("x2_ready"), flag("pe_x2T"), flag("act_x2T"), flag("pool_x2T")
        pe_lg, lg_ready, act_lg, rtok_done = flag("pe_lg"), flag("lg_ready"), flag("act_lg"), flag("rtok_done")
        paired = flag("paired")
        pe_rT, act_rT, dve_r = flag("pe_rT"), flag("act_rT"), flag("dve_r")
        cnt_ready, pe_cnt = flag("cnt_ready"), flag("pe_cnt")
        routed_ready = flag("routed_ready")
        fblk_ready, fpart_ready, fsplit = (flag("fblk_ready"), flag("fpart_ready"), flag("fsplit", 4))
        pe_den = flag("pe_den", 2)
        pe_up, act_up, pe_gt, pe_f, gate_mul, h_ready, pe_dn = (
            flag("pe_up", 2 * HT), flag("act_up", 2 * HT), flag("pe_gt", 2 * HT), flag("pe_f", 2 * HT),
            flag("gate_mul", 2 * HT, base=1), flag("h_ready", 2 * HT), flag("pe_dn", 2 * HT, base=1))
        dve_e = flag("dve_e", 4)
        y_scaled, y_ready, stored = flag("y_scaled", 2, base=1), flag("y_ready", 2), flag("stored", 32, base=16)

        def wait(eng, f, it, n):
            eng.wait_ge(f.sem, f.at(it, n))

        block = ctx.enter_context(nc.Block())

        loads = [
            (cst[:], consts), (cbits[:], bits), (wcat[:], w_cat), (wimp[:], w_imp), (wgate[:], w_gate),
            (gq[:], g_q), (k1s[0:KVL, :], g_kv), (dqn, dqn_t), (dkn, dkn_t),
            (wq.rearrange("p (h d) -> p h d", h=NH)[:, :, KVL:HD], w_q),
            (wdv, w_dv), (wink, w_wink), (winv, w_winv), (wselk, w_selk), (wselv, w_selv),
            (wproj.rearrange("p (g c) -> p g c", g=NG), w_proj.rearrange("(g p) c -> p g c", p=P)),
            (wr[:], w_r), (brb[:], b_r.partition_broadcast(P)),
            (bup[:], b_up), (bgt[:], b_gt), (bdn[0:EXPERTS, 0, :], b_dn), (bdn[EXPERTS:P, 1, :], b_dn),
        ]
        loads_experts = [(wup, w_up), (wgt, w_gt), (selw, select),
                         (wdn.rearrange("p (m c) -> p m c", m=HT), w_dn.rearrange("(m p) c -> p m c", p=P))]

        @block.sync
        def _(sp):
            sp.sem_inc(stored.sem, stored.base)
            sp.dma_start(xres[:], x.rearrange("(n p) c -> p n c", p=P)).then_inc(ld_x.sem, 16)
            sp.wait_ge(zero_done.sem, 6)
            for dst, src in loads:
                sp.dma_start(dst, src).then_inc(ld_w.sem, 16)
            if only_attention:
                sp.wait_ge(x_done.sem, B * NG + x_done.base)
                sp.dma_start(out.rearrange("(n p) c -> p n c", p=P), xres[:]).then_inc(stored.sem, 16)
                sp.wait_ge(stored.sem, 32)
                return
            sp.wait_ge(x_done.sem, B * NG + x_done.base)
            for dst, src in loads_experts:
                sp.dma_start(dst, src).then_inc(ld_e.sem, 16)
            with sp.Fori(0, NBLK) as jj:
                for half in range(2):
                    wait(sp, y_ready, jj, half + 1)
                    sp.dma_start(out.rearrange("(b t p) c -> b p t c", t=TT, p=P)[half * NBLK + jj],
                                 yout[half][:]).then_inc(stored.sem, 16)
            sp.wait_ge(stored.sem, 16 * B + stored.base)

        @block.gpsimd
        def _(pool):
            pool.memset(k1[:], 0.0).then_inc(zero_done.sem, 1)
            pool.memset(ktok[:], 0.0).then_inc(zero_done.sem, 1)
            pool.memset(kstok[:], 0.0).then_inc(zero_done.sem, 1)
            pool.memset(v13[:], 1.0).then_inc(zero_done.sem, 1)
            pool.memset(k1s[:], 1.0 / NH).then_inc(zero_done.sem, 1)
            pool.memset(bdn[:], 0.0).then_inc(zero_done.sem, 1)
            with pool.Fori(0, B) as b:
                with pool.Fori(0, NG) as g:
                    it = b * NG + g
                    for n, tok, a_, b_ in ((1, qtok, ra[:], rb[:]), (2, ktok, rak, rbk)):
                        wait(pool, rope_ab, it, n)
                        pool.tensor_tensor(tok[:, :, :, KVL:KVL + ROPE].rearrange("p t h c -> p (t h) c"),
                                           a_.rearrange("p t h c -> p (t h) c"),
                                           b_.rearrange("p t h c -> p (t h) c"), ALU.add).then_inc(rope_sum.sem, 1)
                    wait(pool, rope_ab, it, 3)
                    pool.tensor_tensor(kstok[:, :, KVL:KVL + ROPE], ksa, ksb, ALU.add).then_inc(rope_sum.sem, 1)
                    for h in range(HPG):
                        wait(pool, onum_ready, it, h + 1)
                        num = onum[:, h % 2].rearrange("p (t a) v -> p t a v", a=2)
                        pool.tensor_tensor(osum[:], num[:, :, 0], num[:, :, 1], ALU.add).then_inc(osum_done.sem, 1)
                        wait(pool, osum_done, it, h + 1)
                        if h == 0:
                            wait(pool, o2_ready, it, 1)
                        pool.tensor_tensor(att[:, :, h * VD:(h + 1) * VD], osum[:], o2[:, :, h], ALU.add)\
                            .then_inc(att_ready.sem, 1)
                        wait(pool, att_ready, it, h + 1)
                if not only_attention:
                    wait(pool, act_x2T, b, 1)
                    pool.tensor_copy(x2nT[:, bass.ds(b * T, T)], attT[:]).then_inc(pool_x2T.sem, 1)
            if only_attention:
                return
            with pool.Fori(0, NBLK) as jj:
                pool.wait_ge(routed_ready.sem, 1)
                wait(pool, pe_dn, jj, 0)
                pool.tensor_copy(fblk[:], routed[:, bass.ds(jj * T, T)]).then_inc(fblk_ready.sem, 1)
                for half in range(2):
                    wait(pool, y_scaled, jj, half + 1)
                    pool.tensor_tensor(yout[half][:].rearrange("p t c -> p (t c)"),
                                       yout[half][:].rearrange("p t c -> p (t c)"),
                                       xres[:, bass.ds((half * NBLK + jj) * TT, TT), :].rearrange("p t c -> p (t c)"),
                                       ALU.add).then_inc(y_ready.sem, 1)

        @block.scalar
        def _(act):
            act.wait_ge(ld_w.sem, 16 * len(loads))
            act.wait_ge(pe_abs.sem, 1)
            act.activation(wq.rearrange("p (h d) -> p h d", h=NH)[:, :, 0:KVL],
                           bank(0)[0:QL, :].rearrange("p (h d) -> p h d", h=NH), ACT.Copy).then_inc(act_abs.sem, 1)
            with act.Fori(0, B) as b:
                wait(act, pe_xnT, b, 1)
                act.activation(xnT[:], bank(4), ACT.Copy).then_inc(act_xnT.sem, 1)
                wait(act, pe_cat, b, 1)
                act.activation(pc[:].rearrange("p (i t) c -> p i (t c)", i=2), banks[:, 0:2, 0:2 * (QL + KVL + ROPE)],
                               ACT.Copy).then_inc(act_cat.sem, 1)
                wait(act, pe_nk, b, 1)
                act.activation(k1T[:], bank(3), ACT.Copy, scale=k1s[:]).then_inc(act_nk.sem, 1)
                wait(act, gl_ready, b, 1)
                act.activation(gl[:, 4:7], gl[:, 0:3], ACT.Exp, bias=gl[:, 3:4], accum_out=gl[:, 7:8])\
                    .then_inc(act_gl.sem, 1)
                with act.Fori(0, NG) as g:
                    it = b * NG + g
                    for t in range(TT):
                        wait(act, pe_qkv, it, t + 1)
                        s = 2 * (t % 2)
                        act.activation(qtok[:, t].rearrange("p h d -> p (h d)"), bank(s), ACT.Copy)
                        act.activation(ktok[:, t, :, KVL:HD],
                                       bank(s + 1)[:, 0:HPG * KD].rearrange("p (h d) -> p h d", h=HPG), ACT.Copy)
                        act.activation(v13[:, 1, t, :, 0:VD],
                                       bank(s + 1)[:, HPG * KD:].rearrange("p (h d) -> p h d", h=HPG), ACT.Copy)\
                            .then_inc(act_qkv.sem, 1)
                    wait(act, pe_v1, it, 1)
                    act.activation(v13[:, 0].rearrange("p t h c -> p (t h) c")[:, :, 0:VD],
                                   bank(4).rearrange("p (n d) -> p n d", d=VD), ACT.Copy).then_inc(act_v1.sem, 1)
                    wait(act, pe_sel, it, 1)
                    act.activation(ksraw[:].rearrange("p h d -> p (h d)"), bank(5)[0:KEEP, 0:HPG * KD], ACT.Copy)
                    act.activation(kstok[:, :, KVL + ROPE:HD],
                                   bank(5)[0:KEEP, 0:HPG * KD].rearrange("p (h d) -> p h d", h=HPG)[:, :, ROPE:KD],
                                   ACT.Copy).then_inc(act_sel.sem, 1)
                    for h in range(HPG):
                        wait(act, pe_turn, it, 2 * h + 1)
                        act.activation(qT[:, h], bank((2 * h) % 4), ACT.Copy).then_inc(act_turn.sem, 1)
                    wait(act, s2_shift, it, 1)
                    act.activation(p2e[:], p2[:], ACT.Exp).then_inc(act_e2.sem, 1)
                    for u in range(NU):
                        W = (u % TT + 1) * P
                        wait(act, maxed, it, u + 1)
                        if u >= 2:
                            wait(act, turned, it, u - 1)
                        for a in range(2):
                            ins = act.activation(prob[:, u % 2, a, 0:W], banks[:, 2 * (u % 2) + a, 0:W], ACT.Exp,
                                                 bias=nmax[:, u % 2, a:a + 1])
                        ins.then_inc(weighed.sem, 1)
                    wait(act, pe_attT, it, 1)
                    act.activation(attT[:], bank(0), ACT.Copy).then_inc(attT_ready.sem, 1)
                if not only_attention:
                    wait(act, pe_x2T, b, 1)
                    act.activation(attT[:], bank(0), ACT.Copy).then_inc(act_x2T.sem, 1)
                    wait(act, lg_ready, b, 1)
                    act.activation(p2e[:].rearrange("p a b -> p (a b)")[:, 0:TT * EXPERTS],
                                   p2[:].rearrange("p a b -> p (a b)")[:, 0:TT * EXPERTS], ACT.Exp)\
                        .then_inc(act_lg.sem, 1)
            if only_attention:
                return
            act.wait_ge(rtok_done.sem, B)
            for s in range(2):
                act.activation(rpair.rearrange("p (n s e) -> p n s e", s=2, e=EXPERTS)[:, :, s],
                               rtok[:, s * NBLK * TT:(s + 1) * NBLK * TT], ACT.Copy).then_inc(paired.sem, 1)
            for n in range(HALF // T):
                act.wait_ge(pe_rT.sem, n + 1)
                act.activation(score[:, n * T:(n + 1) * T], bank(n), ACT.Copy).then_inc(act_rT.sem, 1)
            with act.Fori(0, NBLK) as jj:
                for n in range(2 * HT):
                    m = n % HT
                    wait(act, pe_up, jj, n + 1)
                    if n >= 2:
                        wait(act, gate_mul, jj, n - 1)
                    else:
                        wait(act, gate_mul, jj, 0)
                    act.activation(siluT[:, n % 2], bank(n % 2), ACT.Silu, bias=bup[:, m:m + 1])\
                        .then_inc(act_up.sem, 1)

        @block.tensor
        def _(pe):
            pe.sem_inc(pe_dn.sem, pe_dn.base)
            pe.wait_ge(ld_w.sem, 16 * len(loads))
            pe.wait_ge(cast_done.sem, 2)
            for h in range(NH):
                mm = pe.matmul(bank(0)[0:QL, h * KVL:(h + 1) * KVL], dqn[:, h * QL:(h + 1) * QL],
                               dkn[:, h * KVL:(h + 1) * KVL], start=True, stop=True)
            mm.then_inc(pe_abs.sem, 1)
            pe.wait_ge(act_abs.sem, 1)
            with pe.Fori(0, B) as b:
                wait(pe, xn_ready, b, 1)
                for t in range(TT):
                    mm = pe.transpose(bank(4)[:, t * P:(t + 1) * P], xn[:, t], ident)
                mm.then_inc(pe_xnT.sem, 1)
                wait(pe, act_xnT, b, 1)
                NC_ = QL + KVL + ROPE
                for t in range(TT):
                    mm = pe.matmul(banks[:, t // 2, (t % 2) * NC_:(t % 2 + 1) * NC_], xnT[:, t * P:(t + 1) * P],
                                   wcat[:], start=True, stop=True)
                mm.then_inc(pe_cat.sem, 1)
                pe.matmul(bank(5)[0:1, :], wimp[:], xnT[:], start=True, stop=True).then_inc(pe_imp.sem, 1)
                wait(pe, xsb_ready, b, 1)
                pe.matmul(bank(6)[:, 0:3], xsb[:], wgate[:], start=True, stop=True).then_inc(pe_gl.sem, 1)
                wait(pe, k1_ready, b, 1)
                for t in range(TT):
                    pe.transpose(bank(2)[0:QL, t * P:(t + 1) * P], nq[:, t], ident)
                for t in range(TT):
                    mm = pe.transpose(bank(3)[:, t * P:(t + 1) * P], k1[:, t], ident)
                mm.then_inc(pe_nk.sem, 1)
                wait(pe, key_row, b, 1)
                for t in range(TT):
                    mm = pe.matmul(bank(7)[:, t:t + 1], imp[:, 3, t * P:(t + 1) * P], K("ones", slice(0, 1))[:, 0:1],
                                   start=True, stop=True)
                mm.then_inc(pe_key.sem, 1)
                wait(pe, sel_ready, b, 1)
                for t in range(TT):
                    mm = pe.matmul(bank(5)[:, 0:KEEP], xn[:, t], selm[:, t], start=(t == 0), stop=(t == TT - 1))
                mm.then_inc(pe_selT.sem, 1)
                with pe.Fori(0, NG) as g:
                    it = b * NG + g
                    wait(pe, selT_ready, b, 1)
                    wait(pe, act_nk, b, 1)
                    for t in range(TT):
                        s = 2 * (t % 2)
                        if t >= 2:
                            wait(pe, act_qkv, it, t - 1)
                        elif t == 0:
                            wait(pe, x_done, it, 0)
                        tile = slice(t * P, (t + 1) * P)
                        pe.matmul(bank(s), nqT[:, tile], wq[:, bass.ds(g * HPG * HD, HPG * HD)], start=True, stop=True)
                        pe.matmul(bank(s + 1)[:, 0:HPG * KD], xnT[:, tile], wink[:, bass.ds(g * HPG * KD, HPG * KD)],
                                  start=True, stop=True)
                        pe.matmul(bank(s + 1)[:, HPG * KD:], xnT[:, tile], winv[:, bass.ds(g * HPG * VD, HPG * VD)],
                                  start=True, stop=True).then_inc(pe_qkv.sem, 1)
                    for t in range(TT):
                        mm = pe.matmul(bank(4)[:, t * HPG * VD:(t + 1) * HPG * VD], k1T[0:KVL, t * P:(t + 1) * P],
                                       wdv[:, bass.ds(g * HPG * VD, HPG * VD)], start=True, stop=True)
                    mm.then_inc(pe_v1.sem, 1)
                    pe.matmul(bank(5)[0:KEEP, 0:HPG * KD], selT[:, 0], wselk[:, bass.ds(g * HPG * KD, HPG * KD)],
                              start=True, stop=True)
                    pe.matmul(bank(6)[:, 0:HPG * VD], selT[:].rearrange("p h k -> p (h k)"),
                              wselv[:, bass.ds(g * HPG * VD, HPG * VD)], start=True, stop=True).then_inc(pe_sel.sem, 1)
                    wait(pe, act_qkv, it, TT)
                    for j in range(2 * HPG):
                        h = j // 2
                        if j < 2:
                            wait(pe, rope_sum, it, j + 1)
                        if j == 6:
                            wait(pe, rope_sum, it, 3)
                        if j >= 4:
                            if j % 2:
                                wait(pe, dve_turn, it, j // 2 - 1)
                            else:
                                wait(pe, act_turn, it, j // 2 - 1)
                        for t in range(TT):
                            mm = pe.transpose(bank(j % 4)[:, t * P:(t + 1) * P], (ktok if j % 2 else qtok)[:, t, h],
                                              ident)
                        mm.then_inc(pe_turn.sem, 1)
                    for h in range(HPG):
                        mm = pe.transpose(bank(7)[:, h * KEEP:(h + 1) * KEEP], kstok[:, h], ident[0:KEEP, 0:KEEP])
                    mm.then_inc(pe_ksT.sem, 1)
                    wait(pe, ksT_ready, it, 1)
                    wait(pe, act_turn, it, HPG)
                    wait(pe, dve_turn, it, HPG)
                    for t in range(TT):
                        for h in range(HPG):
                            c = (t * HPG + h) * KEEP
                            mm = pe.matmul(bank(7)[:, c:c + KEEP], qT[:, h, t * P:(t + 1) * P], ksT[:, h],
                                           start=True, stop=True)
                    mm.then_inc(pe_s2.sem, 1)

                    def scores(u):
                        h, qt = divmod(u, TT)
                        W = (qt + 1) * P
                        if u >= 2:
                            wait(pe, weighed, it, u - 1)
                        for a, keys in ((0, k1T), (1, k3T[:, h])):
                            s = 2 * (u % 2) + a
                            pe.matmul(bank(s)[:, 0:W], qT[:, h, qt * P:(qt + 1) * P], keys[:, 0:W],
                                      start=True, stop=False, skip_group_check=True)
                            mm = pe.matmul(bank(s)[:, qt * P:W], identb[:], maskb[:], start=False, stop=True,
                                           skip_group_check=True)
                        mm.then_inc(scored.sem, 1)

                    def turn(u):
                        wait(pe, weighed, it, u + 1)
                        if u >= 1:
                            wait(pe, pT_ready, it, u)
                        for a in range(2):
                            for kb in range(u % TT + 1):
                                mm = pe.transpose(bank(4 + a)[:, kb * P:(kb + 1) * P],
                                                  prob[:, u % 2, a, kb * P:(kb + 1) * P], ident)
                        mm.then_inc(turned.sem, 1)

                    def weigh_values(u):
                        h, qt = divmod(u, TT)
                        wait(pe, pT_ready, it, u + 1)
                        if qt == 0 and h >= 2:
                            wait(pe, onum_ready, it, h - 1)
                        if u == TT:
                            wait(pe, o2_ready, it, 1)
                        for a in range(2):
                            c = (qt * 2 + a) * VA
                            for kb in range(qt + 1):
                                mm = pe.matmul(bank(6 + h % 2)[:, c:c + VA], pT[:, u % 2, a, kb * P:(kb + 1) * P],
                                               v13[:, a, kb, h], start=(kb == 0), stop=(kb == qt))
                        mm.then_inc(summed.sem, 1)

                    wait(pe, vsd_ready, it, 1)
                    scores(0)
                    for u in range(NU):
                        if u + 1 < NU:
                            scores(u + 1)
                        if u == 0:
                            wait(pe, act_v1, it, 1)
                        turn(u)
                        if u == 1:
                            wait(pe, act_e2, it, 1)
                            for t in range(TT):
                                mm = pe.transpose(bank(7)[:, t * P:(t + 1) * P],
                                                  p2e[:, t * HPG:(t + 1) * HPG].rearrange("p h k -> p (h k)"), ident)
                            mm.then_inc(pe_t2.sem, 1)
                        if u == 2:
                            wait(pe, p2T_ready, it, 1)
                            for t in range(TT):
                                mm = pe.matmul(bank(7)[:, t * P:(t + 1) * P], p2T[:, t * P:(t + 1) * P], vsd[:],
                                               start=True, stop=True)
                            mm.then_inc(pe_o2.sem, 1)
                        if u >= 1:
                            weigh_values(u - 1)
                    weigh_values(NU - 1)
                    wait(pe, att_ready, it, HPG)
                    for t in range(TT):
                        mm = pe.transpose(bank(0)[:, t * P:(t + 1) * P], att[:, t], ident)
                    mm.then_inc(pe_attT.sem, 1)
                    wait(pe, attT_ready, it, 1)
                    for t in range(TT):
                        mm = pe.matmul(bank(1)[:, t * P:(t + 1) * P], attT[:, t * P:(t + 1) * P],
                                       wproj[:, bass.ds(g * C, C)], start=True, stop=True)
                    mm.then_inc(pe_y.sem, 1)
                if not only_attention:
                    wait(pe, x2_ready, b, 1)
                    for t in range(TT):
                        mm = pe.transpose(bank(0)[:, t * P:(t + 1) * P], xn[:, t], ident)
                    mm.then_inc(pe_x2T.sem, 1)
                    wait(pe, act_x2T, b, 1)
                    for t in range(TT):
                        mm = pe.matmul(bank(2)[:, t * EXPERTS:(t + 1) * EXPERTS], attT[:, t * P:(t + 1) * P], wr[:],
                                       start=True, stop=True)
                    mm.then_inc(pe_lg.sem, 1)
            if only_attention:
                return
            pe.wait_ge(paired.sem, 2)
            for n in range(HALF // P):
                mm = pe.transpose(bank(n // TT)[:, (n % TT) * P:(n % TT + 1) * P], rpair[:, n * P:(n + 1) * P], ident)
                if n % TT == TT - 1:
                    mm.then_inc(pe_rT.sem, 1)
            for n in range(len(SCORE_ROUNDS) + 1 + len(INDEX_ROUNDS)):
                width = 1 if n == len(SCORE_ROUNDS) else CAND
                pe.wait_ge(cnt_ready.sem, n + 1)
                pe.matmul(bank(4)[:, 0:width], K("ones"), cnt[:, 0:width], start=True, stop=True).then_inc(pe_cnt.sem, 1)
            n += 1
            for m in ("pair", "pair", "lower"):
                n += 1
                pe.wait_ge(cnt_ready.sem, n)
                pe.matmul(bank(4)[:, 0:1], K(m), cnt[:, 0:1], start=True, stop=True).then_inc(pe_cnt.sem, 1)
            pe.wait_ge(ld_e.sem, 16 * len(loads_experts))
            with pe.Fori(0, NBLK) as jj:
                wait(pe, fblk_ready, jj, 1)
                wait(pe, fpart_ready, jj, 1)

                def up(n):
                    half, m = divmod(n, HT)
                    s = n % 2
                    if n >= 2:
                        wait(pe, act_up, jj, n - 1)
                        wait(pe, gate_mul, jj, n - 1)
                        wait(pe, h_ready, jj, n - 1)
                    cols = bass.ds((half * NBLK + jj) * T, T)
                    pe.matmul(bank(s), wup[:, m * P:(m + 1) * P], x2nT[:, cols], start=True, stop=True)\
                        .then_inc(pe_up.sem, 1)
                    pe.matmul(bank(2 + s), wgt[:, m * P:(m + 1) * P], x2nT[:, cols], start=True, stop=True)\
                        .then_inc(pe_gt.sem, 1)
                    for i in range(3):
                        mm = pe.matmul(bank(4 + s), selw[:, n], fpart[:, i], start=(i == 0), stop=(i == 2))
                    mm.then_inc(pe_f.sem, 1)

                def down(n):
                    half, m = divmod(n, HT)
                    if m == 0:
                        wait(pe, y_scaled, jj, half)
                        for t in range(TT):
                            pe.matmul(bank(7)[:, t:t + 1], fblk[:, t * P:(t + 1) * P], K("half")[:, half:half + 1],
                                      start=True, stop=True)
                        for t in range(TT):
                            pe.matmul(bank(6)[:, t * C:(t + 1) * C], fblk[:, t * P:(t + 1) * P], bdn[:, half],
                                      start=(t == 0), stop=False, skip_group_check=True)
                    wait(pe, h_ready, jj, n + 1)
                    for t in range(TT):
                        mm = pe.matmul(bank(6)[:, t * C:(t + 1) * C], hT[:, n % 2, t * P:(t + 1) * P],
                                       wdn[:, m * C:(m + 1) * C], start=False, stop=(m == HT - 1),
                                       skip_group_check=True)
                    mm.then_inc(pe_dn.sem, 1)

                up(0)
                for n in range(2 * HT):
                    if n + 1 < 2 * HT:
                        up(n + 1)
                    down(n)

        @block.vector
        def _(dve):
            dve.wait_ge(ld_w.sem, 16 * len(loads))
            dve.tensor_copy(identb[:], ident).then_inc(cast_done.sem, 1)
            dve.tensor_copy(maskb[:], K("mask")).then_inc(cast_done.sem, 1)
            dve.memset(carrier[:], 0.0)
            for f in (x_done, gate_mul, y_scaled):
                dve.sem_inc(f.sem, f.base)
            dve.wait_ge(ld_x.sem, 16)

            def rsqrt(step, v, y, t):
                step(dve.tensor_scalar(t.bitcast(I32), v.bitcast(I32), 1, None, ALU.logical_shift_right))
                step(dve.tensor_scalar(y.bitcast(I32), t.bitcast(I32), -1.0, RSQRT_MAGIC, ALU.mult, ALU.add))
                for _ in range(3):
                    step(dve.scalar_tensor_tensor(t, y, -0.5, y, ALU.mult, ALU.mult))
                    step(dve.tensor_tensor(t, t, v, ALU.mult))
                    step(dve.scalar_tensor_tensor(y, t, 1.5, y, ALU.add, ALU.mult))

            def norm(step, src, dst):
                mean, var, y, tmp = st[:, 0:4], st[:, 4:8], st[:, 8:12], st[:, 12:16]
                step(dve.tensor_scalar(xc[:], src, 1.0, None, ALU.mult))
                step(dve.tensor_reduce(mean, xc[:], AX.X, ALU.add))
                step(dve.tensor_scalar(mean, mean, 1.0 / C, None, ALU.mult))
                step(dve.tensor_tensor(xc[:], xc[:], mean.unsqueeze(2).to_broadcast([P, TT, C]), ALU.subtract))
                step(dve.tensor_tensor(sq[:], xc[:], xc[:], ALU.mult))
                step(dve.tensor_reduce(var, sq[:], AX.X, ALU.add))
                step(dve.tensor_scalar(var, var, 1.0 / C, EPS_LN, ALU.mult, ALU.add))
                rsqrt(step, var, y, tmp)
                return dve.tensor_tensor(dst, xc[:], y.unsqueeze(2).to_broadcast([P, TT, C]), ALU.mult)

            def rope(src, cosine, sine, a, b_):
                H = ROPE // 2
                dve.tensor_tensor(a, src, cosine, ALU.mult)
                dve.tensor_tensor(b_[..., 0:H], src[..., H:ROPE], sine[..., 0:H], ALU.mult)
                return dve.tensor_tensor(b_[..., H:ROPE], src[..., 0:H], sine[..., H:ROPE], ALU.mult)

            def table(name):
                return K(name).rearrange("p (t c) -> p t c", t=TT)

            with dve.Fori(0, B) as b:
                step = Chain(dve, dve_b, b)
                rows = xres[:, bass.ds(b * TT, TT), :]
                norm(step, rows, xn[:]).then_inc(xn_ready.sem, 1)
                wait(dve, act_xnT, b, 1)
                step(dve.tensor_reduce(st[:, 16:17], xnT[:], AX.X, ALU.add))
                dve.tensor_scalar(xsb[:], K("ones"), st[:, 16:17], 1.0 / T, ALU.mult, ALU.mult)\
                    .then_inc(xsb_ready.sem, 1)
                wait(dve, act_cat, b, 1)
                step(dve.tensor_tensor(sq[:], pc[:, :, 0:QL + KVL], pc[:, :, 0:QL + KVL], ALU.mult))
                ms = st[:, 20:28]
                step(dve.tensor_reduce(ms[:, 0:4], sq[:, :, 0:QL], AX.X, ALU.add))
                step(dve.tensor_reduce(ms[:, 4:8], sq[:, :, QL:QL + KVL], AX.X, ALU.add))
                step(dve.tensor_scalar(ms[:, 0:4], ms[:, 0:4], 1.0 / QL, EPS_RMS, ALU.mult, ALU.add))
                step(dve.tensor_scalar(ms[:, 4:8], ms[:, 4:8], 1.0 / KVL, EPS_RMS, ALU.mult, ALU.add))
                rsqrt(step, ms, st[:, 28:36], st[:, 36:44])
                dve.tensor_tensor(nq[:], pc[:, :, 0:QL], st[:, 28:32].unsqueeze(2).to_broadcast([P, TT, QL]), ALU.mult)
                dve.tensor_tensor(k1[:, :, 0:KVL], pc[:, :, QL:QL + KVL],
                                  st[:, 32:36].unsqueeze(2).to_broadcast([P, TT, KVL]), ALU.mult)
                step(rope(pc[:, :, QL + KVL:], table("ropeC"), table("ropeS"), ra[:, :, 0], rb[:, :, 0]))
                dve.tensor_tensor(k1[:, :, KVL:KVL + ROPE], ra[:, :, 0], rb[:, :, 0], ALU.add)\
                    .then_inc(k1_ready.sem, 1)
                wait(dve, pe_gl, b, 1)
                step(dve.tensor_copy(gl[:, 0:3], bank(6)[:, 0:3]))
                dve.tensor_reduce(gl[:, 3:4], gl[:, 0:3], AX.X, ALU.max, negate=True).then_inc(gl_ready.sem, 1)
                wait(dve, pe_imp, b, 1)
                step(dve.tensor_copy(imp[:, 0], bank(5)[0:1, :]))
                for _ in range(KEEP // 8):
                    dve.tensor_copy(carrier[:, 0:1], carrier[:, 1:2])
                    step(dve.max(top8[:], imp[:, 0]))
                    dve.tensor_copy(carrier[:, 0:1], carrier[:, 1:2])
                    step(dve.match_replace(imp[:, 0], top8[:], imp[:, 0], TAKEN))
                step(dve.tensor_scalar(imp[:, 1], imp[:, 0], TAKEN, None, ALU.is_equal))
                step(dve.tensor_tensor_scan(imp[:, 2], imp[:, 1], imp[:, 1], 0.0, ALU.add, ALU.max))
                dve.tensor_tensor(imp[:, 3], imp[:, 2], imp[:, 1], ALU.mult).then_inc(key_row.sem, 1)
                wait(dve, pe_nk, b, 1)
                dve.tensor_scalar(nqT[:], bank(2)[0:QL, :], gq[:], float(KD) ** -0.5, ALU.mult, ALU.mult)
                wait(dve, pe_key, b, 1)
                step(dve.tensor_copy(key[:], bank(7)[:, 0:TT]))
                dve.tensor_tensor(selm[:], K("count").unsqueeze(1).to_broadcast([P, TT, KEEP]),
                                  key[:].unsqueeze(2).to_broadcast([P, TT, KEEP]), ALU.is_equal)\
                    .then_inc(sel_ready.sem, 1)
                wait(dve, pe_selT, b, 1)
                dve.tensor_copy(selT[:], bank(5)[:, 0:KEEP].unsqueeze(1).to_broadcast([P, HPG, KEEP]))\
                    .then_inc(selT_ready.sem, 1)
                wait(dve, act_gl, b, 1)
                step(dve.reciprocal(gl[:, 8:9], gl[:, 7:8]))
                dve.tensor_scalar(g13[:, 0:1], gl[:, 4:5], gl[:, 8:9], None, ALU.mult)
                dve.tensor_scalar(g2[:], gl[:, 5:6], gl[:, 8:9], None, ALU.mult)
                dve.tensor_scalar(g13[:, 1:2], gl[:, 6:7], gl[:, 8:9], None, ALU.mult).then_inc(gates_ready.sem, 1)
                step.close()

                with dve.Fori(0, NG) as g:
                    it = b * NG + g
                    step = Chain(dve, dve_g, it)
                    wait(dve, act_qkv, it, TT)
                    H = ROPE // 2
                    for tok, a_, b_ in ((qtok, ra[:], rb[:]), (ktok, rak, rbk)):
                        cs = table("ropeC").unsqueeze(2).to_broadcast([P, TT, HPG, ROPE])
                        sn = table("ropeS").unsqueeze(2).to_broadcast([P, TT, HPG, ROPE])
                        rope(tok[:, :, :, KVL:KVL + ROPE], cs, sn, a_, b_).then_inc(rope_ab.sem, 1)
                    wait(dve, act_sel, it, 1)
                    cs = table("ropeC")[0:KEEP, 0:1].to_broadcast([KEEP, HPG, ROPE])
                    sn = table("ropeS")[0:KEEP, 0:1].to_broadcast([KEEP, HPG, ROPE])
                    rope(ksraw[:, :, 0:ROPE], cs, sn, ksa, ksb).then_inc(rope_ab.sem, 1)
                    wait(dve, pe_sel, it, 1)
                    dve.tensor_tensor(vsd[:], bank(6)[:, 0:HPG * VD], K("diag"), ALU.mult).then_inc(vsd_ready.sem, 1)
                    for h in range(HPG):
                        wait(dve, pe_turn, it, 2 * h + 2)
                        dve.tensor_copy(k3T[:, h], bank((2 * h + 1) % 4)).then_inc(dve_turn.sem, 1)
                    wait(dve, pe_ksT, it, 1)
                    dve.tensor_copy(ksT[:].rearrange("p h k -> p (h k)"), bank(7)[:, 0:HPG * KEEP])\
                        .then_inc(ksT_ready.sem, 1)
                    wait(dve, pe_s2, it, 1)
                    s2 = bank(7).rearrange("p (n k) -> p n k", k=KEEP)
                    step(dve.tensor_reduce(n2[:, 0], s2, AX.X, ALU.max, negate=True))
                    dve.tensor_tensor(p2[:], s2, n2[:, 0].unsqueeze(2).to_broadcast([P, TT * HPG, KEEP]), ALU.add)\
                        .then_inc(s2_shift.sem, 1)

                    def row_max(u):
                        W = (u % TT + 1) * P
                        wait(dve, scored, it, u + 1)
                        if u >= 2:
                            wait(dve, weighed, it, u - 1)
                        dve.tensor_reduce(nmax[:, u % 2], banks[:, 2 * (u % 2):2 * (u % 2) + 2, 0:W], AX.X, ALU.max,
                                          negate=True).then_inc(maxed.sem, 1)

                    def outputs(h):
                        if h == 0:
                            wait(dve, gates_ready, b, 1)
                        wait(dve, summed, it, (h + 1) * TT)
                        if h >= 2:
                            wait(dve, osum_done, it, h - 1)
                        o = bank(6 + h % 2)[:, 0:2 * TT * VA].rearrange("p (n v) -> p n v", v=VA)
                        step(dve.reciprocal(rec[:, 0], o[:, :, VD]))
                        step(dve.tensor_tensor(rec[:, 1].rearrange("p (t a) -> p t a", a=2),
                                               rec[:, 0].rearrange("p (t a) -> p t a", a=2),
                                               g13[:].unsqueeze(1).to_broadcast([P, TT, 2]), ALU.mult))
                        dve.tensor_tensor(onum[:, h % 2], o[:, :, 0:VD],
                                          rec[:, 1].unsqueeze(2).to_broadcast([P, 2 * TT, VD]), ALU.mult)\
                            .then_inc(onum_ready.sem, 1)

                    row_max(0)
                    for u in range(NU):
                        if u + 1 < NU:
                            row_max(u + 1)
                        W = (u % TT + 1) * P
                        wait(dve, turned, it, u + 1)
                        if u >= 2:
                            wait(dve, summed, it, u - 1)
                        dve.tensor_copy(pT[:, u % 2, :, 0:W], banks[:, 4:6, 0:W]).then_inc(pT_ready.sem, 1)
                        if u == 1:
                            wait(dve, act_e2, it, 1)
                            step(dve.tensor_reduce(n2[:, 1], p2e[:], AX.X, ALU.add))
                            step(dve.reciprocal(n2[:, 2], n2[:, 1]))
                            step(dve.tensor_scalar(n2[:, 3], n2[:, 2], g2[:], None, ALU.mult))
                            wait(dve, pe_t2, it, 1)
                            dve.tensor_copy(p2T[:], bank(7)).then_inc(p2T_ready.sem, 1)
                        if u == 3:
                            wait(dve, pe_o2, it, 1)
                            dve.tensor_tensor(o2[:].rearrange("p t h v -> p (t h) v"),
                                              bank(7).rearrange("p (n v) -> p n v", v=VD),
                                              n2[:, 3].unsqueeze(2).to_broadcast([P, TT * HPG, VD]), ALU.mult)\
                                .then_inc(o2_ready.sem, 1)
                        if u >= TT and u % TT == 1:
                            outputs(u // TT - 1)
                    outputs(HPG - 1)
                    wait(dve, pe_y, it, 1)
                    wait(dve, x_done, it, 0)
                    dve.tensor_tensor(rows.rearrange("p t c -> p (t c)"), rows.rearrange("p t c -> p (t c)"), bank(1),
                                      ALU.add).then_inc(x_done.sem, 1)
                    step.close()
                if not only_attention:
                    wait(dve, x_done, b * NG + NG, 0)
                    step = Chain(dve, dve_b2, b)
                    norm(step, rows, xn[:]).then_inc(x2_ready.sem, 1)
                    lg = p2[:].rearrange("p a b -> p (a b)")[:, 0:TT * EXPERTS].rearrange("p (t e) -> p t e", t=TT)
                    le = p2e[:].rearrange("p a b -> p (a b)")[:, 0:TT * EXPERTS].rearrange("p (t e) -> p t e", t=TT)
                    wait(dve, pe_lg, b, 1)
                    step(dve.tensor_tensor(lg, bank(2)[:, 0:TT * EXPERTS].rearrange("p (t e) -> p t e", t=TT),
                                           brb[:].unsqueeze(1).to_broadcast([P, TT, EXPERTS]), ALU.add))
                    step(dve.tensor_reduce(st[:, 44:48], lg, AX.X, ALU.max))
                    dve.tensor_tensor(lg, lg, st[:, 44:48].unsqueeze(2).to_broadcast([P, TT, EXPERTS]), ALU.subtract)\
                        .then_inc(lg_ready.sem, 1)
                    wait(dve, act_lg, b, 1)
                    step(dve.tensor_reduce(st[:, 48:52], le, AX.X, ALU.add))
                    step(dve.reciprocal(st[:, 52:56], st[:, 48:52]))
                    dve.tensor_tensor(rtok[:, bass.ds(b * TT, TT), :], le,
                                      st[:, 52:56].unsqueeze(2).to_broadcast([P, TT, EXPERTS]), ALU.mult)\
                        .then_inc(rtok_done.sem, 1)
                    step.close()
            if only_attention:
                return

            step = Chain(dve, dve_r, 0)
            dve.wait_ge(act_rT.sem, HALF // T)
            bufs = [sortA, sortB]
            src, dst = score, 0
            size = 2
            while size <= HALF:
                a = src.rearrange("p (n k) -> p n k", k=size)
                o = bufs[dst].rearrange("p (n k) -> p n k", k=size)
                h = size // 2
                lo, hi = a[:, :, 0:h], a[:, :, h:size][:, :, ::-1]
                dve.tensor_tensor(o[:, :, 0:h], lo, hi, ALU.max)
                step(dve.tensor_tensor(o[:, :, h:size], lo, hi, ALU.min))
                src, dst = bufs[dst], 1 - dst
                src, dst = halvings(dve, step, src, dst, bufs, h)
                size *= 2
            other = routed
            step(dve.tensor_copy(other[0:EXPERTS, :], src[EXPERTS:P, :]))
            step(dve.tensor_copy(other[EXPERTS:P, :], src[0:EXPERTS, :]))
            dve.tensor_tensor(bufs[dst][0:EXPERTS, :], src[0:EXPERTS, :], other[0:EXPERTS, ::-1], ALU.max)
            step(dve.tensor_tensor(bufs[dst][EXPERTS:P, :], src[EXPERTS:P, :], other[EXPERTS:P, ::-1], ALU.min))
            src, dst = bufs[dst], 1 - dst
            src, dst = halvings(dve, step, src, dst, bufs, HALF)
            srt = src.rearrange("p (g k) -> p g k", k=GROUP)
            step(dve.tensor_reduce(gsum[:], srt, AX.X, ALU.add))
            step(dve.tensor_copy(glast[:], srt[:, :, GROUP - 1]))
            step(dve.memset(found[:], 0.0))
            n = 0
            for r in range(len(SCORE_ROUNDS)):
                step(dve.tensor_tensor(cand[:].bitcast(I32), cbits[:, r * CAND:(r + 1) * CAND],
                                       found[:, CAND:CAND + 1].bitcast(I32).to_broadcast([P, CAND]), ALU.bitwise_or))
                step(dve.tensor_tensor(gcmp[:], gsum[:].unsqueeze(1).to_broadcast([P, CAND, NGR]),
                                       cand[:].unsqueeze(2).to_broadcast([P, CAND, NGR]), ALU.is_ge))
                dve.tensor_reduce(cnt[:], gcmp[:], AX.X, ALU.add).then_inc(cnt_ready.sem, 1)
                n += 1
                dve.wait_ge(pe_cnt.sem, n)
                step(dve.scalar_tensor_tensor(found[:, 0:CAND], bank(4)[:, 0:CAND], float(BUDGET), cand[:],
                                              ALU.is_ge, ALU.mult))
                step(dve.tensor_reduce(found[:, CAND:CAND + 1], found[:], AX.X, ALU.max))
            kth = rs[:, 0:1]
            step(dve.tensor_copy(kth, found[:, CAND:CAND + 1]))
            step(dve.tensor_scalar(gm[:, 0], gsum[:], kth, None, ALU.is_gt))
            step(dve.tensor_scalar(gm[:, 1], gsum[:], kth, None, ALU.is_equal))
            dve.tensor_reduce(cnt[:, 0:1], gm[:, 0], AX.X, ALU.add).then_inc(cnt_ready.sem, 1)
            n += 1
            dve.wait_ge(pe_cnt.sem, n)
            room = rs[:, 1:2]
            step(dve.tensor_scalar(room, bank(4)[:, 0:1], -1.0, float(BUDGET), ALU.mult, ALU.add))
            step(dve.tensor_scalar(gkey[:], gm[:, 1], -1e6, 1e6, ALU.mult, ALU.add))
            step(dve.tensor_tensor(gkey[:], gkey[:], K("gidx"), ALU.add))
            step(dve.memset(found[:], 0.0))
            for r in range(len(INDEX_ROUNDS)):
                a = CONST["irnd"][0] + r * CAND
                step(dve.tensor_scalar(cand[:], cst[:, a:a + CAND], found[:, CAND:CAND + 1], None, ALU.add))
                step(dve.tensor_tensor(gcmp[:], gkey[:].unsqueeze(1).to_broadcast([P, CAND, NGR]),
                                       cand[:].unsqueeze(2).to_broadcast([P, CAND, NGR]), ALU.is_lt))
                dve.tensor_reduce(cnt[:], gcmp[:], AX.X, ALU.add).then_inc(cnt_ready.sem, 1)
                n += 1
                dve.wait_ge(pe_cnt.sem, n)
                step(dve.scalar_tensor_tensor(found[:, 0:CAND], bank(4)[:, 0:CAND], room, cand[:],
                                              ALU.is_le, ALU.mult))
                step(dve.tensor_reduce(found[:, CAND:CAND + 1], found[:], AX.X, ALU.max))
            step(dve.tensor_scalar(gm[:, 2], gkey[:], found[:, CAND:CAND + 1], None, ALU.is_lt))
            step(dve.tensor_tensor(gm[:, 3], gm[:, 0], gm[:, 2], ALU.add))
            dve.tensor_reduce(cnt[:, 0:1], gm[:, 3], AX.X, ALU.add).then_inc(cnt_ready.sem, 1)
            step(dve.tensor_tensor(gm[:, 0], gm[:, 3], glast[:], ALU.mult))
            step(dve.tensor_scalar(gm[:, 1], gm[:, 3], -BIG, BIG, ALU.mult, ALU.add))
            step(dve.tensor_tensor(gm[:, 2], gm[:, 0], gm[:, 1], ALU.add))
            low = rs[:, 2:3]
            step(dve.tensor_reduce(low, gm[:, 2], AX.X, ALU.min))
            step(dve.tensor_copy(rs[0:EXPERTS, 3:4], rs[EXPERTS:P, 2:3]))
            step(dve.tensor_copy(rs[EXPERTS:P, 3:4], rs[0:EXPERTS, 2:3]))
            step(dve.tensor_tensor(rs[:, 4:5], low, rs[:, 3:4], ALU.min))
            low = rs[:, 4:5]
            n += 1
            dve.wait_ge(pe_cnt.sem, n)
            step(dve.tensor_scalar(rs[:, 5:6], bank(4)[:, 0:1], float(GROUP), None, ALU.mult))
            step(dve.tensor_scalar(above, score, low, None, ALU.is_gt))
            step(dve.tensor_scalar(equal, score, low, None, ALU.is_equal))
            dve.tensor_reduce(cnt[:, 0:1], above, AX.X, ALU.add).then_inc(cnt_ready.sem, 1)
            n += 1
            dve.wait_ge(pe_cnt.sem, n)
            step(dve.tensor_tensor(rs[:, 6:7], rs[:, 5:6], bank(4)[:, 0:1], ALU.subtract))
            dve.tensor_reduce(cnt[:, 0:1], equal, AX.X, ALU.add).then_inc(cnt_ready.sem, 1)
            n += 1
            dve.wait_ge(pe_cnt.sem, n)
            step(dve.tensor_copy(rs[:, 7:8], bank(4)[:, 0:1]))
            step(dve.tensor_tensor_scan(sortA, equal, equal, rs[:, 7:8], ALU.add, ALU.max))
            step(dve.scalar_tensor_tensor(sortB, sortA, rs[:, 6:7], equal, ALU.is_le, ALU.mult))
            step(dve.tensor_tensor(sortA, sortB, above, ALU.add))
            dve.tensor_tensor(routed, sortA, score, ALU.mult).then_inc(routed_ready.sem, 1)

            with dve.Fori(0, NBLK) as jj:
                wait(dve, fblk_ready, jj, 1)
                split = Chain(dve, fsplit, jj)
                split(dve.tensor_copy(fpart[:, 0], fblk[:]))
                split(dve.tensor_tensor(frest[0], fblk[:], fpart[:, 0], ALU.subtract))
                split(dve.tensor_copy(fpart[:, 1], frest[0]))
                split(dve.tensor_tensor(frest[1], frest[0], fpart[:, 1], ALU.subtract))
                split.close()
                dve.tensor_copy(fpart[:, 2], frest[1]).then_inc(fpart_ready.sem, 1)
                step = Chain(dve, dve_e, jj)
                for n in range(2 * HT):
                    half, m = divmod(n, HT)
                    wait(dve, pe_gt, jj, n + 1)
                    wait(dve, act_up, jj, n + 1)
                    dve.scalar_tensor_tensor(gateT[:, n % 2], bank(2 + n % 2), bgt[:, m:m + 1], siluT[:, n % 2],
                                             ALU.add, ALU.mult).then_inc(gate_mul.sem, 1)
                    wait(dve, pe_f, jj, n + 1)
                    wait(dve, gate_mul, jj, n + 1)
                    if n >= 2:
                        wait(dve, pe_dn, jj, n - 1)
                    else:
                        wait(dve, pe_dn, jj, 0)
                    dve.tensor_tensor(hT[:, n % 2], gateT[:, n % 2], bank(4 + n % 2), ALU.mult)\
                        .then_inc(h_ready.sem, 1)
                    if m == HT - 1:
                        wait(dve, pe_dn, jj, n + 1)
                        wait(dve, stored, jj, 0)
                        step(dve.tensor_scalar(yrec[:, 0], bank(7)[:, 0:TT], EPS_DEN, None, ALU.add))
                        step(dve.reciprocal(yrec[:, 1], yrec[:, 0]))
                        dve.tensor_tensor(yout[half][:], bank(6).rearrange("p (t c) -> p t c", t=TT),
                                          yrec[:, 1].unsqueeze(2).to_broadcast([P, TT, C]), ALU.mult)\
                            .then_inc(y_scaled.sem, 1)
                step.close()


def halvings(dve, step, src, dst, bufs, size):
    d = size // 2
    while d >= 1:
        a = src.rearrange("p (n k) -> p n k", k=2 * d)
        o = bufs[dst].rearrange("p (n k) -> p n k", k=2 * d)
        dve.tensor_tensor(o[:, :, 0:d], a[:, :, 0:d], a[:, :, d:2 * d], ALU.max)
        step(dve.tensor_tensor(o[:, :, d:2 * d], a[:, :, 0:d], a[:, :, d:2 * d], ALU.min))
        src, dst = bufs[dst], 1 - dst
        d //= 2
    return src, dst


def constants():
    f = (np.float32(1.0) / np.float32(10000.0) ** (np.arange(0, ROPE, 2, dtype=np.float32) / np.float32(ROPE)))
    a = np.outer(np.arange(T, dtype=np.float32), f.astype(np.float32)).astype(np.float32)
    cos, sin = np.cos(a), np.sin(a)
    lane = np.arange(P)
    tiles = lambda m: m.reshape(TT, P, -1).transpose(1, 0, 2).reshape(P, -1)
    parts = {
        "ident": np.eye(P),
        "mask": np.where(lane[None, :] > lane[:, None], MASKED, 0.0),
        "ropeC": tiles(np.concatenate([cos, cos], 1)),
        "ropeS": tiles(np.concatenate([-sin, sin], 1)),
        "diag": (lane[:, None] // KEEP == lane[None, :] // VD) * 1.0,
        "count": np.tile(np.arange(1, KEEP + 1), (P, 1)),
        "pair": (lane[:, None] % EXPERTS == lane[None, :] % EXPERTS) * 1.0,
        "lower": (lane[None, :] == lane[:, None] + EXPERTS) * 1.0,
        "ones": np.ones((P, P)),
        "half": (lane[:, None] // EXPERTS == np.arange(2)[None, :]) * 1.0,
        "gidx": ((lane[:, None] // EXPERTS) * NGR + np.arange(NGR)[None, :]) * EXPERTS + lane[:, None] % EXPERTS,
        "irnd": np.tile(np.concatenate([np.arange(1, CAND + 1) << s for s in INDEX_ROUNDS]), (P, 1)),
    }
    cst = np.zeros((P, NCONST), np.float32)
    for name, (i, j) in CONST.items():
        cst[:, i:j] = parts[name]
    bits = np.tile(np.concatenate([np.arange(1, CAND + 1) << s for s in SCORE_ROUNDS]), (P, 1)).astype(np.int32)
    expert = np.arange(HT)[:, None] * EPT + lane[None, :] // HID
    one = (lane[:, None, None] % EXPERTS == expert[None]) * 1.0
    sel = np.concatenate([one * (lane[:, None, None] // EXPERTS == s) for s in range(2)], 1)
    return cst, bits, sel


def kernel(**inputs):
    import ml_dtypes
    import concourse.bacc as _bacc
    from concourse.bass_utils import run_bass_kernel_spmd as _run

    w = {k: np.asarray(v) for k, v in inputs.items()}
    A = lambda n: w["L0_attn_" + n]
    F = lambda n: w["L0_ffn_" + n]
    cst, bits, sel = constants()

    def rope_first(m):
        m = m.reshape(C, NH, KD)
        return np.concatenate([m[:, :, NOPE:], m[:, :, :NOPE]], 2).reshape(C, NH * KD)

    arrays = {
        "x": A("x").reshape(NTOK, C),
        "w_cat": np.concatenate([A("w_cq"), A("w_ckv"), A("w_krope")], 1),
        "w_imp": A("w_imp"), "w_gate": A("w_gate"),
        "g_q": A("g_qnorm").reshape(QL, 1), "g_kv": A("g_kvnorm").reshape(KVL, 1),
        "w_q": np.concatenate([A("w_dq_rope").reshape(QL, NH, ROPE), A("w_dq_nope").reshape(QL, NH, NOPE)], 2),
        "dqn_t": A("w_dq_nope").reshape(QL, NH, NOPE).transpose(2, 1, 0).reshape(NOPE, NH * QL),
        "dkn_t": A("w_dk_nope").reshape(KVL, NH, NOPE).transpose(2, 1, 0).reshape(NOPE, NH * KVL),
        "w_dv": A("w_dv"), "w_wink": rope_first(A("w_wink")), "w_winv": A("w_winv"),
        "w_selk": rope_first(A("w_selk")), "w_selv": A("w_selv"), "w_proj": A("w_proj"),
        "w_r": F("Wr"), "b_r": F("br").reshape(EXPERTS),
        "w_up": F("Wup").transpose(1, 0, 2).reshape(C, EXPERTS * HID), "b_up": F("bup").reshape(HT, P).T,
        "w_gt": F("Wgate").transpose(1, 0, 2).reshape(C, EXPERTS * HID), "b_gt": F("bgate").reshape(HT, P).T,
        "w_dn": F("Wdown").reshape(EXPERTS * HID, C), "b_dn": F("bdown"),
        "consts": cst, "bits": bits, "select": sel.astype(ml_dtypes.bfloat16),
    }
    nc = _bacc.Bacc("TRN2", target_bir_lowering=False, num_devices=1)
    args, sent = [], {}
    for name, a in arrays.items():
        a = np.ascontiguousarray(a)
        sent["in_" + name] = a
        args.append(nc.dram_tensor("in_" + name, a.shape, mybir.dt.from_np(a.dtype), kind="ExternalInput").ap())
    out = nc.dram_tensor("out_x", (NTOK, C), F32, kind="ExternalOutput").ap()
    build(nc, *args, out, only_attention=ONLY)
    r = _run(nc, [sent], core_ids=[0])
    return r.results[0]["out_x"].reshape(B, T, C)
```

```python
from contextlib import ExitStack

import numpy as np

import concourse.bass as bass
from concourse import mybir

F32 = mybir.dt.float32
BF16 = mybir.dt.bfloat16
I32 = mybir.dt.int32
ALU = mybir.AluOpType
ACT = mybir.ActivationFunctionType
AX = mybir.AxisListType

P = 128
B, T, C = 8, 512, 128
NH, NOPE, ROPE, VD = 16, 32, 64, 32
QL, KVL, KEEP = 96, 32, 32
CAT = QL + KVL + ROPE
HD = KVL + ROPE + NOPE
KD = ROPE + NOPE
HPG = 4
NG = NH // HPG
TT = T // P
NU = HPG * TT
EXPERTS, HID, GROUP, TOPK = 64, 32, 64, 16
NTOK = B * T
HALF = NTOK // 2
NGR = HALF // GROUP
BUDGET = NTOK // GROUP * TOPK
HT = EXPERTS * HID // P
EPT = P // HID
NBLK = B // 2
EPS_LN, EPS_RMS, EPS_DEN = 1e-5, 1e-6, 1e-6
MASKED = -1e30
N_P, N_S, N_T = 47, 2, 21
NARROW = NU // 2
PROJ_SLOT = [0, 1, 4, 6]
ROPE_SLOT = [1, 2, 5, 7]
TURN_SLOT = [2, 5, 7, 9]
TAKEN = -3.0e38
BIG = 3.0e38
RSQRT_MAGIC = float(0x5F3759DF)
SCORE_ROUNDS = [27, 23, 19, 15, 11, 7, 3, 0]
INDEX_ROUNDS = [9, 5, 1, 0]
CAND = 15

CONST = {}
_at = 0
for _name, _n in (("ident", P), ("mask", P), ("ropeC", TT * ROPE), ("ropeS", TT * ROPE), ("diag", HPG * VD),
                  ("count", KEEP), ("pair", P), ("lower", P), ("ones", P), ("half", 2), ("gidx", NGR),
                  ("irnd", len(INDEX_ROUNDS) * CAND)):
    CONST[_name] = (_at, _at + _n)
    _at += _n
NCONST = _at



class Flag:

    def __init__(self, sem, per, base=0):
        self.sem, self.per, self.base = sem, per, base

    def at(self, it, n):
        return it * self.per + n + self.base


class Chain:

    def __init__(self, eng, flag, it):
        self.eng, self.flag, self.it, self.n = eng, flag, it, 0

    def __call__(self, ins):
        self.n += 1
        ins.then_inc(self.flag.sem, 1)
        self.eng.wait_ge(self.flag.sem, self.flag.at(self.it, self.n))

    def close(self):
        assert self.n == self.flag.per, (self.n, self.flag.per)


def build(nc, x, w_cat, w_imp, w_gate, g_q, g_kv, w_q, dqn_t, dkn_t, w_dv, w_wink, w_winv, w_selk, w_selv, w_proj,
          w_r, b_r, w_up, b_up, w_gt, b_gt, w_dn, b_dn, consts, bits, select, out):
    with ExitStack() as ctx:
        def sb(name, shape, dt=F32):
            return ctx.enter_context(nc.sbuf_tensor(name, shape, dt))

        def flag(name, per=1, base=0):
            return Flag(ctx.enter_context(nc.semaphore(name)), per, base)

        banks = ctx.enter_context(nc.psum_tensor("banks", [P, 8, 512], F32))

        def bank(i):
            return banks[:, i, :]

        xres = sb("xres", [P, B * TT, C])
        rtok = sb("rtok", [P, B * TT, EXPERTS])
        cst = sb("cst", [P, NCONST])
        cbits = sb("cbits", [P, len(SCORE_ROUNDS) * CAND], I32)
        identb = sb("identb", [P, P], BF16)
        maskb = sb("maskb", [P, P], BF16)
        wcat = sb("wcat", [P, CAT])
        wimp = sb("wimp", [P, 1])
        wgate = sb("wgate", [P, 3])
        gq = sb("gq", [QL, 2])
        k1s = sb("k1s", [P, 1])
        wr = sb("wr", [P, EXPERTS])
        brb = sb("brb", [P, EXPERTS])
        bup = sb("bup", [P, HT])
        bgt = sb("bgt", [P, HT])
        bdn = sb("bdn", [P, 2, C])
        wide = sb("wide", [P, 3 * HT * P + HT * C])
        room = [0]

        def part(rows, cols):
            room[0] += cols
            return wide[0:rows, room[0] - cols:room[0]]

        wq = part(QL, NH * HD)
        wink = part(P, NH * KD)
        winv = part(P, NH * VD)
        wselk = part(P, NH * KD)
        wselv = part(P, NH * VD)
        wdv = part(KVL, NH * VD)
        wproj = part(P, NG * C)
        room[0] = 0
        wup = part(P, HT * P)
        wgt = part(P, HT * P)
        wdn = part(P, HT * C)
        selw = part(P, HT * P).bitcast(BF16).rearrange("p (n c) -> p n c", n=2 * HT)

        xn = sb("xn", [P, TT, C])
        sq = sb("sq", [P, TT, C])
        st = sb("st", [P, 64])
        xnT = sb("xnT", [P, T])
        pc = sb("pc", [P, TT, CAT])
        k1 = sb("k1", [P, TT, HD])
        nqT = sb("nqT", [QL, T])
        k1n = sb("k1n", [P, T])
        k1T = sb("k1T", [P, T])
        row_a = sq[0:1].rearrange("p t c -> p (t c)")
        row_b = pc[0:1].rearrange("p t c -> p (t c)")[:, 0:T]
        top8 = sb("top8", [1, 8])
        carrier = sb("carrier", [1, 2])
        key = sb("key", [P, TT])
        selm = sb("selm", [P, TT, KEEP])
        selT = sb("selT", [P, HPG, KEEP])
        xsb = sb("xsb", [P, P])
        gl = sb("gl", [P, 16])
        gate = sb("gate", [P, 3])

        qk = sb("qk", [P, 2, 2 * HPG, HD])
        ra = sb("ra", [P, 2 * HPG, ROPE])
        rb = sb("rb", [P, 2 * HPG, ROPE])
        qT = sb("qT", [P, 2, HPG, T])
        k3T = sb("k3T", [P, 2, HPG, T])
        v13 = sb("v13", [P, 2, 2, TT, HPG, VD])
        kstok = sb("kstok", [P, HPG, HD])
        ksraw = sb("ksraw", [KEEP, HPG, KD])
        ksT = sb("ksT", [P, HPG, KEEP])
        vsd = sb("vsd", [P, HPG * VD])
        p2 = sb("p2", [P, TT * HPG, KEEP])
        p2T = sb("p2T", [P, T])
        n2 = sb("n2", [P, 3, TT * HPG])
        prob = sb("prob", [P, 3, 2, T])
        probx = sb("probx", [P, 2, P])
        nmax = sb("nmax", [P, 2, 2])
        den = sb("den", [P, 2, 2])
        rec = sb("rec", [P, 2, 2])
        pTe = sb("pTe", [P, HPG, 2, (TT - 1) * P])
        pTo = sb("pTo", [P, HPG, 2, TT * P])
        attT = sb("attT", [P, T])
        x2dram = nc.dram_tensor("x2dram", (B, P, T), F32, kind="Internal").ap()

        def span(u):
            return (u // HPG + 1) * P

        def probs(u):
            if u == 3:
                return probx[:]
            return prob[:, u % 3 if u < 3 else (u - 4) % 3, :, 0:span(u)]

        def score_tiles(u):
            s = 2 * (u % 2)
            if u < NARROW:
                return bank(s).rearrange("p (a c) -> p a c", a=2)[:, :, 0:span(u)]
            return banks[:, s:s + 2, 0:span(u)]

        def turn_tiles(u):
            if u < NARROW:
                return bank(4 + u % 2).rearrange("p (a c) -> p a c", a=2)[:, :, 0:span(u)]
            return banks[:, 4:6, 0:span(u)]

        def turned_tile(qt):
            return pTo if qt % 2 else pTe

        dqn = pTo[:].rearrange("p a b c -> p (a b c)")[0:NOPE, 0:NH * QL]
        dkn = pTo[:].rearrange("p a b c -> p (a b c)")[0:NOPE, NH * QL:NH * (QL + KVL)]

        flat = lambda t: t.rearrange("p a b c -> p (a b c)")
        sortA = qT[:, 0].rearrange("p a b -> p (a b)")
        sortB = qT[:, 1].rearrange("p a b -> p (a b)")
        score = k3T[:, 0].rearrange("p a b -> p (a b)")
        rpair = sortB
        routed = k3T[:, 1].rearrange("p a b -> p (a b)")
        above = flat(pTe[:])[:, 0:HALF]
        equal = flat(prob[:])[:, 0:HALF]
        gsum = sb("gsum", [P, NGR])
        glast = sb("glast", [P, NGR])
        gcmp = p2[:].rearrange("p a b -> p (a b)")[:, 0:CAND * NGR].rearrange("p (c g) -> p c g", g=NGR)
        gkey = sb("gkey", [P, NGR])
        gm = sb("gm", [P, 4, NGR])
        rs = sb("rs", [P, 16])
        cand = sb("cand", [P, CAND])
        cnt = sb("cnt", [P, CAND])
        found = sb("found", [P, CAND + 1])

        x2nT = flat(pTo[:])
        hid = flat(pTe[:]).rearrange("p (n c) -> p n c", c=T)
        siluT, gateT, hT = hid[:, 0:2], hid[:, 2:4], hid[:, 4:6]
        fblk = p2T
        frest = [p2[:].rearrange("p a b -> p (a b)"), attT[:]]
        fpart = prob[:, 0].rearrange("p a b -> p (a b)").bitcast(BF16)[:, 0:3 * T].rearrange("p (i c) -> p i c", i=3)
        yout = [xn, sq]
        yrec = sb("yrec", [P, 2, TT])

        def K(name, rows=slice(0, P)):
            a, b = CONST[name]
            return cst[rows, a:b]

        ident = K("ident")

        ld_x, ld_w, ld_e = flag("ld_x"), flag("ld_w"), flag("ld_e")
        cast_done, zero_done = flag("cast_done"), flag("zero_done")
        pe_abs, act_abs, gq_ready = flag("pe_abs"), flag("act_abs"), flag("gq_ready")
        dve_p = flag("dve_p", N_P)
        xn_ready, pe_xnT, act_xnT = flag("xn_ready"), flag("pe_xnT"), flag("act_xnT")
        pe_cat, act_cat = flag("pe_cat", 2), flag("act_cat", 2)
        k1_ab, k1_ready = flag("k1_ab"), flag("k1_ready")
        pe_nq, act_nq, pe_k1, act_k1, k1T_ready = (flag("pe_nq"), flag("act_nq"), flag("pe_k1"), flag("act_k1"),
                                                   flag("k1T_ready"))
        pe_imp, imp_read, key_row, pe_key, sel_ready = (flag("pe_imp"), flag("imp_read"), flag("key_row"),
                                                        flag("pe_key"), flag("sel_ready"))
        pe_selT, selT_ready = flag("pe_selT"), flag("selT_ready")
        xsb_ready, pe_gl, gl_read, gl_ready, act_gl, gates_ready = (
            flag("xsb_ready"), flag("pe_gl"), flag("gl_read"), flag("gl_ready"), flag("act_gl"), flag("gates_ready"))
        dve_s = flag("dve_s", N_S)
        pe_q, act_q, pe_k, act_k = flag("pe_q", TT), flag("act_q", TT), flag("pe_k", TT), flag("act_k", TT)
        rope_ab, rope_sum = flag("rope_ab", TT), flag("rope_sum", TT)
        pe_tq, act_tq, pe_tk, act_tk = flag("pe_tq", TT), flag("act_tq", TT), flag("pe_tk", TT), flag("act_tk", TT)
        pe_v3, act_v3, pe_v1, act_v1 = flag("pe_v3"), flag("act_v3"), flag("pe_v1"), flag("act_v1")
        pe_sel, act_sel, vsd_ready, ks_ab, ks_sum, pe_ksT, act_ksT = (
            flag("pe_sel"), flag("act_sel"), flag("vsd_ready"), flag("ks_ab"), flag("ks_sum"), flag("pe_ksT"),
            flag("act_ksT"))
        pe_s2T, act_s2T, pe_s2, s2_shift, act_e2, n2_ready, p2_ready, pe_t2, act_t2 = (
            flag("pe_s2T"), flag("act_s2T"), flag("pe_s2"), flag("s2_shift"), flag("act_e2"), flag("n2_ready"),
            flag("p2_ready"), flag("pe_t2"), flag("act_t2"))
        scored, maxed, weighed, rec_ready, normed, turned, pT_ready = (
            flag("scored", NU), flag("maxed", NU), flag("weighed", NU), flag("rec_ready", NU), flag("normed", NU),
            flag("turned", NU), flag("pT_ready", NU))
        summed, pe_osel, att_ready, pe_y, x_done = (flag("summed", TT), flag("pe_osel"), flag("att_ready"),
                                                    flag("pe_y"), flag("x_done"))
        dve_t = flag("dve_t", N_T)
        x2_ready, pe_x2T, act_x2T, spilled = flag("x2_ready"), flag("pe_x2T"), flag("act_x2T"), flag("spilled", 16)
        lg_read = flag("lg_read")
        pe_lg, lg_ready, act_lg, rtok_done = flag("pe_lg"), flag("lg_ready"), flag("act_lg"), flag("rtok_done")
        paired = flag("paired")
        pe_rT, act_rT, dve_r = flag("pe_rT"), flag("act_rT"), flag("dve_r")
        cnt_ready, pe_cnt = flag("cnt_ready"), flag("pe_cnt")
        routed_ready = flag("routed_ready")
        fblk_ready, fpart_ready, fsplit = (flag("fblk_ready"), flag("fpart_ready"), flag("fsplit", 4))
        pe_den = flag("pe_den", 2)
        pe_up, act_up, pe_gt, pe_f, gate_mul, h_ready, pe_dn = (
            flag("pe_up", 2 * HT), flag("act_up", 2 * HT), flag("pe_gt", 2 * HT), flag("pe_f", 2 * HT),
            flag("gate_mul", 2 * HT, base=1), flag("h_ready", 2 * HT), flag("pe_dn", 2 * HT, base=1))
        dve_e = flag("dve_e", 4)
        y_scaled, y_ready, stored = flag("y_scaled", 2, base=1), flag("y_ready", 2), flag("stored", 32, base=16)

        block = ctx.enter_context(nc.Block())

        loads = [
            (cst[:], consts), (cbits[:], bits), (wcat[:], w_cat), (wimp[:], w_imp), (wgate[:], w_gate),
            (gq[:, 0:1], g_q), (k1s[0:KVL, :], g_kv), (dqn, dqn_t), (dkn, dkn_t),
            (wq.rearrange("p (h d) -> p h d", h=NH)[:, :, KVL:HD], w_q),
            (wdv, w_dv), (wink, w_wink), (winv, w_winv), (wselk, w_selk), (wselv, w_selv),
            (wproj.rearrange("p (g c) -> p g c", g=NG), w_proj.rearrange("(g p) c -> p g c", p=P)),
            (wr[:], w_r), (brb[:], b_r.partition_broadcast(P)),
            (bup[:], b_up), (bgt[:], b_gt), (bdn[0:EXPERTS, 0, :], b_dn), (bdn[EXPERTS:P, 1, :], b_dn),
        ]
        loads_experts = [(wup, w_up), (wgt, w_gt), (selw, select),
                         (wdn.rearrange("p (m c) -> p m c", m=HT), w_dn.rearrange("(m p) c -> p m c", p=P))]

        @block.sync
        def _(sp):
            sp.sem_inc(stored.sem, stored.base)
            sp.dma_start(xres[:], x.rearrange("(n p) c -> p n c", p=P)).then_inc(ld_x.sem, 16)
            sp.wait_ge(zero_done.sem, 5)
            for dst, src in loads:
                sp.dma_start(dst, src).then_inc(ld_w.sem, 16)

            def spill(tb):
                sp.wait_ge(act_x2T.sem, act_x2T.at(tb, 1))
                sp.dma_start(x2dram[tb], attT[:]).then_inc(spilled.sem, 16)

            with sp.Fori(1, B) as b:
                spill(b - 1)
            spill(B - 1)
            sp.wait_ge(spilled.sem, 16 * B)
            sp.wait_ge(x_done.sem, B * NG)
            sp.dma_start(x2nT.rearrange("p (b c) -> p b c", b=B), x2dram.rearrange("b p c -> p b c"))\
                .then_inc(ld_e.sem, 16)
            for dst, src in loads_experts:
                sp.dma_start(dst, src).then_inc(ld_e.sem, 16)
            with sp.Fori(0, NBLK) as jj:
                for half in range(2):
                    sp.wait_ge(y_ready.sem, y_ready.at(jj, half + 1))
                    sp.dma_start(out.rearrange("(b t p) c -> b p t c", t=TT, p=P)[half * NBLK + jj],
                                 yout[half][:]).then_inc(stored.sem, 16)
            sp.wait_ge(stored.sem, 16 * B + stored.base)

        @block.gpsimd
        def _(pool):
            pool.memset(k1[:], 0.0).then_inc(zero_done.sem, 1)
            pool.memset(qk[:], 0.0).then_inc(zero_done.sem, 1)
            pool.memset(kstok[:], 0.0).then_inc(zero_done.sem, 1)
            pool.memset(k1s[:], 1.0 / NH).then_inc(zero_done.sem, 1)
            pool.memset(bdn[:], 0.0).then_inc(zero_done.sem, 1)

            def normalise(it, u):
                pool.wait_ge(rec_ready.sem, rec_ready.at(it, u + 1))
                p = probs(u)
                pool.tensor_tensor(p, p, rec[:, u % 2].unsqueeze(2).to_broadcast([P, 2, span(u)]), ALU.mult)\
                    .then_inc(normed.sem, 1)

            def sum_heads(S, t):
                pool.wait_ge(rope_ab.sem, rope_ab.at(S, t + 1))
                pool.tensor_tensor(qk[:, t % 2, :, KVL:KVL + ROPE], ra[:], rb[:], ALU.add).then_inc(rope_sum.sem, 1)

            def sum_selected(S):
                pool.wait_ge(ks_ab.sem, ks_ab.at(S, 1))
                pool.tensor_tensor(kstok[0:KEEP, :, KVL:KVL + ROPE], ra[0:KEEP, 0:HPG], rb[0:KEEP, 0:HPG], ALU.add)\
                    .then_inc(ks_sum.sem, 1)

            def sum_shared(pb):
                pool.wait_ge(k1_ab.sem, k1_ab.at(pb, 1))
                pool.tensor_tensor(k1[:, :, KVL:KVL + ROPE], ra[:, 0:TT], rb[:, 0:TT], ALU.add)\
                    .then_inc(k1_ready.sem, 1)

            def normalise_selected(S):
                pool.wait_ge(n2_ready.sem, n2_ready.at(S, 1))
                pool.tensor_tensor(p2[:], p2[:], n2[:, 2].unsqueeze(2).to_broadcast([P, TT * HPG, KEEP]), ALU.mult)\
                    .then_inc(p2_ready.sem, 1)

            def group(b, g, first, last):
                it = b * NG + g
                for u in range(NU):
                    if u > 0:
                        normalise(it, u - 1)
                    elif not (first and g == 0):
                        normalise(it - 1, NU - 1)
                    if last and g == NG - 1:
                        continue
                    if u in ROPE_SLOT:
                        sum_heads(it + 1, ROPE_SLOT.index(u))
                    if u == 9:
                        sum_selected(it + 1)
                    if u == 13 and g == 2 and not last:
                        sum_shared(b + 1)
                    if u == 14:
                        normalise_selected(it + 1)

            sum_shared(0)
            for t in range(TT):
                sum_heads(0, t)
            sum_selected(0)
            normalise_selected(0)
            for g in range(NG):
                group(0, g, True, False)
            with pool.Fori(1, B - 1) as b:
                for g in range(NG):
                    group(b, g, False, False)
            for g in range(NG):
                group(B - 1, g, False, True)
            normalise(B * NG - 1, NU - 1)

            with pool.Fori(0, NBLK) as jj:
                pool.wait_ge(routed_ready.sem, 1)
                pool.wait_ge(pe_dn.sem, pe_dn.at(jj, 0))
                pool.tensor_copy(fblk[:], routed[:, bass.ds(jj * T, T)]).then_inc(fblk_ready.sem, 1)
                for half in range(2):
                    pool.wait_ge(y_scaled.sem, y_scaled.at(jj, half + 1))
                    pool.tensor_tensor(yout[half][:].rearrange("p t c -> p (t c)"),
                                       yout[half][:].rearrange("p t c -> p (t c)"),
                                       xres[:, bass.ds((half * NBLK + jj) * TT, TT), :].rearrange("p t c -> p (t c)"),
                                       ALU.add).then_inc(y_ready.sem, 1)

        @block.scalar
        def _(act):
            act.wait_ge(ld_w.sem, 16 * len(loads))
            act.wait_ge(pe_abs.sem, 1)
            act.activation(wq.rearrange("p (h d) -> p h d", h=NH)[:, :, 0:KVL],
                           bank(0)[0:QL, :].rearrange("p (h d) -> p h d", h=NH), ACT.Copy).then_inc(act_abs.sem, 1)
            side = bank(7)

            def xnT_out(pb):
                act.wait_ge(pe_xnT.sem, pe_xnT.at(pb, 1))
                act.activation(xnT[:], side, ACT.Copy).then_inc(act_xnT.sem, 1)

            def cat_out(pb, i):
                act.wait_ge(pe_cat.sem, pe_cat.at(pb, i + 1))
                act.activation(pc[:, 2 * i:2 * i + 2].rearrange("p t c -> p (t c)"), side[:, 0:2 * CAT], ACT.Copy)\
                    .then_inc(act_cat.sem, 1)

            def nq_out(pb):
                if isinstance(pb, int) and pb == 0:
                    act.wait_ge(gq_ready.sem, 1)
                act.wait_ge(pe_nq.sem, pe_nq.at(pb, 1))
                act.activation(nqT[:], side[0:QL, :], ACT.Copy, scale=gq[:, 1:2]).then_inc(act_nq.sem, 1)

            def k1_out(pb):
                act.wait_ge(pe_k1.sem, pe_k1.at(pb, 1))
                act.activation(k1n[:], side, ACT.Copy, scale=k1s[:]).then_inc(act_k1.sem, 1)

            def shared_keys(batch):
                act.wait_ge(act_k1.sem, act_k1.at(batch, 1))
                act.activation(k1T[:], k1n[:], ACT.Copy).then_inc(k1T_ready.sem, 1)

            def gate_exp(pb):
                act.wait_ge(gl_ready.sem, gl_ready.at(pb, 1))
                act.activation(gl[:, 4:7], gl[:, 0:3], ACT.Exp, bias=gl[:, 3:4], accum_out=gl[:, 7:8])\
                    .then_inc(act_gl.sem, 1)

            def q_out(S, t):
                act.wait_ge(pe_q.sem, pe_q.at(S, t + 1))
                act.activation(qk[:, t % 2, 0:HPG].rearrange("p h d -> p (h d)"), side, ACT.Copy)\
                    .then_inc(act_q.sem, 1)

            def k_out(S, t):
                act.wait_ge(pe_k.sem, pe_k.at(S, t + 1))
                act.activation(qk[:, t % 2, HPG:, KVL:HD],
                               bank(1)[:, 0:HPG * KD].rearrange("p (h d) -> p h d", h=HPG), ACT.Copy)\
                    .then_inc(act_k.sem, 1)

            def tq_out(S, t, par):
                act.wait_ge(pe_tq.sem, pe_tq.at(S, t + 1))
                act.activation(qT[:, par, :, t * P:(t + 1) * P], side.rearrange("p (h c) -> p h c", h=HPG), ACT.Copy)\
                    .then_inc(act_tq.sem, 1)

            def tk_out(S, t, par):
                act.wait_ge(pe_tk.sem, pe_tk.at(S, t + 1))
                src = side if t == 3 else bank(1)
                act.activation(k3T[:, par, :, t * P:(t + 1) * P], src.rearrange("p (h c) -> p h c", h=HPG), ACT.Copy)\
                    .then_inc(act_tk.sem, 1)

            def v3_out(S, par, batch):
                act.wait_ge(gates_ready.sem, gates_ready.at(batch, 1))
                act.wait_ge(pe_v3.sem, pe_v3.at(S, 1))
                act.activation(v13[:, par, 1].rearrange("p t h c -> p (t h c)"), side, ACT.Copy, scale=gate[:, 2:3])\
                    .then_inc(act_v3.sem, 1)

            def v1_out(S, par):
                act.wait_ge(pe_v1.sem, pe_v1.at(S, 1))
                act.activation(v13[:, par, 0].rearrange("p t h c -> p (t h c)"), bank(1), ACT.Copy, scale=gate[:, 0:1])\
                    .then_inc(act_v1.sem, 1)

            def sel_out(S):
                act.wait_ge(pe_sel.sem, pe_sel.at(S, 1))
                act.activation(ksraw[:].rearrange("p h d -> p (h d)"), side[0:KEEP, 0:HPG * KD], ACT.Copy)
                act.activation(kstok[0:KEEP, :, KVL + ROPE:HD],
                               side[0:KEEP, 0:HPG * KD].rearrange("p (h d) -> p h d", h=HPG)[:, :, ROPE:KD],
                               ACT.Copy).then_inc(act_sel.sem, 1)

            def ksT_out(S):
                act.wait_ge(pe_ksT.sem, pe_ksT.at(S, 1))
                act.activation(ksT[:], side.rearrange("p (h k) -> p h k", h=HPG)[:, :, 0:KEEP], ACT.Copy)\
                    .then_inc(act_ksT.sem, 1)

            def s2T_out(S):
                act.wait_ge(pe_s2T.sem, pe_s2T.at(S, 1))
                act.activation(p2[:].rearrange("p n k -> p (n k)"), side, ACT.Copy).then_inc(act_s2T.sem, 1)

            def selected_exp(S):
                act.wait_ge(s2_shift.sem, s2_shift.at(S, 1))
                act.activation(p2[:], p2[:], ACT.Exp).then_inc(act_e2.sem, 1)

            def t2_out(S):
                act.wait_ge(pe_t2.sem, pe_t2.at(S, 1))
                act.activation(p2T[:], side, ACT.Copy).then_inc(act_t2.sem, 1)

            def exponentials(it, u, first):
                act.wait_ge(maxed.sem, maxed.at(it, u + 1))
                if u >= 3:
                    act.wait_ge(turned.sem, turned.at(it, u - 2))
                elif not first:
                    act.wait_ge(turned.sem, turned.at(it - 1, NU + u - 2))
                for a in range(2):
                    ins = act.activation(probs(u)[:, a], score_tiles(u)[:, a], ACT.Exp,
                                         bias=nmax[:, u % 2, a:a + 1], accum_out=den[:, u % 2, a:a + 1])
                ins.then_inc(weighed.sem, 1)

            def att_out(it, tb=None):
                act.wait_ge(summed.sem, summed.at(it, TT))
                if tb is not None:
                    act.wait_ge(spilled.sem, spilled.at(tb, 16))
                act.activation(attT[:], bank(6), ACT.Copy).then_inc(att_ready.sem, 1)

            def x2T_out(tb):
                act.wait_ge(pe_x2T.sem, pe_x2T.at(tb, 1))
                act.activation(attT[:], side, ACT.Copy).then_inc(act_x2T.sem, 1)

            def router_exp(tb):
                act.wait_ge(lg_ready.sem, lg_ready.at(tb, 1))
                act.activation(sq[:, 2:4], sq[:, 0:2], ACT.Exp).then_inc(act_lg.sem, 1)

            def group(b, g, first, last):
                it = b * NG + g
                S, par = it + 1, (g + 1) % 2
                sides = not (last and g == NG - 1)
                batch = b + (g == NG - 1)
                for u in range(NU):
                    if sides:
                        if u in (0, 1, 4, 6):
                            q_out(S, PROJ_SLOT.index(u))
                        if u in (2, 5, 7, 9):
                            tq_out(S, TURN_SLOT.index(u), par)
                        if u == 3:
                            v3_out(S, par, batch)
                        if u == 8:
                            sel_out(S)
                        if u == 10:
                            tk_out(S, 3, par)
                        if u == 11:
                            s2T_out(S)
                        if g == 2 and not last:
                            if u == 14:
                                nq_out(b + 1)
                            if u == 15:
                                k1_out(b + 1)
                    if u == NU - 1 and g == NG - 1 and not last:
                        act.wait_ge(scored.sem, scored.at(it, NU))
                        shared_keys(b + 1)
                    exponentials(it, u, first and g == 0)
                    if sides:
                        if u in PROJ_SLOT:
                            k_out(S, PROJ_SLOT.index(u))
                        if u in (2, 5, 7):
                            tk_out(S, TURN_SLOT.index(u), par)
                        if u == 3:
                            v1_out(S, par)
                        if u == 10:
                            ksT_out(S)
                        if u == 13:
                            selected_exp(S)
                        if u == 15:
                            t2_out(S)
                        if g == 2 and not last:
                            if u == 8:
                                xnT_out(b + 1)
                            if u == 9:
                                cat_out(b + 1, 0)
                            if u == 10:
                                cat_out(b + 1, 1)
                            if u == 12:
                                gate_exp(b + 1)
                        if g == 0 and not first:
                            if u == 12:
                                x2T_out(b - 1)
                            if u == 14:
                                router_exp(b - 1)
                    if u == 3 and not (first and g == 0):
                        att_out(it - 1, b - 1 if g == 1 and not first else None)

            xnT_out(0)
            cat_out(0, 0)
            cat_out(0, 1)
            gate_exp(0)
            nq_out(0)
            k1_out(0)
            shared_keys(0)
            for t in range(TT):
                q_out(0, t)
                k_out(0, t)
                tq_out(0, t, 0)
                tk_out(0, t, 0)
            v3_out(0, 0, 0)
            v1_out(0, 0)
            sel_out(0)
            ksT_out(0)
            s2T_out(0)
            selected_exp(0)
            t2_out(0)
            for g in range(NG):
                group(0, g, True, False)
            with act.Fori(1, B - 1) as b:
                for g in range(NG):
                    group(b, g, False, False)
            for g in range(NG):
                group(B - 1, g, False, True)
            att_out(B * NG - 1)
            x2T_out(B - 1)
            router_exp(B - 1)

            act.wait_ge(rtok_done.sem, B)
            for s in range(2):
                act.activation(rpair.rearrange("p (n s e) -> p n s e", s=2, e=EXPERTS)[:, :, s],
                               rtok[:, s * NBLK * TT:(s + 1) * NBLK * TT], ACT.Copy).then_inc(paired.sem, 1)
            for n in range(HALF // T):
                act.wait_ge(pe_rT.sem, n + 1)
                act.activation(score[:, n * T:(n + 1) * T], bank(n), ACT.Copy).then_inc(act_rT.sem, 1)
            with act.Fori(0, NBLK) as jj:
                for n in range(2 * HT):
                    m = n % HT
                    act.wait_ge(pe_up.sem, pe_up.at(jj, n + 1))
                    if n >= 2:
                        act.wait_ge(gate_mul.sem, gate_mul.at(jj, n - 1))
                    else:
                        act.wait_ge(gate_mul.sem, gate_mul.at(jj, 0))
                    act.activation(siluT[:, n % 2], bank(n % 2), ACT.Silu, bias=bup[:, m:m + 1])\
                        .then_inc(act_up.sem, 1)

        @block.tensor
        def _(pe):
            pe.sem_inc(pe_dn.sem, pe_dn.base)
            pe.wait_ge(ld_w.sem, 16 * len(loads))
            pe.wait_ge(cast_done.sem, 2)
            for h in range(NH):
                mm = pe.matmul(bank(0)[0:QL, h * KVL:(h + 1) * KVL], dqn[:, h * QL:(h + 1) * QL],
                               dkn[:, h * KVL:(h + 1) * KVL], start=True, stop=True)
            mm.then_inc(pe_abs.sem, 1)
            pe.wait_ge(act_abs.sem, 1)
            side, side_b, side_c = bank(7), bank(1), bank(3)

            def tile(t):
                return slice(t * P, (t + 1) * P)

            def xnT_in(pb):
                pe.wait_ge(xn_ready.sem, xn_ready.at(pb, 1))
                for t in range(TT):
                    mm = pe.transpose(side[:, tile(t)], xn[:, t], ident)
                mm.then_inc(pe_xnT.sem, 1)

            def cat_in(pb, i):
                for t in range(2):
                    mm = pe.matmul(side[:, t * CAT:(t + 1) * CAT], xnT[:, tile(2 * i + t)], wcat[:],
                                   start=True, stop=True)
                mm.then_inc(pe_cat.sem, 1)

            def gate_in(pb):
                pe.wait_ge(xsb_ready.sem, xsb_ready.at(pb, 1))
                pe.matmul(side[:, 0:3], xsb[:], wgate[:], start=True, stop=True).then_inc(pe_gl.sem, 1)

            def imp_in(pb):
                pe.matmul(side[0:1, :], wimp[:], xnT[:], start=True, stop=True).then_inc(pe_imp.sem, 1)

            def nq_in(pb):
                pe.wait_ge(k1_ab.sem, k1_ab.at(pb, 1))
                for t in range(TT):
                    mm = pe.transpose(side[0:QL, tile(t)], pc[:, t, 0:QL], ident)
                mm.then_inc(pe_nq.sem, 1)

            def k1_in(pb):
                pe.wait_ge(k1_ready.sem, k1_ready.at(pb, 1))
                for t in range(TT):
                    mm = pe.transpose(side[:, tile(t)], k1[:, t], ident)
                mm.then_inc(pe_k1.sem, 1)

            def key_in(pb):
                pe.wait_ge(key_row.sem, key_row.at(pb, 1))
                for t in range(TT):
                    mm = pe.matmul(side_c[:, t:t + 1], row_a[:, tile(t)], K("ones", slice(0, 1))[:, 0:1],
                                   start=True, stop=True)
                mm.then_inc(pe_key.sem, 1)

            def selT_in(pb):
                pe.wait_ge(sel_ready.sem, sel_ready.at(pb, 1))
                for t in range(TT):
                    mm = pe.matmul(side_c[:, 0:KEEP], xn[:, t], selm[:, t], start=(t == 0), stop=(t == TT - 1))
                mm.then_inc(pe_selT.sem, 1)

            def q_in(S, t, gn, batch):
                if gn == 0 and t == 0:
                    pe.wait_ge(act_nq.sem, act_nq.at(batch, 1))
                pe.matmul(side, nqT[:, tile(t)], wq[:, gn * HPG * HD:(gn + 1) * HPG * HD], start=True, stop=True)\
                    .then_inc(pe_q.sem, 1)

            def k_in(S, t, gn):
                pe.matmul(side_b[:, 0:HPG * KD], xnT[:, tile(t)], wink[:, gn * HPG * KD:(gn + 1) * HPG * KD],
                          start=True, stop=True).then_inc(pe_k.sem, 1)

            def tq_in(S, t):
                pe.wait_ge(rope_sum.sem, rope_sum.at(S, t + 1))
                for h in range(HPG):
                    mm = pe.transpose(side[:, tile(h)], qk[:, t % 2, h], ident)
                mm.then_inc(pe_tq.sem, 1)

            def tk_in(S, t):
                dst = side if t == 3 else side_b
                for h in range(HPG):
                    mm = pe.transpose(dst[:, tile(h)], qk[:, t % 2, HPG + h], ident)
                mm.then_inc(pe_tk.sem, 1)

            def v3_in(S, gn):
                for t in range(TT):
                    mm = pe.matmul(side[:, tile(t)], xnT[:, tile(t)], winv[:, gn * HPG * VD:(gn + 1) * HPG * VD],
                                   start=True, stop=True)
                mm.then_inc(pe_v3.sem, 1)

            def v1_in(S, gn, batch):
                pe.wait_ge(act_k1.sem, act_k1.at(batch, 1))
                for t in range(TT):
                    mm = pe.matmul(side_b[:, tile(t)], k1n[0:KVL, tile(t)], wdv[:, gn * HPG * VD:(gn + 1) * HPG * VD],
                                   start=True, stop=True)
                mm.then_inc(pe_v1.sem, 1)

            def sel_in(S, gn, batch):
                pe.wait_ge(selT_ready.sem, selT_ready.at(batch, 1))
                pe.matmul(side[0:KEEP, 0:HPG * KD], selT[:, 0], wselk[:, gn * HPG * KD:(gn + 1) * HPG * KD],
                          start=True, stop=True)
                pe.matmul(side[:, HPG * KD:], selT[:].rearrange("p h k -> p (h k)"),
                          wselv[:, gn * HPG * VD:(gn + 1) * HPG * VD], start=True, stop=True).then_inc(pe_sel.sem, 1)

            def ksT_in(S):
                pe.wait_ge(ks_sum.sem, ks_sum.at(S, 1))
                for h in range(HPG):
                    mm = pe.transpose(side[:, tile(h)], kstok[:, h], ident)
                mm.then_inc(pe_ksT.sem, 1)

            def s2T_in(S, par):
                pe.wait_ge(act_ksT.sem, act_ksT.at(S, 1))
                pe.wait_ge(act_tq.sem, act_tq.at(S, TT))
                for h in range(HPG):
                    mm = pe.matmul(side[h * KEEP:(h + 1) * KEEP, :], ksT[:, h], qT[:, par, h], start=True, stop=True,
                                   tile_position=(0, h * KEEP))
                mm.then_inc(pe_s2T.sem, 1)

            def s2_in(S):
                pe.wait_ge(act_s2T.sem, act_s2T.at(S, 1))
                for t in range(TT):
                    mm = pe.transpose(side[:, tile(t)], p2[:, t * HPG:(t + 1) * HPG].rearrange("p h k -> p (h k)"),
                                      ident)
                mm.then_inc(pe_s2.sem, 1)

            def t2_in(S):
                pe.wait_ge(p2_ready.sem, p2_ready.at(S, 1))
                for t in range(TT):
                    mm = pe.transpose(side[:, tile(t)], p2[:, t * HPG:(t + 1) * HPG].rearrange("p h k -> p (h k)"),
                                      ident)
                mm.then_inc(pe_t2.sem, 1)

            def scores(it, b, g, u, first):
                qt, h = divmod(u, HPG)
                W, par = span(u), g % 2
                if u == 0:
                    pe.wait_ge(act_tk.sem, act_tk.at(it, TT))
                    if g == 0:
                        pe.wait_ge(k1T_ready.sem, k1T_ready.at(b, 1))
                if u >= 2:
                    pe.wait_ge(weighed.sem, weighed.at(it, u - 1))
                elif not first:
                    pe.wait_ge(weighed.sem, weighed.at(it - 1, NU + u - 1))
                out_ = score_tiles(u)
                for a, keys in ((0, k1T), (1, k3T[:, par, h])):
                    pe.matmul(out_[:, a], qT[:, par, h, tile(qt)], keys[:, 0:W],
                              start=True, stop=False, skip_group_check=True)
                    mm = pe.matmul(out_[:, a, tile(qt)], identb[:], maskb[:], start=False, stop=True,
                                   skip_group_check=True)
                mm.then_inc(scored.sem, 1)

            def turn(it, u, very_first=False):
                pe.wait_ge(normed.sem, normed.at(it, u + 1))
                if u > NARROW:
                    pe.wait_ge(pT_ready.sem, pT_ready.at(it, u))
                elif u >= 2:
                    pe.wait_ge(pT_ready.sem, pT_ready.at(it, u if u == NARROW else u - 1))
                elif not very_first:
                    pe.wait_ge(pT_ready.sem, pT_ready.at(it - 1, NU))
                for a in range(2):
                    for kb in range(u // HPG + 1):
                        mm = pe.transpose(turn_tiles(u)[:, a, tile(kb)], probs(u)[:, a, tile(kb)], ident)
                mm.then_inc(turned.sem, 1)

            def weigh_selected(it, first):
                pe.wait_ge(vsd_ready.sem, vsd_ready.at(it, 1))
                pe.wait_ge(act_t2.sem, act_t2.at(it, 1))
                if not first:
                    pe.wait_ge(att_ready.sem, att_ready.at(it - 1, 1))
                pe.matmul(bank(6), vsd[:], p2T[:], start=True, stop=False, skip_group_check=True)\
                    .then_inc(pe_osel.sem, 1)

            def weigh_values(it, g, qt):
                pe.wait_ge(pT_ready.sem, pT_ready.at(it, (qt + 1) * HPG))
                pe.wait_ge(act_v1.sem, act_v1.at(it, 1))
                for a in range(2):
                    for kb in range(qt + 1):
                        for h in range(HPG):
                            mm = pe.matmul(bank(6)[h * VD:(h + 1) * VD, tile(qt)], v13[:, g % 2, a, kb, h],
                                           turned_tile(qt)[:, h, a, tile(kb)], start=False,
                                           stop=(a == 1 and kb == qt), skip_group_check=True,
                                           tile_position=(0, h * VD))
                mm.then_inc(summed.sem, 1)

            def project(it, g):
                pe.wait_ge(att_ready.sem, att_ready.at(it, 1))
                for t in range(TT):
                    mm = pe.matmul(side_c[:, tile(t)], attT[:, tile(t)], wproj[:, g * C:(g + 1) * C],
                                   start=True, stop=True)
                mm.then_inc(pe_y.sem, 1)

            def x2T_in(tb):
                pe.wait_ge(x2_ready.sem, x2_ready.at(tb, 1))
                for t in range(TT):
                    mm = pe.transpose(side[:, tile(t)], xn[:, t], ident)
                mm.then_inc(pe_x2T.sem, 1)

            def router_in(tb):
                pe.wait_ge(act_x2T.sem, act_x2T.at(tb, 1))
                for t in range(TT):
                    mm = pe.matmul(side[:, t * EXPERTS:(t + 1) * EXPERTS], attT[:, tile(t)], wr[:],
                                   start=True, stop=True)
                mm.then_inc(pe_lg.sem, 1)

            def group(b, g, first, last):
                it = b * NG + g
                S, gn, par = it + 1, (g + 1) % NG, (g + 1) % 2
                batch = b + (g == NG - 1)
                sides = not (last and g == NG - 1)
                start = first and g == 0
                opening = g == 2 and not last
                closing = g == 0 and not first
                for u in range(NU):
                    if u == 8 and sides:
                        pe.wait_ge(act_tk.sem, act_tk.at(S, 3))
                    if u == 9 and sides and g == 3:
                        pe.wait_ge(selT_ready.sem, selT_ready.at(b + 1, 1))
                    elif u == 9 and not start:
                        pe.wait_ge(x_done.sem, x_done.at(it - 1, 1))
                    scores(it, b, g, u, start)
                    if sides:
                        if u == 0:
                            pe.wait_ge(act_t2.sem, act_t2.at(it, 1))
                            q_in(S, 0, gn, batch)
                        if u == 1:
                            pe.wait_ge(act_q.sem, act_q.at(S, 1))
                            q_in(S, 1, gn, batch)
                        if u == 2:
                            pe.wait_ge(act_q.sem, act_q.at(S, 2))
                            tq_in(S, 0)
                        if u == 3:
                            pe.wait_ge(act_tq.sem, act_tq.at(S, 1))
                            v3_in(S, gn)
                        if u == 4:
                            pe.wait_ge(act_v3.sem, act_v3.at(S, 1))
                            q_in(S, 2, gn, batch)
                        if u == 5:
                            pe.wait_ge(act_q.sem, act_q.at(S, 3))
                            tq_in(S, 1)
                        if u == 6:
                            pe.wait_ge(act_tq.sem, act_tq.at(S, 2))
                            q_in(S, 3, gn, batch)
                        if u == 7:
                            pe.wait_ge(act_q.sem, act_q.at(S, 4))
                            tq_in(S, 2)
                        if u == 8:
                            pe.wait_ge(act_tq.sem, act_tq.at(S, 3))
                            sel_in(S, gn, batch)
                        if u == 9:
                            if opening:
                                pe.wait_ge(act_xnT.sem, act_xnT.at(b + 1, 1))
                            else:
                                pe.wait_ge(vsd_ready.sem, vsd_ready.at(S, 1))
                            tq_in(S, 3)
                        if u == 10:
                            if opening:
                                pe.wait_ge(act_cat.sem, act_cat.at(b + 1, 1))
                            else:
                                pe.wait_ge(act_tq.sem, act_tq.at(S, 4))
                            tk_in(S, 3)
                        if u == 11:
                            if opening:
                                pe.wait_ge(act_cat.sem, act_cat.at(b + 1, 2))
                            else:
                                pe.wait_ge(act_ksT.sem, act_ksT.at(S, 1))
                            s2T_in(S, par)
                    if opening:
                        if u == 13:
                            pe.wait_ge(s2_shift.sem, s2_shift.at(S, 1))
                            imp_in(b + 1)
                        if u == 14:
                            pe.wait_ge(imp_read.sem, imp_read.at(b + 1, 1))
                            nq_in(b + 1)
                        if u == 15:
                            pe.wait_ge(act_nq.sem, act_nq.at(b + 1, 1))
                            k1_in(b + 1)
                    if u >= 2:
                        turn(it, u - 2, start)
                    elif not start:
                        turn(it - 1, NU + u - 2)
                    if u % HPG == 2:
                        if u >= 6:
                            weigh_values(it, g, (u - 6) // HPG)
                        elif not start:
                            weigh_values(it - 1, g + 1, TT - 1)
                    if u == 5:
                        weigh_selected(it, start)
                    if sides:
                        if u == 0:
                            pe.wait_ge(act_v1.sem, act_v1.at(it, 1))
                            k_in(S, 0, gn)
                        if u == 1:
                            pe.wait_ge(act_k.sem, act_k.at(S, 1))
                            k_in(S, 1, gn)
                        if u == 2:
                            pe.wait_ge(act_k.sem, act_k.at(S, 2))
                            tk_in(S, 0)
                        if u == 3:
                            pe.wait_ge(act_tk.sem, act_tk.at(S, 1))
                            v1_in(S, gn, batch)
                        if u == 4:
                            pe.wait_ge(act_v1.sem, act_v1.at(S, 1))
                            k_in(S, 2, gn)
                        if u == 5:
                            pe.wait_ge(act_k.sem, act_k.at(S, 3))
                            tk_in(S, 1)
                        if u == 6:
                            pe.wait_ge(act_tk.sem, act_tk.at(S, 2))
                            k_in(S, 3, gn)
                        if u == 7:
                            pe.wait_ge(act_k.sem, act_k.at(S, 4))
                            tk_in(S, 2)
                        if u == 10:
                            pe.wait_ge(act_tk.sem, act_tk.at(S, 4))
                            ksT_in(S)
                        if u == 12:
                            if opening:
                                pe.wait_ge(gl_read.sem, gl_read.at(b + 1, 1))
                            else:
                                pe.wait_ge(act_s2T.sem, act_s2T.at(S, 1))
                            s2_in(S)
                    if opening:
                        if u == 8:
                            pe.wait_ge(vsd_ready.sem, vsd_ready.at(S, 1))
                            xnT_in(b + 1)
                        if u == 9:
                            pe.wait_ge(act_tq.sem, act_tq.at(S, 4))
                            cat_in(b + 1, 0)
                        if u == 10:
                            pe.wait_ge(act_ksT.sem, act_ksT.at(S, 1))
                            cat_in(b + 1, 1)
                        if u == 11:
                            pe.wait_ge(act_s2T.sem, act_s2T.at(S, 1))
                            gate_in(b + 1)
                    if closing:
                        if u == 12:
                            pe.wait_ge(s2_shift.sem, s2_shift.at(S, 1))
                            x2T_in(b - 1)
                        if u == 13:
                            router_in(b - 1)
                    if u == 15 and sides:
                        if opening:
                            pe.wait_ge(act_k1.sem, act_k1.at(b + 1, 1))
                        elif closing:
                            pe.wait_ge(lg_read.sem, lg_read.at(b - 1, 1))
                        else:
                            pe.wait_ge(s2_shift.sem, s2_shift.at(S, 1))
                        t2_in(S)
                    if u == 4 and not start:
                        project(it - 1, (g - 1) % NG)
                    if sides and g == 3:
                        if u == 5:
                            pe.wait_ge(x_done.sem, x_done.at(it - 1, 1))
                            key_in(b + 1)
                        if u == 6:
                            selT_in(b + 1)

            xnT_in(0)
            pe.wait_ge(act_xnT.sem, act_xnT.at(0, 1))
            cat_in(0, 0)
            pe.wait_ge(act_cat.sem, act_cat.at(0, 1))
            cat_in(0, 1)
            pe.wait_ge(act_cat.sem, act_cat.at(0, 2))
            gate_in(0)
            pe.wait_ge(gl_read.sem, gl_read.at(0, 1))
            imp_in(0)
            pe.wait_ge(imp_read.sem, imp_read.at(0, 1))
            nq_in(0)
            pe.wait_ge(act_nq.sem, act_nq.at(0, 1))
            k1_in(0)
            pe.wait_ge(act_k1.sem, act_k1.at(0, 1))
            for t in range(TT):
                if t > 0:
                    pe.wait_ge(act_tq.sem, act_tq.at(0, t))
                q_in(0, t, 0, 0)
                if t > 0:
                    pe.wait_ge(act_tk.sem, act_tk.at(0, t))
                k_in(0, t, 0)
                pe.wait_ge(act_q.sem, act_q.at(0, t + 1))
                tq_in(0, t)
                pe.wait_ge(act_k.sem, act_k.at(0, t + 1))
                if t == TT - 1:
                    pe.wait_ge(act_tq.sem, act_tq.at(0, TT))
                tk_in(0, t)
            v1_in(0, 0, 0)
            pe.wait_ge(act_tk.sem, act_tk.at(0, TT))
            v3_in(0, 0)
            key_in(0)
            selT_in(0)
            pe.wait_ge(act_v3.sem, act_v3.at(0, 1))
            sel_in(0, 0, 0)
            pe.wait_ge(vsd_ready.sem, vsd_ready.at(0, 1))
            ksT_in(0)
            s2T_in(0, 0)
            s2_in(0)
            pe.wait_ge(s2_shift.sem, s2_shift.at(0, 1))
            t2_in(0)
            for g in range(NG):
                group(0, g, True, False)
            with pe.Fori(1, B - 1) as b:
                for g in range(NG):
                    group(b, g, False, False)
            for g in range(NG):
                group(B - 1, g, False, True)
            it = B * NG - 1
            turn(it, NU - 2)
            turn(it, NU - 1)
            weigh_values(it, NG - 1, TT - 1)
            project(it, NG - 1)
            x2T_in(B - 1)
            router_in(B - 1)

            pe.wait_ge(paired.sem, 2)
            for n in range(HALF // P):
                mm = pe.transpose(bank(n // TT)[:, (n % TT) * P:(n % TT + 1) * P], rpair[:, n * P:(n + 1) * P], ident)
                if n % TT == TT - 1:
                    mm.then_inc(pe_rT.sem, 1)
            for n in range(len(SCORE_ROUNDS) + 1 + len(INDEX_ROUNDS)):
                width = 1 if n == len(SCORE_ROUNDS) else CAND
                pe.wait_ge(cnt_ready.sem, n + 1)
                pe.matmul(bank(4)[:, 0:width], K("ones"), cnt[:, 0:width], start=True, stop=True).then_inc(pe_cnt.sem, 1)
            n += 1
            for m in ("pair", "pair", "lower"):
                n += 1
                pe.wait_ge(cnt_ready.sem, n)
                pe.matmul(bank(4)[:, 0:1], K(m), cnt[:, 0:1], start=True, stop=True).then_inc(pe_cnt.sem, 1)
            pe.wait_ge(ld_e.sem, 16 * (len(loads_experts) + 1))
            with pe.Fori(0, NBLK) as jj:
                pe.wait_ge(fblk_ready.sem, fblk_ready.at(jj, 1))
                pe.wait_ge(fpart_ready.sem, fpart_ready.at(jj, 1))

                def up(n):
                    half, m = divmod(n, HT)
                    s = n % 2
                    if n >= 2:
                        pe.wait_ge(act_up.sem, act_up.at(jj, n - 1))
                        pe.wait_ge(gate_mul.sem, gate_mul.at(jj, n - 1))
                        pe.wait_ge(h_ready.sem, h_ready.at(jj, n - 1))
                    cols = bass.ds((half * NBLK + jj) * T, T)
                    pe.matmul(bank(s), wup[:, m * P:(m + 1) * P], x2nT[:, cols], start=True, stop=True)\
                        .then_inc(pe_up.sem, 1)
                    pe.matmul(bank(2 + s), wgt[:, m * P:(m + 1) * P], x2nT[:, cols], start=True, stop=True)\
                        .then_inc(pe_gt.sem, 1)
                    for i in range(3):
                        mm = pe.matmul(bank(4 + s), selw[:, n], fpart[:, i], start=(i == 0), stop=(i == 2))
                    mm.then_inc(pe_f.sem, 1)

                def down(n):
                    half, m = divmod(n, HT)
                    if m == 0:
                        pe.wait_ge(y_scaled.sem, y_scaled.at(jj, half))
                        for t in range(TT):
                            pe.matmul(bank(7)[:, t:t + 1], fblk[:, t * P:(t + 1) * P], K("half")[:, half:half + 1],
                                      start=True, stop=True)
                        for t in range(TT):
                            pe.matmul(bank(6)[:, t * C:(t + 1) * C], fblk[:, t * P:(t + 1) * P], bdn[:, half],
                                      start=(t == 0), stop=False, skip_group_check=True)
                    pe.wait_ge(h_ready.sem, h_ready.at(jj, n + 1))
                    for t in range(TT):
                        mm = pe.matmul(bank(6)[:, t * C:(t + 1) * C], hT[:, n % 2, t * P:(t + 1) * P],
                                       wdn[:, m * C:(m + 1) * C], start=False, stop=(m == HT - 1),
                                       skip_group_check=True)
                    mm.then_inc(pe_dn.sem, 1)

                up(0)
                for n in range(2 * HT):
                    if n + 1 < 2 * HT:
                        up(n + 1)
                    down(n)

        @block.vector
        def _(dve):
            dve.wait_ge(ld_w.sem, 16 * len(loads))
            dve.tensor_copy(identb[:], ident).then_inc(cast_done.sem, 1)
            dve.tensor_copy(maskb[:], K("mask")).then_inc(cast_done.sem, 1)
            dve.memset(carrier[:], 0.0)
            dve.tensor_scalar(gq[:, 1:2], gq[:, 0:1], float(KD) ** -0.5, None, ALU.mult).then_inc(gq_ready.sem, 1)
            for f in (gate_mul, y_scaled):
                dve.sem_inc(f.sem, f.base)
            dve.wait_ge(ld_x.sem, 16)
            side = bank(7)

            def rsqrt(step, v, y, t, parts=(0, 1)):
                if 0 in parts:
                    step(dve.tensor_scalar(t.bitcast(I32), v.bitcast(I32), 1, None, ALU.logical_shift_right))
                    step(dve.tensor_scalar(y.bitcast(I32), t.bitcast(I32), -1.0, RSQRT_MAGIC, ALU.mult, ALU.add))
                for _ in range((0 in parts) + 2 * (1 in parts)):
                    step(dve.scalar_tensor_tensor(t, y, -0.5, y, ALU.mult, ALU.mult))
                    step(dve.tensor_tensor(t, t, v, ALU.mult))
                    step(dve.scalar_tensor_tensor(y, t, 1.5, y, ALU.add, ALU.mult))

            def norm(step, rows, k, ready):
                mean, var, y, tmp = st[:, 0:4], st[:, 4:8], st[:, 8:12], st[:, 12:16]
                if k == 0:
                    step(dve.tensor_scalar(xn[:], rows, 1.0, None, ALU.mult))
                    step(dve.tensor_reduce(mean, xn[:], AX.X, ALU.add))
                if k == 1:
                    step(dve.tensor_scalar(mean, mean, 1.0 / C, None, ALU.mult))
                    step(dve.tensor_tensor(xn[:], xn[:], mean.unsqueeze(2).to_broadcast([P, TT, C]), ALU.subtract))
                if k == 2:
                    step(dve.tensor_tensor(sq[:], xn[:], xn[:], ALU.mult))
                    step(dve.tensor_reduce(var, sq[:], AX.X, ALU.add))
                if k == 3:
                    step(dve.tensor_scalar(var, var, 1.0 / C, EPS_LN, ALU.mult, ALU.add))
                    rsqrt(step, var, y, tmp, (0,))
                if k == 4:
                    rsqrt(step, var, y, tmp, (1,))
                if k == 5:
                    dve.tensor_tensor(xn[:], xn[:], y.unsqueeze(2).to_broadcast([P, TT, C]), ALU.mult)\
                        .then_inc(ready.sem, 1)

            def rope(src, cosine, sine, a, b_):
                H = ROPE // 2
                dve.tensor_tensor(a, src, cosine, ALU.mult)
                dve.tensor_tensor(b_[..., 0:H], src[..., H:ROPE], sine[..., 0:H], ALU.mult)
                return dve.tensor_tensor(b_[..., H:ROPE], src[..., 0:H], sine[..., H:ROPE], ALU.mult)

            def table(name):
                return K(name).rearrange("p (t c) -> p t c", t=TT)

            def rows_of(batch):
                return xres[:, bass.ds(batch * TT, TT), :]

            def mean_of_batch(step, pb):
                dve.wait_ge(act_xnT.sem, act_xnT.at(pb, 1))
                step(dve.tensor_reduce(st[:, 16:17], xnT[:], AX.X, ALU.add))
                dve.tensor_scalar(xsb[:], K("ones"), st[:, 16:17], 1.0 / T, ALU.mult, ALU.mult)\
                    .then_inc(xsb_ready.sem, 1)

            ms = st[:, 20:28]

            def squares(step, pb):
                dve.wait_ge(act_cat.sem, act_cat.at(pb, 2))
                step(dve.tensor_tensor(sq[:], pc[:, :, 0:QL + KVL], pc[:, :, 0:QL + KVL], ALU.mult))
                step(dve.tensor_reduce(ms[:, 0:4], sq[:, :, 0:QL], AX.X, ALU.add))
                step(dve.tensor_reduce(ms[:, 4:8], sq[:, :, QL:QL + KVL], AX.X, ALU.add))

            def roots(step):
                step(dve.tensor_scalar(ms[:, 0:4], ms[:, 0:4], 1.0 / QL, EPS_RMS, ALU.mult, ALU.add))
                step(dve.tensor_scalar(ms[:, 4:8], ms[:, 4:8], 1.0 / KVL, EPS_RMS, ALU.mult, ALU.add))
                rsqrt(step, ms, st[:, 28:36], st[:, 36:44])

            def latents(pb):
                if not (isinstance(pb, int) and pb == 0):
                    dve.wait_ge(ks_sum.sem, ks_sum.at(pb * NG - 1, 1))
                dve.tensor_tensor(pc[:, :, 0:QL], pc[:, :, 0:QL], st[:, 28:32].unsqueeze(2).to_broadcast([P, TT, QL]),
                                  ALU.mult)
                dve.tensor_tensor(k1[:, :, 0:KVL], pc[:, :, QL:QL + KVL],
                                  st[:, 32:36].unsqueeze(2).to_broadcast([P, TT, KVL]), ALU.mult)
                rope(pc[:, :, QL + KVL:], table("ropeC"), table("ropeS"), ra[:, 0:TT], rb[:, 0:TT])\
                    .then_inc(k1_ab.sem, 1)

            def gate_logits(step, pb):
                dve.wait_ge(pe_gl.sem, pe_gl.at(pb, 1))
                dve.tensor_copy(gl[:, 0:3], side[:, 0:3]).then_inc(gl_read.sem, 1)
                dve.wait_ge(gl_read.sem, gl_read.at(pb, 1))
                dve.tensor_reduce(gl[:, 3:4], gl[:, 0:3], AX.X, ALU.max, negate=True).then_inc(gl_ready.sem, 1)

            def gates(step, pb):
                dve.wait_ge(act_gl.sem, act_gl.at(pb, 1))
                step(dve.reciprocal(gl[:, 8:9], gl[:, 7:8]))
                if not (isinstance(pb, int) and pb == 0):
                    dve.wait_ge(act_v1.sem, act_v1.at(pb * NG - 1, 1))
                dve.tensor_scalar(gate[:], gl[:, 4:7], gl[:, 8:9], None, ALU.mult).then_inc(gates_ready.sem, 1)

            def imp_out(pb):
                dve.wait_ge(pe_imp.sem, pe_imp.at(pb, 1))
                dve.tensor_copy(row_a, side[0:1, :]).then_inc(imp_read.sem, 1)
                dve.wait_ge(imp_read.sem, imp_read.at(pb, 1))

            def top_round(step):
                dve.tensor_copy(carrier[:, 0:1], carrier[:, 1:2])
                step(dve.max(top8[:], row_a))
                dve.tensor_copy(carrier[:, 0:1], carrier[:, 1:2])
                step(dve.match_replace(row_a, top8[:], row_a, TAKEN))

            def ranks(step, pb):
                dve.wait_ge(act_nq.sem, act_nq.at(pb, 1))
                step(dve.tensor_scalar(row_b, row_a, TAKEN, None, ALU.is_equal))
                step(dve.tensor_tensor_scan(row_a, row_b, row_b, 0.0, ALU.add, ALU.max))
                dve.tensor_tensor(row_a, row_a, row_b, ALU.mult).then_inc(key_row.sem, 1)

            def one_hot(step, pb):
                dve.wait_ge(pe_key.sem, pe_key.at(pb, 1))
                step(dve.tensor_copy(key[:], bank(3)[:, 0:TT]))
                dve.tensor_tensor(selm[:], K("count").unsqueeze(1).to_broadcast([P, TT, KEEP]),
                                  key[:].unsqueeze(2).to_broadcast([P, TT, KEEP]), ALU.is_equal)\
                    .then_inc(sel_ready.sem, 1)

            def selT_out(pb):
                dve.wait_ge(pe_selT.sem, pe_selT.at(pb, 1))
                dve.tensor_copy(selT[:], bank(3)[:, 0:KEEP].unsqueeze(1).to_broadcast([P, HPG, KEEP]))\
                    .then_inc(selT_ready.sem, 1)

            def rope_heads(S, t):
                dve.wait_ge(act_k.sem, act_k.at(S, t + 1))
                if t > 0:
                    dve.wait_ge(rope_sum.sem, rope_sum.at(S, t))
                cs = table("ropeC")[:, t:t + 1].to_broadcast([P, 2 * HPG, ROPE])
                sn = table("ropeS")[:, t:t + 1].to_broadcast([P, 2 * HPG, ROPE])
                rope(qk[:, t % 2, :, KVL:KVL + ROPE], cs, sn, ra[:], rb[:]).then_inc(rope_ab.sem, 1)

            def vsd_out(S):
                dve.wait_ge(act_sel.sem, act_sel.at(S, 1))
                dve.scalar_tensor_tensor(vsd[:], side[:, HPG * KD:], gate[:, 1:2], K("diag"), ALU.mult, ALU.mult)\
                    .then_inc(vsd_ready.sem, 1)

            def rope_selected(S):
                dve.wait_ge(act_sel.sem, act_sel.at(S, 1))
                dve.wait_ge(rope_sum.sem, rope_sum.at(S, TT))
                cs = table("ropeC")[0:KEEP, 0:1].to_broadcast([KEEP, HPG, ROPE])
                sn = table("ropeS")[0:KEEP, 0:1].to_broadcast([KEEP, HPG, ROPE])
                rope(ksraw[:, :, 0:ROPE], cs, sn, ra[0:KEEP, 0:HPG], rb[0:KEEP, 0:HPG]).then_inc(ks_ab.sem, 1)

            def selected_shift(step, S):
                dve.wait_ge(pe_s2.sem, pe_s2.at(S, 1))
                s2 = side.rearrange("p (n k) -> p n k", k=KEEP)
                step(dve.tensor_reduce(n2[:, 0], s2, AX.X, ALU.max, negate=True))
                dve.tensor_tensor(p2[:], s2, n2[:, 0].unsqueeze(2).to_broadcast([P, TT * HPG, KEEP]), ALU.add)\
                    .then_inc(s2_shift.sem, 1)

            def selected_sum(step, S):
                dve.wait_ge(act_e2.sem, act_e2.at(S, 1))
                step(dve.tensor_reduce(n2[:, 1], p2[:], AX.X, ALU.add))
                dve.reciprocal(n2[:, 2], n2[:, 1]).then_inc(n2_ready.sem, 1)

            def row_max(it, u, first):
                dve.wait_ge(scored.sem, scored.at(it, u + 1))
                if u >= 2:
                    dve.wait_ge(weighed.sem, weighed.at(it, u - 1))
                elif not first:
                    dve.wait_ge(weighed.sem, weighed.at(it - 1, NU + u - 1))
                dve.tensor_reduce(nmax[:, u % 2], score_tiles(u), AX.X, ALU.max,
                                  negate=True).then_inc(maxed.sem, 1)

            def one_over(it, u, first=False):
                dve.wait_ge(weighed.sem, weighed.at(it, u + 1))
                if u >= 2:
                    dve.wait_ge(normed.sem, normed.at(it, u - 1))
                elif not first:
                    dve.wait_ge(normed.sem, normed.at(it - 1, NU + u - 1))
                dve.reciprocal(rec[:, u % 2], den[:, u % 2]).then_inc(rec_ready.sem, 1)

            def turned_out(it, u, first=False):
                qt, h = divmod(u, HPG)
                dve.wait_ge(turned.sem, turned.at(it, u + 1))
                if h == 0:
                    if qt >= 2:
                        dve.wait_ge(summed.sem, summed.at(it, qt - 1))
                    elif not first:
                        dve.wait_ge(summed.sem, summed.at(it - 1, qt + 3))
                dve.tensor_copy(turned_tile(qt)[:, h, :, 0:span(u)], turn_tiles(u))\
                    .then_inc(pT_ready.sem, 1)

            def add_share(it, batch):
                rows = rows_of(batch).rearrange("p t c -> p (t c)")
                dve.wait_ge(pe_y.sem, pe_y.at(it, 1))
                if not (isinstance(it, int) and it == 0):
                    dve.wait_ge(x_done.sem, x_done.at(it, 0))
                dve.tensor_tensor(rows, rows, bank(3), ALU.add).then_inc(x_done.sem, 1)

            lg, le = (sq[:, 2 * i:2 * i + 2].rearrange("p a (b e) -> p (a b) e", e=EXPERTS) for i in range(2))

            def router_logits(step, tb):
                dve.wait_ge(pe_lg.sem, pe_lg.at(tb, 1))
                dve.tensor_tensor(lg, side[:, 0:TT * EXPERTS].rearrange("p (t e) -> p t e", t=TT),
                                  brb[:].unsqueeze(1).to_broadcast([P, TT, EXPERTS]), ALU.add).then_inc(lg_read.sem, 1)
                dve.wait_ge(lg_read.sem, lg_read.at(tb, 1))
                step(dve.tensor_reduce(st[:, 44:48], lg, AX.X, ALU.max))
                dve.tensor_tensor(lg, lg, st[:, 44:48].unsqueeze(2).to_broadcast([P, TT, EXPERTS]), ALU.subtract)\
                    .then_inc(lg_ready.sem, 1)

            def router_probs(step, tb):
                dve.wait_ge(act_lg.sem, act_lg.at(tb, 1))
                step(dve.tensor_reduce(st[:, 48:52], le, AX.X, ALU.add))
                step(dve.reciprocal(st[:, 52:56], st[:, 48:52]))
                dve.tensor_tensor(rtok[:, bass.ds(tb * TT, TT), :], le,
                                  st[:, 52:56].unsqueeze(2).to_broadcast([P, TT, EXPERTS]), ALU.mult)\
                    .then_inc(rtok_done.sem, 1)

            def group(b, g, first, last, chains):
                it = b * NG + g
                S = it + 1
                start = first and g == 0
                sides = not (last and g == NG - 1)
                if sides:
                    step_s = Chain(dve, dve_s, S)
                if g == 2 and not last:
                    chains["p"] = Chain(dve, dve_p, b + 1)
                if g == 0 and not first:
                    chains["t"] = Chain(dve, dve_t, b - 1)
                for u in range(NU):
                    if u > 0:
                        one_over(it, u - 1, start)
                    elif not start:
                        one_over(it - 1, NU - 1)
                    row_max(it, u, start)
                    if u >= 2:
                        turned_out(it, u - 2, start)
                    elif not start:
                        turned_out(it - 1, NU + u - 2)
                    if u == 5 and not start:
                        add_share(it - 1, b if g else b - 1)
                    if g == 2 and u == 12 and not last:
                        gate_logits(chains["p"], b + 1)
                    if sides:
                        if u in ROPE_SLOT:
                            rope_heads(S, ROPE_SLOT.index(u))
                        if u == 8:
                            vsd_out(S)
                        if u == 9:
                            rope_selected(S)
                        if u == 12:
                            selected_shift(step_s, S)
                        if u == 14:
                            selected_sum(step_s, S)
                        if g == NG - 1:
                            if u < 4:
                                top_round(chains["p"])
                            if u == 4:
                                ranks(chains["p"], b + 1)
                            if u == 6:
                                one_hot(chains["p"], b + 1)
                            if u == 7:
                                selT_out(b + 1)
                                chains["p"].close()
                    if g == 0 and not first:
                        step = chains["t"]
                        if u == 6:
                            dve.wait_ge(x_done.sem, x_done.at(it - 1, 1))
                        if 6 <= u < 12:
                            norm(step, rows_of(b - 1), u - 6, x2_ready)
                        if u == 14:
                            router_logits(step, b - 1)
                        if u == 15:
                            router_probs(step, b - 1)
                            step.close()
                    if g == 2 and not last:
                        step = chains["p"]
                        if u == 1 and not first:
                            dve.wait_ge(pe_x2T.sem, pe_x2T.at(b - 1, 1))
                        if 1 <= u < 7:
                            norm(step, rows_of(b + 1), u - 1, xn_ready)
                        if u == 9:
                            mean_of_batch(step, b + 1)
                        if u == 11:
                            squares(step, b + 1)
                        if u == 12:
                            roots(step)
                        if u == 13:
                            latents(b + 1)
                            gates(step, b + 1)
                            imp_out(b + 1)
                if sides:
                    step_s.close()

            step = Chain(dve, dve_p, 0)
            for k in range(6):
                norm(step, rows_of(0), k, xn_ready)
            mean_of_batch(step, 0)
            squares(step, 0)
            gate_logits(step, 0)
            roots(step)
            latents(0)
            gates(step, 0)
            imp_out(0)
            for t in range(TT):
                if t == 0:
                    dve.wait_ge(k1_ready.sem, k1_ready.at(0, 1))
                rope_heads(0, t)
            for _ in range(KEEP // 8):
                top_round(step)
            ranks(step, 0)
            one_hot(step, 0)
            selT_out(0)
            step.close()
            vsd_out(0)
            rope_selected(0)
            step = Chain(dve, dve_s, 0)
            selected_shift(step, 0)
            selected_sum(step, 0)
            step.close()
            chains = {}
            for g in range(NG):
                group(0, g, True, False, chains)
            with dve.Fori(1, B - 1) as b:
                for g in range(NG):
                    group(b, g, False, False, chains)
            for g in range(NG):
                group(B - 1, g, False, True, chains)
            it = B * NG - 1
            one_over(it, NU - 1)
            turned_out(it, NU - 2)
            turned_out(it, NU - 1)
            add_share(it, B - 1)
            step = Chain(dve, dve_t, B - 1)
            dve.wait_ge(x_done.sem, x_done.at(it, 1))
            for k in range(6):
                norm(step, rows_of(B - 1), k, x2_ready)
            router_logits(step, B - 1)
            router_probs(step, B - 1)
            step.close()
            dve.wait_ge(spilled.sem, 16 * B)

            step = Chain(dve, dve_r, 0)
            dve.wait_ge(act_rT.sem, HALF // T)
            bufs = [sortA, sortB]
            src, dst = score, 0
            size = 2
            while size <= HALF:
                a = src.rearrange("p (n k) -> p n k", k=size)
                o = bufs[dst].rearrange("p (n k) -> p n k", k=size)
                h = size // 2
                lo, hi = a[:, :, 0:h], a[:, :, h:size][:, :, ::-1]
                dve.tensor_tensor(o[:, :, 0:h], lo, hi, ALU.max)
                step(dve.tensor_tensor(o[:, :, h:size], lo, hi, ALU.min))
                src, dst = bufs[dst], 1 - dst
                src, dst = halvings(dve, step, src, dst, bufs, h)
                size *= 2
            other = routed
            step(dve.tensor_copy(other[0:EXPERTS, :], src[EXPERTS:P, :]))
            step(dve.tensor_copy(other[EXPERTS:P, :], src[0:EXPERTS, :]))
            dve.tensor_tensor(bufs[dst][0:EXPERTS, :], src[0:EXPERTS, :], other[0:EXPERTS, ::-1], ALU.max)
            step(dve.tensor_tensor(bufs[dst][EXPERTS:P, :], src[EXPERTS:P, :], other[EXPERTS:P, ::-1], ALU.min))
            src, dst = bufs[dst], 1 - dst
            src, dst = halvings(dve, step, src, dst, bufs, HALF)
            srt = src.rearrange("p (g k) -> p g k", k=GROUP)
            step(dve.tensor_reduce(gsum[:], srt, AX.X, ALU.add))
            step(dve.tensor_copy(glast[:], srt[:, :, GROUP - 1]))
            step(dve.memset(found[:], 0.0))
            n = 0
            for r in range(len(SCORE_ROUNDS)):
                step(dve.tensor_tensor(cand[:].bitcast(I32), cbits[:, r * CAND:(r + 1) * CAND],
                                       found[:, CAND:CAND + 1].bitcast(I32).to_broadcast([P, CAND]), ALU.bitwise_or))
                step(dve.tensor_tensor(gcmp[:], gsum[:].unsqueeze(1).to_broadcast([P, CAND, NGR]),
                                       cand[:].unsqueeze(2).to_broadcast([P, CAND, NGR]), ALU.is_ge))
                dve.tensor_reduce(cnt[:], gcmp[:], AX.X, ALU.add).then_inc(cnt_ready.sem, 1)
                n += 1
                dve.wait_ge(pe_cnt.sem, n)
                step(dve.scalar_tensor_tensor(found[:, 0:CAND], bank(4)[:, 0:CAND], float(BUDGET), cand[:],
                                              ALU.is_ge, ALU.mult))
                step(dve.tensor_reduce(found[:, CAND:CAND + 1], found[:], AX.X, ALU.max))
            kth = rs[:, 0:1]
            step(dve.tensor_copy(kth, found[:, CAND:CAND + 1]))
            step(dve.tensor_scalar(gm[:, 0], gsum[:], kth, None, ALU.is_gt))
            step(dve.tensor_scalar(gm[:, 1], gsum[:], kth, None, ALU.is_equal))
            dve.tensor_reduce(cnt[:, 0:1], gm[:, 0], AX.X, ALU.add).then_inc(cnt_ready.sem, 1)
            n += 1
            dve.wait_ge(pe_cnt.sem, n)
            room = rs[:, 1:2]
            step(dve.tensor_scalar(room, bank(4)[:, 0:1], -1.0, float(BUDGET), ALU.mult, ALU.add))
            step(dve.tensor_scalar(gkey[:], gm[:, 1], -1e6, 1e6, ALU.mult, ALU.add))
            step(dve.tensor_tensor(gkey[:], gkey[:], K("gidx"), ALU.add))
            step(dve.memset(found[:], 0.0))
            for r in range(len(INDEX_ROUNDS)):
                a = CONST["irnd"][0] + r * CAND
                step(dve.tensor_scalar(cand[:], cst[:, a:a + CAND], found[:, CAND:CAND + 1], None, ALU.add))
                step(dve.tensor_tensor(gcmp[:], gkey[:].unsqueeze(1).to_broadcast([P, CAND, NGR]),
                                       cand[:].unsqueeze(2).to_broadcast([P, CAND, NGR]), ALU.is_lt))
                dve.tensor_reduce(cnt[:], gcmp[:], AX.X, ALU.add).then_inc(cnt_ready.sem, 1)
                n += 1
                dve.wait_ge(pe_cnt.sem, n)
                step(dve.scalar_tensor_tensor(found[:, 0:CAND], bank(4)[:, 0:CAND], room, cand[:],
                                              ALU.is_le, ALU.mult))
                step(dve.tensor_reduce(found[:, CAND:CAND + 1], found[:], AX.X, ALU.max))
            step(dve.tensor_scalar(gm[:, 2], gkey[:], found[:, CAND:CAND + 1], None, ALU.is_lt))
            step(dve.tensor_tensor(gm[:, 3], gm[:, 0], gm[:, 2], ALU.add))
            dve.tensor_reduce(cnt[:, 0:1], gm[:, 3], AX.X, ALU.add).then_inc(cnt_ready.sem, 1)
            step(dve.tensor_tensor(gm[:, 0], gm[:, 3], glast[:], ALU.mult))
            step(dve.tensor_scalar(gm[:, 1], gm[:, 3], -BIG, BIG, ALU.mult, ALU.add))
            step(dve.tensor_tensor(gm[:, 2], gm[:, 0], gm[:, 1], ALU.add))
            low = rs[:, 2:3]
            step(dve.tensor_reduce(low, gm[:, 2], AX.X, ALU.min))
            step(dve.tensor_copy(rs[0:EXPERTS, 3:4], rs[EXPERTS:P, 2:3]))
            step(dve.tensor_copy(rs[EXPERTS:P, 3:4], rs[0:EXPERTS, 2:3]))
            step(dve.tensor_tensor(rs[:, 4:5], low, rs[:, 3:4], ALU.min))
            low = rs[:, 4:5]
            n += 1
            dve.wait_ge(pe_cnt.sem, n)
            step(dve.tensor_scalar(rs[:, 5:6], bank(4)[:, 0:1], float(GROUP), None, ALU.mult))
            step(dve.tensor_scalar(above, score, low, None, ALU.is_gt))
            step(dve.tensor_scalar(equal, score, low, None, ALU.is_equal))
            dve.tensor_reduce(cnt[:, 0:1], above, AX.X, ALU.add).then_inc(cnt_ready.sem, 1)
            n += 1
            dve.wait_ge(pe_cnt.sem, n)
            step(dve.tensor_tensor(rs[:, 6:7], rs[:, 5:6], bank(4)[:, 0:1], ALU.subtract))
            dve.tensor_reduce(cnt[:, 0:1], equal, AX.X, ALU.add).then_inc(cnt_ready.sem, 1)
            n += 1
            dve.wait_ge(pe_cnt.sem, n)
            step(dve.tensor_copy(rs[:, 7:8], bank(4)[:, 0:1]))
            step(dve.tensor_tensor_scan(sortA, equal, equal, rs[:, 7:8], ALU.add, ALU.max))
            step(dve.scalar_tensor_tensor(sortB, sortA, rs[:, 6:7], equal, ALU.is_le, ALU.mult))
            step(dve.tensor_tensor(sortA, sortB, above, ALU.add))
            dve.tensor_tensor(routed, sortA, score, ALU.mult).then_inc(routed_ready.sem, 1)

            with dve.Fori(0, NBLK) as jj:
                dve.wait_ge(fblk_ready.sem, fblk_ready.at(jj, 1))
                split = Chain(dve, fsplit, jj)
                split(dve.tensor_copy(fpart[:, 0], fblk[:]))
                split(dve.tensor_tensor(frest[0], fblk[:], fpart[:, 0], ALU.subtract))
                split(dve.tensor_copy(fpart[:, 1], frest[0]))
                split(dve.tensor_tensor(frest[1], frest[0], fpart[:, 1], ALU.subtract))
                split.close()
                dve.tensor_copy(fpart[:, 2], frest[1]).then_inc(fpart_ready.sem, 1)
                step = Chain(dve, dve_e, jj)
                for n in range(2 * HT):
                    half, m = divmod(n, HT)
                    dve.wait_ge(pe_gt.sem, pe_gt.at(jj, n + 1))
                    dve.wait_ge(act_up.sem, act_up.at(jj, n + 1))
                    dve.scalar_tensor_tensor(gateT[:, n % 2], bank(2 + n % 2), bgt[:, m:m + 1], siluT[:, n % 2],
                                             ALU.add, ALU.mult).then_inc(gate_mul.sem, 1)
                    dve.wait_ge(pe_f.sem, pe_f.at(jj, n + 1))
                    dve.wait_ge(gate_mul.sem, gate_mul.at(jj, n + 1))
                    if n >= 2:
                        dve.wait_ge(pe_dn.sem, pe_dn.at(jj, n - 1))
                    else:
                        dve.wait_ge(pe_dn.sem, pe_dn.at(jj, 0))
                    dve.tensor_tensor(hT[:, n % 2], gateT[:, n % 2], bank(4 + n % 2), ALU.mult)\
                        .then_inc(h_ready.sem, 1)
                    if m == HT - 1:
                        dve.wait_ge(pe_dn.sem, pe_dn.at(jj, n + 1))
                        dve.wait_ge(stored.sem, stored.at(jj, 0))
                        step(dve.tensor_scalar(yrec[:, 0], bank(7)[:, 0:TT], EPS_DEN, None, ALU.add))
                        step(dve.reciprocal(yrec[:, 1], yrec[:, 0]))
                        dve.tensor_tensor(yout[half][:], bank(6).rearrange("p (t c) -> p t c", t=TT),
                                          yrec[:, 1].unsqueeze(2).to_broadcast([P, TT, C]), ALU.mult)\
                            .then_inc(y_scaled.sem, 1)
                step.close()


def halvings(dve, step, src, dst, bufs, size):
    d = size // 2
    while d >= 1:
        a = src.rearrange("p (n k) -> p n k", k=2 * d)
        o = bufs[dst].rearrange("p (n k) -> p n k", k=2 * d)
        dve.tensor_tensor(o[:, :, 0:d], a[:, :, 0:d], a[:, :, d:2 * d], ALU.max)
        step(dve.tensor_tensor(o[:, :, d:2 * d], a[:, :, 0:d], a[:, :, d:2 * d], ALU.min))
        src, dst = bufs[dst], 1 - dst
        d //= 2
    return src, dst


def constants():
    f = (np.float32(1.0) / np.float32(10000.0) ** (np.arange(0, ROPE, 2, dtype=np.float32) / np.float32(ROPE)))
    a = np.outer(np.arange(T, dtype=np.float32), f.astype(np.float32)).astype(np.float32)
    cos, sin = np.cos(a), np.sin(a)
    lane = np.arange(P)
    tiles = lambda m: m.reshape(TT, P, -1).transpose(1, 0, 2).reshape(P, -1)
    parts = {
        "ident": np.eye(P),
        "mask": np.where(lane[None, :] > lane[:, None], MASKED, 0.0),
        "ropeC": tiles(np.concatenate([cos, cos], 1)),
        "ropeS": tiles(np.concatenate([-sin, sin], 1)),
        "diag": (lane[:, None] // KEEP == lane[None, :] // VD) * 1.0,
        "count": np.tile(np.arange(1, KEEP + 1), (P, 1)),
        "pair": (lane[:, None] % EXPERTS == lane[None, :] % EXPERTS) * 1.0,
        "lower": (lane[None, :] == lane[:, None] + EXPERTS) * 1.0,
        "ones": np.ones((P, P)),
        "half": (lane[:, None] // EXPERTS == np.arange(2)[None, :]) * 1.0,
        "gidx": ((lane[:, None] // EXPERTS) * NGR + np.arange(NGR)[None, :]) * EXPERTS + lane[:, None] % EXPERTS,
        "irnd": np.tile(np.concatenate([np.arange(1, CAND + 1) << s for s in INDEX_ROUNDS]), (P, 1)),
    }
    cst = np.zeros((P, NCONST), np.float32)
    for name, (i, j) in CONST.items():
        cst[:, i:j] = parts[name]
    bits = np.tile(np.concatenate([np.arange(1, CAND + 1) << s for s in SCORE_ROUNDS]), (P, 1)).astype(np.int32)
    expert = np.arange(HT)[:, None] * EPT + lane[None, :] // HID
    one = (lane[:, None, None] % EXPERTS == expert[None]) * 1.0
    sel = np.concatenate([one * (lane[:, None, None] // EXPERTS == s) for s in range(2)], 1)
    return cst, bits, sel


def kernel(**inputs):
    import ml_dtypes
    import concourse.bacc as _bacc
    from concourse.bass_utils import run_bass_kernel_spmd as _run

    w = {k: np.asarray(v) for k, v in inputs.items()}
    A = lambda n: w["L0_attn_" + n]
    F = lambda n: w["L0_ffn_" + n]
    cst, bits, sel = constants()

    def rope_first(m):
        m = m.reshape(C, NH, KD)
        return np.concatenate([m[:, :, NOPE:], m[:, :, :NOPE]], 2).reshape(C, NH * KD)

    arrays = {
        "x": A("x").reshape(NTOK, C),
        "w_cat": np.concatenate([A("w_cq"), A("w_ckv"), A("w_krope")], 1),
        "w_imp": A("w_imp"), "w_gate": A("w_gate"),
        "g_q": A("g_qnorm").reshape(QL, 1), "g_kv": A("g_kvnorm").reshape(KVL, 1),
        "w_q": np.concatenate([A("w_dq_rope").reshape(QL, NH, ROPE), A("w_dq_nope").reshape(QL, NH, NOPE)], 2),
        "dqn_t": A("w_dq_nope").reshape(QL, NH, NOPE).transpose(2, 1, 0).reshape(NOPE, NH * QL),
        "dkn_t": A("w_dk_nope").reshape(KVL, NH, NOPE).transpose(2, 1, 0).reshape(NOPE, NH * KVL),
        "w_dv": A("w_dv"), "w_wink": rope_first(A("w_wink")), "w_winv": A("w_winv"),
        "w_selk": rope_first(A("w_selk")), "w_selv": A("w_selv"), "w_proj": A("w_proj"),
        "w_r": F("Wr"), "b_r": F("br").reshape(EXPERTS),
        "w_up": F("Wup").transpose(1, 0, 2).reshape(C, EXPERTS * HID), "b_up": F("bup").reshape(HT, P).T,
        "w_gt": F("Wgate").transpose(1, 0, 2).reshape(C, EXPERTS * HID), "b_gt": F("bgate").reshape(HT, P).T,
        "w_dn": F("Wdown").reshape(EXPERTS * HID, C), "b_dn": F("bdown"),
        "consts": cst, "bits": bits, "select": sel.astype(ml_dtypes.bfloat16),
    }
    nc = _bacc.Bacc("TRN2", target_bir_lowering=False, num_devices=1)
    args, sent = [], {}
    for name, a in arrays.items():
        a = np.ascontiguousarray(a)
        sent["in_" + name] = a
        args.append(nc.dram_tensor("in_" + name, a.shape, mybir.dt.from_np(a.dtype), kind="ExternalInput").ap())
    out = nc.dram_tensor("out_x", (NTOK, C), F32, kind="ExternalOutput").ap()
    build(nc, *args, out)
    r = _run(nc, [sent], core_ids=[0])
    return r.results[0]["out_x"].reshape(B, T, C)
```

```python
from contextlib import ExitStack

import numpy as np

import concourse.bass as bass
from concourse import mybir

F32 = mybir.dt.float32
BF16 = mybir.dt.bfloat16
I32 = mybir.dt.int32
ALU = mybir.AluOpType
ACT = mybir.ActivationFunctionType
AX = mybir.AxisListType

P = 128
B, T, C = 8, 512, 128
NH, NOPE, ROPE, VD = 16, 32, 64, 32
QL, KVL, KEEP = 96, 32, 32
CAT = QL + KVL + ROPE
HD = KVL + ROPE + NOPE
KD = ROPE + NOPE
HPG = 4
NG = NH // HPG
TT = T // P
NU = HPG * TT
EXPERTS, HID, GROUP, TOPK = 64, 32, 64, 16
NTOK = B * T
HALF = NTOK // 2
NGR = HALF // GROUP
BUDGET = NTOK // GROUP * TOPK
HT = EXPERTS * HID // P
EPT = P // HID
SORT = 32
NBLK = B // 2
EPS_LN, EPS_RMS, EPS_DEN = 1e-5, 1e-6, 1e-6
MASKED = -1e30
N_P, N_S, N_T = 47, 2, 21
NARROW = NU // 2
PASSES = [(2 << i, (2 << i) >> k) for i in range(9) for k in range(1, i + 2)]
MERGE = 36
PROJ_SLOT = [0, 1, 4, 6]
ROPE_SLOT = [1, 2, 5, 7]
TURN_SLOT = [3, 5, 7, 9]
TAKEN = -3.0e38
BIG = 3.0e38
RSQRT_MAGIC = float(0x5F3759DF)
SCORE_ROUNDS = [27, 23, 19, 15, 11, 7, 3, 0]
INDEX_ROUNDS = [9, 5, 1, 0]
CAND = 15

CONST = {}
_at = 0
for _name, _n in (("ident", P), ("mask", P), ("ropeC", TT * ROPE), ("ropeS", TT * ROPE), ("diag", HPG * VD),
                  ("count", KEEP), ("pair", P), ("lower", P), ("ones", P), ("half", 2), ("gidx", NGR),
                  ("irnd", len(INDEX_ROUNDS) * CAND)):
    CONST[_name] = (_at, _at + _n)
    _at += _n
NCONST = _at



class Flag:

    def __init__(self, sem, per, base=0):
        self.sem, self.per, self.base = sem, per, base

    def at(self, it, n):
        return it * self.per + n + self.base


class Chain:

    def __init__(self, eng, flag, it):
        self.eng, self.flag, self.it, self.n = eng, flag, it, 0

    def __call__(self, ins):
        self.n += 1
        ins.then_inc(self.flag.sem, 1)
        self.eng.wait_ge(self.flag.sem, self.flag.at(self.it, self.n))

    def close(self):
        assert self.n == self.flag.per, (self.n, self.flag.per)


def build(nc, x, w_cat, w_imp, w_gate, g_q, g_kv, w_q, dqn_t, dkn_t, w_dv, w_wink, w_winv, w_selk, w_selv, w_proj,
          w_r, b_r, w_up, b_up, w_gt, b_gt, w_dn, b_dn, consts, bits, select, out):
    with ExitStack() as ctx:
        def sb(name, shape, dt=F32):
            return ctx.enter_context(nc.sbuf_tensor(name, shape, dt))

        def flag(name, per=1, base=0):
            return Flag(ctx.enter_context(nc.semaphore(name)), per, base)

        banks = ctx.enter_context(nc.psum_tensor("banks", [P, 8, 512], F32))

        def bank(i):
            return banks[:, i, :]

        xres = sb("xres", [P, B * TT, C])
        cst = sb("cst", [P, NCONST])
        cbits = sb("cbits", [P, len(SCORE_ROUNDS) * CAND], I32)
        identb = sb("identb", [P, P], BF16)
        maskb = sb("maskb", [P, P], BF16)
        wcat = sb("wcat", [P, CAT])
        wimp = sb("wimp", [P, 1])
        wgate = sb("wgate", [P, 3])
        gq = sb("gq", [QL, 2])
        k1s = sb("k1s", [P, 1])
        wr = sb("wr", [P, EXPERTS])
        brb = sb("brb", [P, EXPERTS])
        bup = sb("bup", [P, HT])
        bgt = sb("bgt", [P, HT])
        bdn = sb("bdn", [P, 2, C])
        wide = sb("wide", [P, 2 * HT * P + HT * P // 2 + HT * C])
        room = [0]

        def part(rows, cols):
            room[0] += cols
            return wide[0:rows, room[0] - cols:room[0]]

        wq = part(QL, NH * HD)
        wink = part(P, NH * KD)
        winv = part(P, NH * VD)
        wselk = part(P, NH * KD)
        wselv = part(P, NH * VD)
        wdv = part(KVL, NH * VD)
        wproj = part(P, NG * C)
        room[0] = 0
        wup = part(P, HT * P)
        wgt = part(P, HT * P)
        wdn = part(P, HT * C)
        selw = part(P, HT * P // 2).bitcast(BF16).rearrange("p (n c) -> p n c", n=HT)

        xn = sb("xn", [P, TT, C])
        sq = sb("sq", [P, TT, C])
        st = sb("st", [P, 64])
        xnT = sb("xnT", [P, T])
        pc = sb("pc", [P, TT, CAT])
        k1 = sb("k1", [P, TT, HD])
        nqT = sb("nqT", [QL, T])
        k1n = sb("k1n", [P, T])
        k1T = sb("k1T", [P, T])
        row_a = sq[0:1].rearrange("p t c -> p (t c)")
        row_b = pc[0:1].rearrange("p t c -> p (t c)")[:, 0:T]
        top8 = sb("top8", [1, 8])
        carrier = sb("carrier", [1, 2])
        key = sb("key", [P, TT])
        selm = sb("selm", [P, TT, KEEP])
        selT = sb("selT", [P, HPG, KEEP])
        xsb = sb("xsb", [P, P])
        gl = sb("gl", [P, 16])
        gate = sb("gate", [P, 3])

        qk = sb("qk", [P, 2, 2 * HPG, HD])
        ra = sb("ra", [P, 2 * HPG, ROPE])
        rb = sb("rb", [P, 2 * HPG, ROPE])
        qT = sb("qT", [P, 2, HPG, T])
        k3T = sb("k3T", [P, 2, HPG, T])
        v13 = sb("v13", [P, 2, 2, TT, HPG, VD])
        kstok = sb("kstok", [P, HPG, HD])
        ksraw = sb("ksraw", [KEEP, HPG, KD])
        ksT = sb("ksT", [P, HPG, KEEP])
        vsd = sb("vsd", [P, HPG * VD])
        p2 = sb("p2", [P, TT * HPG, KEEP])
        p2T = sb("p2T", [P, T])
        n2 = sb("n2", [P, 3, TT * HPG])
        prob = sb("prob", [P, 3, 2, T])
        probx = sb("probx", [P, 2, P])
        nmax = sb("nmax", [P, 2, 2])
        den = sb("den", [P, 2, 2])
        rec = sb("rec", [P, 2, 2])
        pTe = sb("pTe", [P, HPG, 2, (TT - 1) * P])
        pTo = sb("pTo", [P, HPG, 2, TT * P])
        attT = sb("attT", [P, T])
        ptok = sb("ptok", [P, TT, EXPERTS])
        probT = sb("probT", [EXPERTS, T])
        parts = [sb(f"parts{i}", [P, T // 2]) for i in range(2)]
        runs = [sb(f"runs{i}", [EXPERTS, T]) for i in range(2)]
        x2dram = nc.dram_tensor("x2dram", (B, P, T), F32, kind="Internal").ap()
        score_dram = nc.dram_tensor("score_dram", (B, EXPERTS, T), F32, kind="Internal").ap()
        sorted_dram = nc.dram_tensor("sorted_dram", (B, EXPERTS, T), F32, kind="Internal").ap()

        def span(u):
            return (u // HPG + 1) * P

        def probs(u):
            if u == 3:
                return probx[:]
            return prob[:, u % 3 if u < 3 else (u - 4) % 3, :, 0:span(u)]

        def score_tiles(u):
            s = 2 * (u % 2)
            if u < NARROW:
                return bank(s).rearrange("p (a c) -> p a c", a=2)[:, :, 0:span(u)]
            return banks[:, s:s + 2, 0:span(u)]

        def turn_tiles(u):
            if u < NARROW:
                return bank(4 + u % 2).rearrange("p (a c) -> p a c", a=2)[:, :, 0:span(u)]
            return banks[:, 4:6, 0:span(u)]

        def turned_tile(qt):
            return pTo if qt % 2 else pTe

        dqn = pTo[:].rearrange("p a b c -> p (a b c)")[0:NOPE, 0:NH * QL]
        dkn = pTo[:].rearrange("p a b c -> p (a b c)")[0:NOPE, NH * QL:NH * (QL + KVL)]

        flat = lambda t: t.rearrange("p a b c -> p (a b c)")
        sortA = qT[:, 0].rearrange("p a b -> p (a b)")
        sortB = qT[:, 1].rearrange("p a b -> p (a b)")
        score = k3T[:, 0].rearrange("p a b -> p (a b)")
        routed = k3T[:, 1].rearrange("p a b -> p (a b)")
        above = flat(pTe[:])[:, 0:HALF]
        equal = flat(prob[:])[:, 0:HALF]
        gsum = sb("gsum", [P, NGR])
        glast = sb("glast", [P, NGR])
        gcmp = p2[:].rearrange("p a b -> p (a b)")[:, 0:CAND * NGR].rearrange("p (c g) -> p c g", g=NGR)
        gkey = sb("gkey", [P, NGR])
        cabove = sb("cabove", [P, 1])
        gm = sb("gm", [P, 4, NGR])
        rs = sb("rs", [P, 16])
        cand = sb("cand", [P, CAND])
        cnt = sb("cnt", [P, CAND])
        found = sb("found", [P, CAND + 1])

        x2nT = flat(pTo[:])
        hid = flat(pTe[:]).rearrange("p (n c) -> p n c", c=T)
        siluT, gateT, hT = hid[:, 0:2], hid[:, 2:4], hid[:, 4:6]
        fblk = [p2T, xnT]
        frest = [p2[:].rearrange("p a b -> p (a b)"), attT[:]]
        fpart = prob[:, 0].rearrange("p a b -> p (a b)").bitcast(BF16)[:, 0:3 * T].rearrange("p (i c) -> p i c", i=3)
        fsel = prob[0:3 * SORT, 1].rearrange("p a b -> p (a b)").bitcast(BF16)\
            .rearrange("p (s g c) -> p s g c", s=2, g=EXPERTS // SORT)
        yout = [xn, sq]
        yrec = sb("yrec", [P, 2, TT])

        def K(name, rows=slice(0, P)):
            a, b = CONST[name]
            return cst[rows, a:b]

        ident = K("ident")

        ld_x, ld_x_others, ld_w, ld_later, ld_e = flag("ld_x"), flag("ld_x_others"), flag("ld_w"), flag("ld_later"), flag("ld_e")
        cast_done, zero_done = flag("cast_done"), flag("zero_done")
        pe_abs, act_abs, gq_ready = flag("pe_abs"), flag("act_abs"), flag("gq_ready")
        dve_p = flag("dve_p", N_P)
        xn_ready, pe_xnT, act_xnT = flag("xn_ready"), flag("pe_xnT"), flag("act_xnT")
        pe_cat, act_cat = flag("pe_cat", 2), flag("act_cat", 2)
        k1_ab, k1_ready = flag("k1_ab"), flag("k1_ready")
        roots_ready, nq_ready, k1_summed = flag("roots_ready"), flag("nq_ready"), flag("k1_summed")
        pe_nq, act_nq, pe_k1, act_k1, k1T_ready = (flag("pe_nq"), flag("act_nq"), flag("pe_k1"), flag("act_k1"),
                                                   flag("k1T_ready"))
        pe_imp, imp_read, key_row, pe_key, sel_ready = (flag("pe_imp"), flag("imp_read"), flag("key_row"),
                                                        flag("pe_key"), flag("sel_ready"))
        pe_selT, selT_ready = flag("pe_selT"), flag("selT_ready")
        xsb_ready, gl_ready, act_gl, gates_ready = (flag("xsb_ready"), flag("gl_ready"), flag("act_gl"),
                                                    flag("gates_ready"))
        dve_s = flag("dve_s", N_S)
        pe_q, act_q, pe_k, act_k = flag("pe_q", TT), flag("act_q", TT), flag("pe_k", TT), flag("act_k", TT)
        rope_ab, rope_sum = flag("rope_ab", TT), flag("rope_sum", TT)
        pe_tq, act_tq, pe_tk, act_tk = flag("pe_tq", TT), flag("act_tq", TT), flag("pe_tk", TT), flag("act_tk", TT)
        pe_v3, act_v3, pe_v1, act_v1 = flag("pe_v3"), flag("act_v3"), flag("pe_v1"), flag("act_v1")
        pe_sel, act_sel, vsd_ready, ks_ab, ks_sum, pe_ksT, act_ksT = (
            flag("pe_sel"), flag("act_sel"), flag("vsd_ready"), flag("ks_ab"), flag("ks_sum"), flag("pe_ksT"),
            flag("act_ksT"))
        pe_s2T, act_s2T, pe_s2, s2_shift, act_e2, n2_ready, p2_ready, pe_t2, act_t2 = (
            flag("pe_s2T"), flag("act_s2T"), flag("pe_s2"), flag("s2_shift"), flag("act_e2"), flag("n2_ready"),
            flag("p2_ready"), flag("pe_t2"), flag("act_t2"))
        scored, maxed, weighed, rec_ready, normed, turned, pT_ready = (
            flag("scored", NU), flag("maxed", NU), flag("weighed", NU), flag("rec_ready", NU), flag("normed", NU),
            flag("turned", NU), flag("pT_ready", NU))
        summed, att_ready, pe_y, x_done = (flag("summed", TT), flag("att_ready"),
                                                    flag("pe_y"), flag("x_done"))
        dve_t = flag("dve_t", N_T)
        x2_ready, pe_x2T, act_x2T, spilled = flag("x2_ready"), flag("pe_x2T"), flag("act_x2T"), flag("spilled", 16)
        lg_read = flag("lg_read")
        pe_lg, lg_ready, act_lg, probs_ready = flag("pe_lg"), flag("lg_ready"), flag("act_lg"), flag("probs_ready")
        pe_runs, act_runs, presorted = flag("pe_runs"), flag("act_runs"), flag("presorted", len(PASSES), base=1)
        joined = flag("joined")
        score_kept, runs_kept = flag("score_kept", 16, base=16), flag("runs_kept", 16, base=16)
        ld_runs = flag("ld_runs")
        dve_r = flag("dve_r")
        cnt_ready, pe_cnt = flag("cnt_ready"), flag("pe_cnt")
        above_ready, above_counted, routed_ready = flag("above_ready"), flag("above_counted"), flag("routed_ready")
        fblk_ready, fpart_ready, fsplit, placed = (flag("fblk_ready", 2), flag("fpart_ready", 2), flag("fsplit", 8),
                                                   flag("placed", 2 * 6 * 16))
        pe_up, act_up, pe_gt, pe_f, gate_mul, h_ready, pe_dn = (
            flag("pe_up", 2 * HT), flag("act_up", 2 * HT), flag("pe_gt", 2 * HT), flag("pe_f", 2 * HT),
            flag("gate_mul", 2 * HT, base=1), flag("h_ready", 2 * HT), flag("pe_dn", 2 * HT, base=1))
        dve_e = flag("dve_e", 4)
        y_scaled, y_ready, stored = flag("y_scaled", 2, base=1), flag("y_ready", 2), flag("stored", 32, base=16)

        block = ctx.enter_context(nc.Block())

        loads = [
            (cst[:], consts), (wcat[:], w_cat), (wgate[:], w_gate), (dqn, dqn_t), (dkn, dkn_t), (wimp[:], w_imp),
            (wq.rearrange("p (h d) -> p h d", h=NH)[:, :, KVL:HD], w_q), (gq[:, 0:1], g_q), (k1s[0:KVL, :], g_kv),
        ]
        loads_later = [
            (wink, w_wink), (winv, w_winv), (wdv, w_dv), (wselk, w_selk), (wselv, w_selv),
            (wproj.rearrange("p (g c) -> p g c", g=NG), w_proj.rearrange("(g p) c -> p g c", p=P)),
            (wr[:], w_r), (brb[:], b_r.partition_broadcast(P)), (cbits[:], bits),
            (bup[:], b_up), (bgt[:], b_gt), (bdn[0:EXPERTS, 0, :], b_dn), (bdn[EXPERTS:P, 1, :], b_dn),
        ]
        loads_experts = [(wup, w_up), (wgt, w_gt), (selw[0:3 * SORT], select),
                         (wdn.rearrange("p (m c) -> p m c", m=HT), w_dn.rearrange("(m p) c -> p m c", p=P))]

        @block.sync
        def _(sp):
            sp.sem_inc(stored.sem, stored.base)
            tokens = x.rearrange("(n p) c -> p n c", p=P)
            sp.dma_start(xres[:, 0:TT], tokens[:, 0:TT]).then_inc(ld_x.sem, 16)
            sp.wait_ge(zero_done.sem, 2)
            for dst, src in loads:
                sp.dma_start(dst, src).then_inc(ld_w.sem, 16)
            for dst, src in loads_later:
                sp.dma_start(dst, src).then_inc(ld_later.sem, 16)
            sp.dma_start(xres[:, TT:], tokens[:, TT:]).then_inc(ld_x_others.sem, 16)

            def spill(tb):
                sp.wait_ge(act_x2T.sem, act_x2T.at(tb, 1))
                sp.dma_start(x2dram[tb], attT[:]).then_inc(spilled.sem, 16)

            sp.sem_inc(runs_kept.sem, runs_kept.base)
            sp.sem_inc(score_kept.sem, score_kept.base)
            with sp.Fori(1, B) as b:
                tb = b - 1
                spill(tb)
                sp.wait_ge(act_runs.sem, act_runs.at(tb, 1))
                sp.dma_start(score_dram[tb], probT[:]).then_inc(score_kept.sem, 16)
                sp.wait_ge(presorted.sem, presorted.at(tb, len(PASSES)))
                sp.dma_start(sorted_dram[tb], runs[1][:]).then_inc(runs_kept.sem, 16)
            sp.wait_ge(score_kept.sem, 16 * (B - 1) + score_kept.base)
            sp.wait_ge(runs_kept.sem, 16 * (B - 1) + runs_kept.base)
            sp.wait_ge(x_done.sem, B * NG)
            for kept, dst in ((score_dram, score), (sorted_dram, sortA)):
                for half, n in ((0, NBLK), (1, NBLK - 1)):
                    sp.dma_start(dst[half * EXPERTS:(half + 1) * EXPERTS, 0:n * T].rearrange("e (b c) -> e b c", c=T),
                                 kept[half * NBLK:half * NBLK + n].rearrange("b e c -> e b c"))\
                        .then_inc(ld_runs.sem, 16)
            spill(B - 1)
            sp.wait_ge(spilled.sem, 16 * B)
            sp.dma_start(x2nT.rearrange("p (b c) -> p b c", b=B), x2dram.rearrange("b p c -> p b c"))\
                .then_inc(ld_e.sem, 16)
            for dst, src in loads_experts:
                sp.dma_start(dst, src).then_inc(ld_e.sem, 16)

            def place(jj, half):
                for i in range(3):
                    if i < 2:
                        sp.wait_ge(fsplit.sem, fsplit.at(jj, half * 4 + 2 * i + 1))
                    else:
                        sp.wait_ge(fpart_ready.sem, fpart_ready.at(jj, half + 1))
                    for e in range(EXPERTS // SORT):
                        a = half * EXPERTS + e * SORT
                        sp.dma_start(fsel[i * SORT:(i + 1) * SORT, half, e], fpart[a:a + SORT, i])\
                            .then_inc(placed.sem, 16)

            def block_of(jj, last):
                for half in range(2):
                    if half == 0:
                        place(jj, 1)
                    elif not last:
                        place(jj + 1, 0)
                    sp.wait_ge(y_ready.sem, y_ready.at(jj, half + 1))
                    sp.dma_start(out.rearrange("(b t p) c -> b p t c", t=TT, p=P)[half * NBLK + jj],
                                 yout[half][:]).then_inc(stored.sem, 16)

            place(0, 0)
            with sp.Fori(0, NBLK - 1) as jj:
                block_of(jj, False)
            block_of(NBLK - 1, True)
            sp.wait_ge(stored.sem, 16 * B + stored.base)

        @block.gpsimd
        def _(pool):
            for tile, value in ((k1s, 1.0 / NH), (bdn, 0.0), (k1, 0.0), (qk, 0.0), (kstok, 0.0)):
                pool.memset(tile[:], value).then_inc(zero_done.sem, 1)

            def normalise(it, u):
                pool.wait_ge(rec_ready.sem, rec_ready.at(it, u + 1))
                p = probs(u)
                pool.tensor_tensor(p, p, rec[:, u % 2].unsqueeze(2).to_broadcast([P, 2, span(u)]), ALU.mult)\
                    .then_inc(normed.sem, 1)

            def sum_heads(S, t):
                pool.wait_ge(rope_ab.sem, rope_ab.at(S, t + 1))
                pool.tensor_tensor(qk[:, t % 2, :, KVL:KVL + ROPE], ra[:], rb[:], ALU.add).then_inc(rope_sum.sem, 1)

            def sum_selected(S):
                pool.wait_ge(ks_ab.sem, ks_ab.at(S, 1))
                pool.tensor_tensor(kstok[0:KEEP, :, KVL:KVL + ROPE], ra[0:KEEP, 0:HPG], rb[0:KEEP, 0:HPG], ALU.add)\
                    .then_inc(ks_sum.sem, 1)

            def latents(pb):
                pool.wait_ge(roots_ready.sem, roots_ready.at(pb, 1))
                pool.tensor_tensor(pc[:, :, 0:QL], pc[:, :, 0:QL], st[:, 28:32].unsqueeze(2).to_broadcast([P, TT, QL]),
                                   ALU.mult).then_inc(nq_ready.sem, 1)
                pool.tensor_tensor(k1[:, :, 0:KVL], pc[:, :, QL:QL + KVL],
                                   st[:, 32:36].unsqueeze(2).to_broadcast([P, TT, KVL]), ALU.mult)\
                    .then_inc(k1_ready.sem, 1)

            def sum_shared(pb):
                pool.wait_ge(k1_ab.sem, k1_ab.at(pb, 1))
                pool.tensor_tensor(k1[:, :, KVL:KVL + ROPE], ra[:, 0:TT], rb[:, 0:TT], ALU.add)\
                    .then_inc(k1_summed.sem, 1)

            def normalise_selected(S):
                pool.wait_ge(n2_ready.sem, n2_ready.at(S, 1))
                pool.tensor_tensor(p2[:], p2[:], n2[:, 2].unsqueeze(2).to_broadcast([P, TT * HPG, KEEP]), ALU.mult)\
                    .then_inc(p2_ready.sem, 1)

            def group(b, g, first, last):
                it = b * NG + g
                for u in range(NU):
                    if u > 0:
                        normalise(it, u - 1)
                    elif not (first and g == 0):
                        normalise(it - 1, NU - 1)
                    if last and g == NG - 1:
                        continue
                    if u in ROPE_SLOT:
                        sum_heads(it + 1, ROPE_SLOT.index(u))
                    if u == 9:
                        sum_selected(it + 1)
                    if u == 12 and g == 2 and not last:
                        sum_shared(b + 1)
                    if u == 13 and g == 2 and not last:
                        latents(b + 1)
                    if u == 14:
                        normalise_selected(it + 1)

            sum_shared(0)
            latents(0)
            for t in range(TT):
                sum_heads(0, t)
            sum_selected(0)
            normalise_selected(0)
            for g in range(NG):
                group(0, g, True, False)
            with pool.Fori(1, B - 1) as b:
                for g in range(NG):
                    group(b, g, False, False)
            for g in range(NG):
                group(B - 1, g, False, True)
            normalise(B * NG - 1, NU - 1)

            def block_rows(jj, half):
                if half == 0:
                    pool.wait_ge(pe_dn.sem, pe_dn.at(jj, 0 - HT))
                else:
                    pool.wait_ge(pe_dn.sem, pe_dn.at(jj, 0))
                pool.tensor_copy(fblk[half][:], routed[:, bass.ds(jj * T, T)]).then_inc(fblk_ready.sem, 1)

            def block_of(jj, last):
                for half in range(2):
                    if half == 0:
                        block_rows(jj, 1)
                    elif not last:
                        block_rows(jj + 1, 0)
                    pool.wait_ge(y_scaled.sem, y_scaled.at(jj, half + 1))
                    pool.tensor_tensor(yout[half][:].rearrange("p t c -> p (t c)"),
                                       yout[half][:].rearrange("p t c -> p (t c)"),
                                       xres[:, bass.ds((half * NBLK + jj) * TT, TT), :].rearrange("p t c -> p (t c)"),
                                       ALU.add).then_inc(y_ready.sem, 1)

            pool.wait_ge(routed_ready.sem, 1)
            pool.tensor_copy(fblk[0][:], routed[:, 0:T]).then_inc(fblk_ready.sem, 1)
            pool.wait_ge(routed_ready.sem, 2)
            with pool.Fori(0, NBLK - 1) as jj:
                block_of(jj, False)
            block_of(NBLK - 1, True)

        @block.scalar
        def _(act):
            act.wait_ge(ld_w.sem, 16 * len(loads))
            act.wait_ge(zero_done.sem, 5)
            act.wait_ge(pe_abs.sem, 1)
            act.activation(wq.rearrange("p (h d) -> p h d", h=NH)[:, :, 0:KVL],
                           bank(0)[0:QL, :].rearrange("p (h d) -> p h d", h=NH), ACT.Copy).then_inc(act_abs.sem, 1)
            side = bank(7)

            def xnT_out(pb):
                act.wait_ge(pe_xnT.sem, pe_xnT.at(pb, 1))
                act.activation(xnT[:], bank(3), ACT.Copy).then_inc(act_xnT.sem, 1)

            def cat_out(pb, i):
                act.wait_ge(pe_cat.sem, pe_cat.at(pb, i + 1))
                src = side if i else bank(3)
                if i:
                    act.activation(gl[:, 0:3], src[:, 2 * CAT:2 * CAT + 3], ACT.Copy)
                act.activation(pc[:, 2 * i:2 * i + 2].rearrange("p t c -> p (t c)"), src[:, 0:2 * CAT], ACT.Copy)\
                    .then_inc(act_cat.sem, 1)

            def nq_out(pb):
                if isinstance(pb, int) and pb == 0:
                    act.wait_ge(gq_ready.sem, 1)
                act.wait_ge(pe_nq.sem, pe_nq.at(pb, 1))
                act.activation(nqT[:], side[0:QL, :], ACT.Copy, scale=gq[:, 1:2]).then_inc(act_nq.sem, 1)

            def k1_out(pb):
                act.wait_ge(pe_k1.sem, pe_k1.at(pb, 1))
                act.activation(k1n[:], side, ACT.Copy, scale=k1s[:]).then_inc(act_k1.sem, 1)

            def imp_out(pb):
                act.wait_ge(k1_ab.sem, k1_ab.at(pb, 1))
                act.wait_ge(pe_imp.sem, pe_imp.at(pb, 1))
                act.activation(row_a, side[0:1, :], ACT.Copy).then_inc(imp_read.sem, 1)

            def shared_keys(batch):
                act.wait_ge(act_k1.sem, act_k1.at(batch, 1))
                act.activation(k1T[:], k1n[:], ACT.Copy).then_inc(k1T_ready.sem, 1)

            def gate_exp(pb):
                act.wait_ge(gl_ready.sem, gl_ready.at(pb, 1))
                act.activation(gl[:, 4:7], gl[:, 0:3], ACT.Exp, bias=gl[:, 3:4], accum_out=gl[:, 7:8])\
                    .then_inc(act_gl.sem, 1)

            def q_out(S, t):
                act.wait_ge(pe_q.sem, pe_q.at(S, t + 1))
                act.activation(qk[:, t % 2, 0:HPG].rearrange("p h d -> p (h d)"), bank(1), ACT.Copy)\
                    .then_inc(act_q.sem, 1)

            def k_out(S, t):
                act.wait_ge(pe_k.sem, pe_k.at(S, t + 1))
                act.activation(qk[:, t % 2, HPG:, KVL:HD],
                               side[:, 0:HPG * KD].rearrange("p (h d) -> p h d", h=HPG), ACT.Copy)\
                    .then_inc(act_k.sem, 1)

            def tq_out(S, t, par):
                act.wait_ge(pe_tq.sem, pe_tq.at(S, t + 1))
                src = side if t == 3 else bank(1)
                act.activation(qT[:, par, :, t * P:(t + 1) * P], src.rearrange("p (h c) -> p h c", h=HPG), ACT.Copy)\
                    .then_inc(act_tq.sem, 1)

            def tk_out(S, t, par):
                act.wait_ge(pe_tk.sem, pe_tk.at(S, t + 1))
                act.activation(k3T[:, par, :, t * P:(t + 1) * P], side.rearrange("p (h c) -> p h c", h=HPG), ACT.Copy)\
                    .then_inc(act_tk.sem, 1)

            def v3_out(S, par, batch):
                act.wait_ge(gates_ready.sem, gates_ready.at(batch, 1))
                act.wait_ge(pe_v3.sem, pe_v3.at(S, 1))
                act.activation(v13[:, par, 1].rearrange("p t h c -> p (t h c)"), bank(1), ACT.Copy, scale=gate[:, 2:3])\
                    .then_inc(act_v3.sem, 1)

            def v1_out(S, par):
                act.wait_ge(pe_v1.sem, pe_v1.at(S, 1))
                act.activation(v13[:, par, 0].rearrange("p t h c -> p (t h c)"), side, ACT.Copy, scale=gate[:, 0:1])\
                    .then_inc(act_v1.sem, 1)

            def sel_out(S):
                act.wait_ge(pe_sel.sem, pe_sel.at(S, 1))
                act.activation(ksraw[:].rearrange("p h d -> p (h d)"), side[0:KEEP, 0:HPG * KD], ACT.Copy)
                act.activation(kstok[0:KEEP, :, KVL + ROPE:HD],
                               side[0:KEEP, 0:HPG * KD].rearrange("p (h d) -> p h d", h=HPG)[:, :, ROPE:KD],
                               ACT.Copy).then_inc(act_sel.sem, 1)

            def ksT_out(S):
                act.wait_ge(pe_ksT.sem, pe_ksT.at(S, 1))
                act.activation(ksT[:], side.rearrange("p (h k) -> p h k", h=HPG)[:, :, 0:KEEP], ACT.Copy)\
                    .then_inc(act_ksT.sem, 1)

            def s2T_out(S):
                act.wait_ge(pe_s2T.sem, pe_s2T.at(S, 1))
                act.activation(p2[:].rearrange("p n k -> p (n k)"), side, ACT.Copy).then_inc(act_s2T.sem, 1)

            def selected_exp(S):
                act.wait_ge(s2_shift.sem, s2_shift.at(S, 1))
                act.activation(p2[:], p2[:], ACT.Exp).then_inc(act_e2.sem, 1)

            def t2_out(S):
                act.wait_ge(pe_t2.sem, pe_t2.at(S, 1))
                act.activation(p2T[:], side, ACT.Copy).then_inc(act_t2.sem, 1)

            def exponentials(it, u, first):
                act.wait_ge(maxed.sem, maxed.at(it, u + 1))
                if u >= 3:
                    act.wait_ge(turned.sem, turned.at(it, u - 2))
                elif not first:
                    act.wait_ge(turned.sem, turned.at(it - 1, NU + u - 2))
                for a in range(2):
                    ins = act.activation(probs(u)[:, a], score_tiles(u)[:, a], ACT.Exp,
                                         bias=nmax[:, u % 2, a:a + 1], accum_out=den[:, u % 2, a:a + 1])
                ins.then_inc(weighed.sem, 1)

            def att_out(it, tb=None):
                act.wait_ge(summed.sem, summed.at(it, TT))
                if tb is not None:
                    act.wait_ge(spilled.sem, spilled.at(tb, 16))
                act.activation(attT[:], bank(6), ACT.Copy).then_inc(att_ready.sem, 1)

            def x2T_out(tb):
                act.wait_ge(pe_x2T.sem, pe_x2T.at(tb, 1))
                act.activation(attT[:], side, ACT.Copy).then_inc(act_x2T.sem, 1)

            def runs_out(tb, final=False):
                act.wait_ge(pe_runs.sem, pe_runs.at(tb, 1))
                act.wait_ge(presorted.sem, presorted.at(tb, 0))
                act.wait_ge(score_kept.sem, score_kept.at(tb, 0))
                for dst in [probT[:]] + [score[EXPERTS:P, (NBLK - 1) * T:]] * final:
                    dst = dst.rearrange("e (i s c) -> e i s c", s=2, c=P)
                    for s in range(2):
                        src = bank(3)[s * EXPERTS:(s + 1) * EXPERTS, 0:2 * P]
                        act.activation(dst[:, :, s], src.rearrange("e (i c) -> e i c", c=P), ACT.Copy)
                ins = act.activation(parts[0][:], bank(3)[:, 0:2 * P], ACT.Copy)
                ins.then_inc(act_runs.sem, 1)

            def router_exp(tb):
                act.wait_ge(lg_ready.sem, lg_ready.at(tb, 1))
                act.activation(sq[:, 2:4], sq[:, 0:2], ACT.Exp).then_inc(act_lg.sem, 1)

            def group(b, g, first, last):
                it = b * NG + g
                S, par = it + 1, (g + 1) % 2
                sides = not (last and g == NG - 1)
                batch = b + (g == NG - 1)
                for u in range(NU):
                    if sides:
                        if u in PROJ_SLOT:
                            q_out(S, PROJ_SLOT.index(u))
                        if u in TURN_SLOT:
                            tq_out(S, TURN_SLOT.index(u), par)
                        if u == 8:
                            sel_out(S)
                        if u == 10:
                            tk_out(S, 3, par)
                        if u == 11:
                            s2T_out(S)
                        if g == 2 and not last:
                            if u == 15:
                                k1_out(b + 1)
                    if g == 0 and not first and u == 13:
                        x2T_out(b - 1)
                    if u == NU - 1 and g == NG - 1 and not last:
                        act.wait_ge(scored.sem, scored.at(it, NU))
                        shared_keys(b + 1)
                    exponentials(it, u, first and g == 0)
                    if sides:
                        if u in PROJ_SLOT:
                            k_out(S, PROJ_SLOT.index(u))
                        if u in TURN_SLOT[:3]:
                            tk_out(S, TURN_SLOT.index(u), par)
                        if u == 2:
                            v3_out(S, par, batch)
                            v1_out(S, par)
                        if u == 10:
                            ksT_out(S)
                        if u == 13 and g == 2 and not last:
                            imp_out(b + 1)
                        if u == 14 and g == 2 and not last:
                            nq_out(b + 1)
                        if u == 13:
                            selected_exp(S)
                        if u == 15:
                            t2_out(S)
                        if g == 2 and not last:
                            if u == 6:
                                xnT_out(b + 1)
                            if u == 7:
                                cat_out(b + 1, 0)
                            if u == 9:
                                cat_out(b + 1, 1)
                            if u == 12:
                                gate_exp(b + 1)
                        if g == 0 and not first and u == 15:
                            router_exp(b - 1)
                        if g == 1 and not first and u == 1:
                            runs_out(b - 1)
                    if u == 3 and not (first and g == 0):
                        att_out(it - 1, b - 1 if g == 1 and not first else None)

            xnT_out(0)
            cat_out(0, 0)
            cat_out(0, 1)
            gate_exp(0)
            imp_out(0)
            nq_out(0)
            k1_out(0)
            shared_keys(0)
            act.wait_ge(ld_later.sem, 16 * len(loads_later))
            q_out(0, 0)
            k_out(0, 0)
            for t in range(TT):
                if t < TT - 1:
                    q_out(0, t + 1)
                    k_out(0, t + 1)
                tq_out(0, t, 0)
                tk_out(0, t, 0)
            v3_out(0, 0, 0)
            v1_out(0, 0)
            sel_out(0)
            ksT_out(0)
            s2T_out(0)
            selected_exp(0)
            t2_out(0)
            for g in range(NG):
                group(0, g, True, False)
            with act.Fori(1, B - 1) as b:
                for g in range(NG):
                    group(b, g, False, False)
            for g in range(NG):
                group(B - 1, g, False, True)
            att_out(B * NG - 1)
            x2T_out(B - 1)
            router_exp(B - 1)

            runs_out(B - 1, True)
            act.wait_ge(above_ready.sem, 1)
            act.activation(sortB, above, ACT.Copy, accum_out=cabove[:]).then_inc(above_counted.sem, 1)

            with act.Fori(0, NBLK) as jj:
                for n in range(2 * HT):
                    m = n % HT
                    act.wait_ge(pe_up.sem, pe_up.at(jj, n + 1))
                    if n >= 2:
                        act.wait_ge(gate_mul.sem, gate_mul.at(jj, n - 1))
                    else:
                        act.wait_ge(gate_mul.sem, gate_mul.at(jj, 0))
                    act.activation(siluT[:, n % 2], bank(n % 2), ACT.Silu, bias=bup[:, m:m + 1])\
                        .then_inc(act_up.sem, 1)

        @block.tensor
        def _(pe):
            pe.sem_inc(pe_dn.sem, pe_dn.base)
            pe.wait_ge(ld_w.sem, 16 * len(loads))
            pe.wait_ge(cast_done.sem, 2)
            for h in range(NH):
                mm = pe.matmul(bank(0)[0:QL, h * KVL:(h + 1) * KVL], dqn[:, h * QL:(h + 1) * QL],
                               dkn[:, h * KVL:(h + 1) * KVL], start=True, stop=True)
            mm.then_inc(pe_abs.sem, 1)
            pe.wait_ge(act_abs.sem, 1)
            side, side_b, side_c = bank(7), bank(1), bank(3)

            def tile(t):
                return slice(t * P, (t + 1) * P)

            def xnT_in(pb):
                pe.wait_ge(xn_ready.sem, xn_ready.at(pb, 1))
                for t in range(TT):
                    mm = pe.transpose(side_c[:, tile(t)], xn[:, t], ident)
                mm.then_inc(pe_xnT.sem, 1)

            def cat_in(pb, i):
                dst = side if i else side_c
                for t in range(2):
                    mm = pe.matmul(dst[:, t * CAT:(t + 1) * CAT], xnT[:, tile(2 * i + t)], wcat[:],
                                   start=True, stop=True)
                if i:
                    pe.wait_ge(xsb_ready.sem, xsb_ready.at(pb, 1))
                    mm = pe.matmul(dst[:, 2 * CAT:2 * CAT + 3], xsb[:], wgate[:], start=True, stop=True)
                mm.then_inc(pe_cat.sem, 1)

            def imp_in(pb):
                pe.matmul(side[0:1, :], wimp[:], xnT[:], start=True, stop=True).then_inc(pe_imp.sem, 1)

            def nq_in(pb):
                pe.wait_ge(nq_ready.sem, nq_ready.at(pb, 1))
                for t in range(TT):
                    mm = pe.transpose(side[0:QL, tile(t)], pc[:, t, 0:QL], ident)
                mm.then_inc(pe_nq.sem, 1)

            def k1_in(pb):
                pe.wait_ge(k1_ready.sem, k1_ready.at(pb, 1))
                for t in range(TT):
                    mm = pe.transpose(side[:, tile(t)], k1[:, t], ident)
                mm.then_inc(pe_k1.sem, 1)

            def key_in(pb):
                pe.wait_ge(key_row.sem, key_row.at(pb, 1))
                for t in range(TT):
                    mm = pe.matmul(side_c[:, t:t + 1], row_a[:, tile(t)], K("ones", slice(0, 1))[:, 0:1],
                                   start=True, stop=True)
                mm.then_inc(pe_key.sem, 1)

            def selT_in(pb):
                pe.wait_ge(sel_ready.sem, sel_ready.at(pb, 1))
                for t in range(TT):
                    mm = pe.matmul(side_c[:, 0:KEEP], xn[:, t], selm[:, t], start=(t == 0), stop=(t == TT - 1))
                mm.then_inc(pe_selT.sem, 1)

            def q_in(S, t, gn, batch):
                if gn == 0 and t == 0:
                    pe.wait_ge(act_nq.sem, act_nq.at(batch, 1))
                pe.matmul(side_b, nqT[:, tile(t)], wq[:, gn * HPG * HD:(gn + 1) * HPG * HD], start=True, stop=True)\
                    .then_inc(pe_q.sem, 1)

            def k_in(S, t, gn):
                pe.matmul(side[:, 0:HPG * KD], xnT[:, tile(t)], wink[:, gn * HPG * KD:(gn + 1) * HPG * KD],
                          start=True, stop=True).then_inc(pe_k.sem, 1)

            def tq_in(S, t):
                pe.wait_ge(rope_sum.sem, rope_sum.at(S, t + 1))
                dst = side if t == 3 else side_b
                for h in range(HPG):
                    mm = pe.transpose(dst[:, tile(h)], qk[:, t % 2, h], ident)
                mm.then_inc(pe_tq.sem, 1)

            def tk_in(S, t):
                for h in range(HPG):
                    mm = pe.transpose(side[:, tile(h)], qk[:, t % 2, HPG + h], ident)
                mm.then_inc(pe_tk.sem, 1)

            def v3_in(S, gn):
                for t in range(TT):
                    mm = pe.matmul(side_b[:, tile(t)], xnT[:, tile(t)], winv[:, gn * HPG * VD:(gn + 1) * HPG * VD],
                                   start=True, stop=True)
                mm.then_inc(pe_v3.sem, 1)

            def v1_in(S, gn, batch):
                pe.wait_ge(act_k1.sem, act_k1.at(batch, 1))
                for t in range(TT):
                    mm = pe.matmul(side[:, tile(t)], k1n[0:KVL, tile(t)], wdv[:, gn * HPG * VD:(gn + 1) * HPG * VD],
                                   start=True, stop=True)
                mm.then_inc(pe_v1.sem, 1)

            def sel_in(S, gn, batch):
                pe.wait_ge(selT_ready.sem, selT_ready.at(batch, 1))
                pe.matmul(side[0:KEEP, 0:HPG * KD], selT[:, 0], wselk[:, gn * HPG * KD:(gn + 1) * HPG * KD],
                          start=True, stop=True)
                pe.matmul(side[:, HPG * KD:], selT[:].rearrange("p h k -> p (h k)"),
                          wselv[:, gn * HPG * VD:(gn + 1) * HPG * VD], start=True, stop=True).then_inc(pe_sel.sem, 1)

            def ksT_in(S):
                pe.wait_ge(ks_sum.sem, ks_sum.at(S, 1))
                for h in range(HPG):
                    mm = pe.transpose(side[:, tile(h)], kstok[:, h], ident)
                mm.then_inc(pe_ksT.sem, 1)

            def s2T_in(S, par):
                pe.wait_ge(act_ksT.sem, act_ksT.at(S, 1))
                pe.wait_ge(act_tq.sem, act_tq.at(S, TT))
                for h in range(HPG):
                    mm = pe.matmul(side[h * KEEP:(h + 1) * KEEP, :], ksT[:, h], qT[:, par, h], start=True, stop=True,
                                   tile_position=(0, h * KEEP))
                mm.then_inc(pe_s2T.sem, 1)

            def s2_in(S):
                pe.wait_ge(act_s2T.sem, act_s2T.at(S, 1))
                for t in range(TT):
                    mm = pe.transpose(side[:, tile(t)], p2[:, t * HPG:(t + 1) * HPG].rearrange("p h k -> p (h k)"),
                                      ident)
                mm.then_inc(pe_s2.sem, 1)

            def t2_in(S):
                pe.wait_ge(p2_ready.sem, p2_ready.at(S, 1))
                for t in range(TT):
                    mm = pe.transpose(side[:, tile(t)], p2[:, t * HPG:(t + 1) * HPG].rearrange("p h k -> p (h k)"),
                                      ident)
                mm.then_inc(pe_t2.sem, 1)

            def scores(it, b, g, u, first):
                qt, h = divmod(u, HPG)
                W, par = span(u), g % 2
                if u == 0:
                    pe.wait_ge(act_tk.sem, act_tk.at(it, TT))
                    if g == 0:
                        pe.wait_ge(k1T_ready.sem, k1T_ready.at(b, 1))
                if u >= 2:
                    pe.wait_ge(weighed.sem, weighed.at(it, u - 1))
                elif not first:
                    pe.wait_ge(weighed.sem, weighed.at(it - 1, NU + u - 1))
                out_ = score_tiles(u)
                for a, keys in ((0, k1T), (1, k3T[:, par, h])):
                    pe.matmul(out_[:, a], qT[:, par, h, tile(qt)], keys[:, 0:W],
                              start=True, stop=False, skip_group_check=True)
                    mm = pe.matmul(out_[:, a, tile(qt)], identb[:], maskb[:], start=False, stop=True,
                                   skip_group_check=True)
                mm.then_inc(scored.sem, 1)

            def turn(it, u, start=False):
                pe.wait_ge(normed.sem, normed.at(it, u + 1))
                if u > NARROW:
                    pe.wait_ge(pT_ready.sem, pT_ready.at(it, u))
                elif u >= 2:
                    pe.wait_ge(pT_ready.sem, pT_ready.at(it, u if u == NARROW else u - 1))
                elif not start:
                    pe.wait_ge(pT_ready.sem, pT_ready.at(it - 1, NU))
                for a in range(2):
                    for kb in range(u // HPG + 1):
                        mm = pe.transpose(turn_tiles(u)[:, a, tile(kb)], probs(u)[:, a, tile(kb)], ident)
                mm.then_inc(turned.sem, 1)

            def weigh_selected(it, first):
                pe.wait_ge(vsd_ready.sem, vsd_ready.at(it, 1))
                pe.wait_ge(act_t2.sem, act_t2.at(it, 1))
                if not first:
                    pe.wait_ge(att_ready.sem, att_ready.at(it - 1, 1))
                pe.matmul(bank(6), vsd[:], p2T[:], start=True, stop=False, skip_group_check=True)

            def weigh_values(it, g, qt):
                pe.wait_ge(pT_ready.sem, pT_ready.at(it, (qt + 1) * HPG))
                pe.wait_ge(act_v1.sem, act_v1.at(it, 1))
                for a in range(2):
                    for kb in range(qt + 1):
                        for h in range(HPG):
                            mm = pe.matmul(bank(6)[h * VD:(h + 1) * VD, tile(qt)], v13[:, g % 2, a, kb, h],
                                           turned_tile(qt)[:, h, a, tile(kb)], start=False,
                                           stop=(a == 1 and kb == qt), skip_group_check=True,
                                           tile_position=(0, h * VD))
                mm.then_inc(summed.sem, 1)

            def project(it, g):
                pe.wait_ge(att_ready.sem, att_ready.at(it, 1))
                for t in range(TT):
                    mm = pe.matmul(side_c[:, tile(t)], attT[:, tile(t)], wproj[:, g * C:(g + 1) * C],
                                   start=True, stop=True)
                mm.then_inc(pe_y.sem, 1)

            def x2T_in(tb):
                pe.wait_ge(x2_ready.sem, x2_ready.at(tb, 1))
                for t in range(TT):
                    mm = pe.transpose(side[:, tile(t)], xn[:, t], ident)
                mm.then_inc(pe_x2T.sem, 1)

            def router_in(tb):
                pe.wait_ge(act_x2T.sem, act_x2T.at(tb, 1))
                for t in range(TT):
                    mm = pe.matmul(side[:, t * EXPERTS:(t + 1) * EXPERTS], attT[:, tile(t)], wr[:],
                                   start=True, stop=True)
                mm.then_inc(pe_lg.sem, 1)

            def runs_in(tb):
                pe.wait_ge(probs_ready.sem, probs_ready.at(tb, 1))
                for i in range(TT // 2):
                    mm = pe.transpose(side_c[:, tile(i)], ptok[:, 2 * i:2 * i + 2].rearrange("p t e -> p (t e)"),
                                      ident)
                mm.then_inc(pe_runs.sem, 1)

            def group(b, g, first, last):
                it = b * NG + g
                S, gn, par = it + 1, (g + 1) % NG, (g + 1) % 2
                batch = b + (g == NG - 1)
                sides = not (last and g == NG - 1)
                start = first and g == 0
                opening = g == 2 and not last
                closing = g == 0 and not first
                for u in range(NU):
                    if u == 8 and sides:
                        pe.wait_ge(act_tq.sem, act_tq.at(S, 3))
                    if u == 9 and opening:
                        pe.wait_ge(act_cat.sem, act_cat.at(b + 1, 1))
                    elif u == 9 and sides and g == 3:
                        pe.wait_ge(selT_ready.sem, selT_ready.at(b + 1, 1))
                    elif u == 9 and not start:
                        pe.wait_ge(x_done.sem, x_done.at(it - 1, 1))
                    scores(it, b, g, u, start)
                    if sides:
                        if u == 0:
                            q_in(S, 0, gn, batch)
                        if u == 1:
                            pe.wait_ge(act_q.sem, act_q.at(S, 1))
                            q_in(S, 1, gn, batch)
                        if u == 3:
                            pe.wait_ge(act_v3.sem, act_v3.at(S, 1))
                            tq_in(S, 0)
                        if u == 4:
                            pe.wait_ge(act_tq.sem, act_tq.at(S, 1))
                            q_in(S, 2, gn, batch)
                        if u == 5:
                            pe.wait_ge(act_q.sem, act_q.at(S, 3))
                            tq_in(S, 1)
                        if u == 6:
                            pe.wait_ge(act_tq.sem, act_tq.at(S, 2))
                            q_in(S, 3, gn, batch)
                        if u == 7:
                            pe.wait_ge(act_q.sem, act_q.at(S, 4))
                            tq_in(S, 2)
                        if u == 8:
                            pe.wait_ge(act_tk.sem, act_tk.at(S, 3))
                            sel_in(S, gn, batch)
                        if u == 9:
                            pe.wait_ge(vsd_ready.sem, vsd_ready.at(S, 1))
                            tq_in(S, 3)
                        if u == 10:
                            if opening:
                                pe.wait_ge(act_cat.sem, act_cat.at(b + 1, 2))
                            else:
                                pe.wait_ge(act_tq.sem, act_tq.at(S, 4))
                            tk_in(S, 3)
                        if u == 11:
                            pe.wait_ge(act_ksT.sem, act_ksT.at(S, 1))
                            s2T_in(S, par)
                    if opening:
                        if u == 15:
                            pe.wait_ge(act_nq.sem, act_nq.at(b + 1, 1))
                            k1_in(b + 1)
                    if closing:
                        if u == 13:
                            pe.wait_ge(s2_shift.sem, s2_shift.at(S, 1))
                            x2T_in(b - 1)
                        if u == 14:
                            router_in(b - 1)
                    if u >= 2:
                        turn(it, u - 2, start)
                    elif not start:
                        turn(it - 1, NU + u - 2)
                    if u % HPG == 2:
                        if u >= 6:
                            weigh_values(it, g, (u - 6) // HPG)
                        elif not start:
                            weigh_values(it - 1, g + 1, TT - 1)
                    if u == 5:
                        weigh_selected(it, start)
                    if sides:
                        if u == 0:
                            pe.wait_ge(act_t2.sem, act_t2.at(it, 1))
                            k_in(S, 0, gn)
                        if u == 1:
                            pe.wait_ge(act_k.sem, act_k.at(S, 1))
                            k_in(S, 1, gn)
                        if u == 2:
                            pe.wait_ge(act_q.sem, act_q.at(S, 2))
                            v3_in(S, gn)
                            pe.wait_ge(act_k.sem, act_k.at(S, 2))
                            v1_in(S, gn, batch)
                        if u == 3:
                            pe.wait_ge(act_v1.sem, act_v1.at(S, 1))
                            tk_in(S, 0)
                        if u == 4:
                            pe.wait_ge(act_tk.sem, act_tk.at(S, 1))
                            k_in(S, 2, gn)
                        if u == 5:
                            pe.wait_ge(act_k.sem, act_k.at(S, 3))
                            tk_in(S, 1)
                        if u == 6:
                            pe.wait_ge(act_tk.sem, act_tk.at(S, 2))
                            k_in(S, 3, gn)
                        if u == 7:
                            pe.wait_ge(act_k.sem, act_k.at(S, 4))
                            tk_in(S, 2)
                        if u == 10:
                            pe.wait_ge(act_tk.sem, act_tk.at(S, 4))
                            ksT_in(S)
                        if u == 12:
                            s2_in(S)
                    if g == 1 and not first and u == 1:
                        runs_in(b - 1)
                    if opening:
                        if u == 9:
                            pe.wait_ge(act_tq.sem, act_tq.at(S, 4))
                            cat_in(b + 1, 1)
                    if opening and u == 14:
                        pe.wait_ge(imp_read.sem, imp_read.at(b + 1, 1))
                        nq_in(b + 1)
                    if opening and u == 13:
                        pe.wait_ge(s2_shift.sem, s2_shift.at(S, 1))
                        imp_in(b + 1)
                    if u == 15 and sides:
                        if opening:
                            pe.wait_ge(act_k1.sem, act_k1.at(b + 1, 1))
                        elif closing:
                            pe.wait_ge(lg_read.sem, lg_read.at(b - 1, 1))
                        else:
                            pe.wait_ge(s2_shift.sem, s2_shift.at(S, 1))
                        t2_in(S)
                    if g == 1 and not first and u == 4:
                        pe.wait_ge(act_runs.sem, act_runs.at(b - 1, 1))
                    if u == 4 and not start:
                        project(it - 1, (g - 1) % NG)
                    if opening:
                        if u == 6:
                            pe.wait_ge(x_done.sem, x_done.at(it - 1, 1))
                            xnT_in(b + 1)
                        if u == 7:
                            pe.wait_ge(act_xnT.sem, act_xnT.at(b + 1, 1))
                            cat_in(b + 1, 0)
                    if sides and g == 3:
                        if u == 5:
                            pe.wait_ge(x_done.sem, x_done.at(it - 1, 1))
                            key_in(b + 1)
                        if u == 6:
                            selT_in(b + 1)

            xnT_in(0)
            pe.wait_ge(act_xnT.sem, act_xnT.at(0, 1))
            cat_in(0, 0)
            pe.wait_ge(act_cat.sem, act_cat.at(0, 1))
            cat_in(0, 1)
            pe.wait_ge(act_cat.sem, act_cat.at(0, 2))
            imp_in(0)
            pe.wait_ge(imp_read.sem, imp_read.at(0, 1))
            nq_in(0)
            pe.wait_ge(act_nq.sem, act_nq.at(0, 1))
            k1_in(0)
            pe.wait_ge(act_k1.sem, act_k1.at(0, 1))
            q_in(0, 0, 0, 0)
            pe.wait_ge(ld_later.sem, 16 * len(loads_later))
            k_in(0, 0, 0)
            pe.wait_ge(act_q.sem, act_q.at(0, 1))
            q_in(0, 1, 0, 0)
            pe.wait_ge(act_k.sem, act_k.at(0, 1))
            k_in(0, 1, 0)
            pe.wait_ge(act_q.sem, act_q.at(0, 2))
            tq_in(0, 0)
            pe.wait_ge(act_k.sem, act_k.at(0, 2))
            tk_in(0, 0)
            for t in range(1, TT):
                if t < TT - 1:
                    pe.wait_ge(act_tq.sem, act_tq.at(0, t))
                    q_in(0, t + 1, 0, 0)
                    pe.wait_ge(act_tk.sem, act_tk.at(0, t))
                    k_in(0, t + 1, 0)
                    pe.wait_ge(act_q.sem, act_q.at(0, t + 2))
                    tq_in(0, t)
                    pe.wait_ge(act_k.sem, act_k.at(0, t + 2))
                    tk_in(0, t)
                else:
                    pe.wait_ge(act_tk.sem, act_tk.at(0, t))
                    tq_in(0, t)
                    pe.wait_ge(act_tq.sem, act_tq.at(0, t + 1))
                    tk_in(0, t)
            v3_in(0, 0)
            pe.wait_ge(act_tk.sem, act_tk.at(0, TT))
            v1_in(0, 0, 0)
            key_in(0)
            selT_in(0)
            pe.wait_ge(act_v3.sem, act_v3.at(0, 1))
            pe.wait_ge(act_v1.sem, act_v1.at(0, 1))
            sel_in(0, 0, 0)
            pe.wait_ge(vsd_ready.sem, vsd_ready.at(0, 1))
            ksT_in(0)
            s2T_in(0, 0)
            s2_in(0)
            pe.wait_ge(s2_shift.sem, s2_shift.at(0, 1))
            t2_in(0)
            for g in range(NG):
                group(0, g, True, False)
            with pe.Fori(1, B - 1) as b:
                for g in range(NG):
                    group(b, g, False, False)
            for g in range(NG):
                group(B - 1, g, False, True)
            it = B * NG - 1
            turn(it, NU - 2)
            turn(it, NU - 1)
            weigh_values(it, NG - 1, TT - 1)
            project(it, NG - 1)
            x2T_in(B - 1)
            router_in(B - 1)
            runs_in(B - 1)

            for n in range(len(SCORE_ROUNDS) + 1 + len(INDEX_ROUNDS)):
                width = 1 if n == len(SCORE_ROUNDS) else CAND
                pe.wait_ge(cnt_ready.sem, n + 1)
                pe.matmul(bank(4)[:, 0:width], K("ones"), cnt[:, 0:width], start=True, stop=True).then_inc(pe_cnt.sem, 1)
            n += 1
            for m, c in (("pair", 0), ("lower", 1)):
                n += 1
                pe.wait_ge(cnt_ready.sem, n)
                pe.matmul(bank(4)[:, c:c + 1], K(m), cnt[:, c:c + 1], start=True, stop=True).then_inc(pe_cnt.sem, 1)
            pe.wait_ge(above_counted.sem, 1)
            pe.matmul(bank(5)[:, 0:1], K("pair"), cabove[:], start=True, stop=True).then_inc(pe_cnt.sem, 1)
            pe.wait_ge(ld_e.sem, 16 * (len(loads_experts) + 1))
            def up(jj, n):
                half, m = divmod(n, HT)
                s = n % 2
                if n >= 2 or not isinstance(jj, int) or jj > 0:
                    pe.wait_ge(act_up.sem, act_up.at(jj, n - 1))
                    pe.wait_ge(gate_mul.sem, gate_mul.at(jj, n - 1))
                    pe.wait_ge(h_ready.sem, h_ready.at(jj, n - 1))
                cols = bass.ds((half * NBLK + jj) * T, T)
                pe.matmul(bank(s), wup[:, m * P:(m + 1) * P], x2nT[:, cols], start=True, stop=True)\
                    .then_inc(pe_up.sem, 1)
                pe.matmul(bank(2 + s), wgt[:, m * P:(m + 1) * P], x2nT[:, cols], start=True, stop=True)\
                    .then_inc(pe_gt.sem, 1)
                if m == 0:
                    pe.wait_ge(placed.sem, placed.at(jj, (half + 1) * 96))
                mm = pe.matmul(bank(4 + s), selw[0:3 * SORT, m], fsel[:, half, m * EPT // SORT],
                               start=True, stop=True)
                mm.then_inc(pe_f.sem, 1)

            def down(jj, n):
                half, m = divmod(n, HT)
                if m == 0:
                    pe.wait_ge(y_scaled.sem, y_scaled.at(jj, half))
                    pe.wait_ge(fblk_ready.sem, fblk_ready.at(jj, half + 1))
                    for t in range(TT):
                        pe.matmul(bank(7)[:, t:t + 1], fblk[half][:, t * P:(t + 1) * P], K("half")[:, half:half + 1],
                                  start=True, stop=True)
                    for t in range(TT):
                        pe.matmul(bank(6)[:, t * C:(t + 1) * C], fblk[half][:, t * P:(t + 1) * P], bdn[:, half],
                                  start=(t == 0), stop=False, skip_group_check=True)
                pe.wait_ge(h_ready.sem, h_ready.at(jj, n + 1))
                for t in range(TT):
                    mm = pe.matmul(bank(6)[:, t * C:(t + 1) * C], hT[:, n % 2, t * P:(t + 1) * P],
                                   wdn[:, m * C:(m + 1) * C], start=False, stop=(m == HT - 1),
                                   skip_group_check=True)
                mm.then_inc(pe_dn.sem, 1)

            def block_of(jj, last):
                for n in range(2 * HT):
                    if n + 1 < 2 * HT:
                        up(jj, n + 1)
                    elif not last:
                        up(jj + 1, 0)
                    down(jj, n)

            up(0, 0)
            with pe.Fori(0, NBLK - 1) as jj:
                block_of(jj, False)
            block_of(NBLK - 1, True)

        @block.vector
        def _(dve):
            dve.memset(carrier[:], 0.0)
            for f in (gate_mul, y_scaled, presorted):
                dve.sem_inc(f.sem, f.base)
            dve.wait_ge(ld_x.sem, 16)
            side = bank(7)

            def rsqrt(step, v, y, t, parts=(0, 1)):
                if 0 in parts:
                    step(dve.tensor_scalar(t.bitcast(I32), v.bitcast(I32), 1, None, ALU.logical_shift_right))
                    step(dve.tensor_scalar(y.bitcast(I32), t.bitcast(I32), -1.0, RSQRT_MAGIC, ALU.mult, ALU.add))
                for _ in range((0 in parts) + 2 * (1 in parts)):
                    step(dve.scalar_tensor_tensor(t, y, -0.5, y, ALU.mult, ALU.mult))
                    step(dve.tensor_tensor(t, t, v, ALU.mult))
                    step(dve.scalar_tensor_tensor(y, t, 1.5, y, ALU.add, ALU.mult))

            def norm(step, rows, k, ready):
                mean, var, y, tmp = st[:, 0:4], st[:, 4:8], st[:, 8:12], st[:, 12:16]
                if k == 0:
                    step(dve.tensor_scalar(xn[:], rows, 1.0, None, ALU.mult))
                    step(dve.tensor_reduce(mean, xn[:], AX.X, ALU.add))
                if k == 1:
                    step(dve.tensor_scalar(mean, mean, 1.0 / C, None, ALU.mult))
                    step(dve.tensor_tensor(xn[:], xn[:], mean.unsqueeze(2).to_broadcast([P, TT, C]), ALU.subtract))
                if k == 2:
                    step(dve.tensor_tensor(sq[:], xn[:], xn[:], ALU.mult))
                    step(dve.tensor_reduce(var, sq[:], AX.X, ALU.add))
                if k == 3:
                    step(dve.tensor_scalar(var, var, 1.0 / C, EPS_LN, ALU.mult, ALU.add))
                    rsqrt(step, var, y, tmp, (0,))
                if k == 4:
                    rsqrt(step, var, y, tmp, (1,))
                if k == 5:
                    dve.tensor_tensor(xn[:], xn[:], y.unsqueeze(2).to_broadcast([P, TT, C]), ALU.mult)\
                        .then_inc(ready.sem, 1)

            def rope(src, cosine, sine, a, b_):
                H = ROPE // 2
                dve.tensor_tensor(a, src, cosine, ALU.mult)
                dve.tensor_tensor(b_[..., 0:H], src[..., H:ROPE], sine[..., 0:H], ALU.mult)
                return dve.tensor_tensor(b_[..., H:ROPE], src[..., 0:H], sine[..., H:ROPE], ALU.mult)

            def table(name):
                return K(name).rearrange("p (t c) -> p t c", t=TT)

            def rows_of(batch):
                return xres[:, bass.ds(batch * TT, TT), :]

            def mean_of_batch(step, pb):
                dve.wait_ge(act_xnT.sem, act_xnT.at(pb, 1))
                step(dve.tensor_reduce(st[:, 16:17], xnT[:], AX.X, ALU.add))
                dve.tensor_scalar(xsb[:], K("ones"), st[:, 16:17], 1.0 / T, ALU.mult, ALU.mult)\
                    .then_inc(xsb_ready.sem, 1)

            ms = st[:, 20:28]

            def squares(step, pb):
                dve.wait_ge(act_cat.sem, act_cat.at(pb, 2))
                step(dve.tensor_tensor(sq[:], pc[:, :, 0:QL + KVL], pc[:, :, 0:QL + KVL], ALU.mult))
                step(dve.tensor_reduce(ms[:, 0:4], sq[:, :, 0:QL], AX.X, ALU.add))
                step(dve.tensor_reduce(ms[:, 4:8], sq[:, :, QL:QL + KVL], AX.X, ALU.add))

            def roots(step, parts=(0, 1)):
                if 0 in parts:
                    step(dve.tensor_scalar(ms[:, 0:4], ms[:, 0:4], 1.0 / QL, EPS_RMS, ALU.mult, ALU.add))
                    step(dve.tensor_scalar(ms[:, 4:8], ms[:, 4:8], 1.0 / KVL, EPS_RMS, ALU.mult, ALU.add))
                rsqrt(step, ms, st[:, 28:36], st[:, 36:44], parts)
                if 1 in parts:
                    dve.sem_inc(roots_ready.sem, 1)

            def rope_shared(pb):
                if not (isinstance(pb, int) and pb == 0):
                    dve.wait_ge(ks_sum.sem, ks_sum.at(pb * NG - 1, 1))
                rope(pc[:, :, QL + KVL:], table("ropeC"), table("ropeS"), ra[:, 0:TT], rb[:, 0:TT])\
                    .then_inc(k1_ab.sem, 1)

            def gate_logits(step, pb):
                dve.wait_ge(act_cat.sem, act_cat.at(pb, 2))
                dve.tensor_reduce(gl[:, 3:4], gl[:, 0:3], AX.X, ALU.max, negate=True).then_inc(gl_ready.sem, 1)

            def gates(step, pb):
                dve.wait_ge(act_gl.sem, act_gl.at(pb, 1))
                step(dve.reciprocal(gl[:, 8:9], gl[:, 7:8]))
                if not (isinstance(pb, int) and pb == 0):
                    dve.wait_ge(act_v1.sem, act_v1.at(pb * NG - 1, 1))
                dve.tensor_scalar(gate[:], gl[:, 4:7], gl[:, 8:9], None, ALU.mult).then_inc(gates_ready.sem, 1)

            def top_round(step):
                dve.tensor_copy(carrier[:, 0:1], carrier[:, 1:2])
                step(dve.max(top8[:], row_a))
                dve.tensor_copy(carrier[:, 0:1], carrier[:, 1:2])
                step(dve.match_replace(row_a, top8[:], row_a, TAKEN))

            def ranks(step, pb):
                dve.wait_ge(act_nq.sem, act_nq.at(pb, 1))
                step(dve.tensor_scalar(row_b, row_a, TAKEN, None, ALU.is_equal))
                step(dve.tensor_tensor_scan(row_a, row_b, row_b, 0.0, ALU.add, ALU.max))
                dve.tensor_tensor(row_a, row_a, row_b, ALU.mult).then_inc(key_row.sem, 1)

            def one_hot(step, pb):
                dve.wait_ge(pe_key.sem, pe_key.at(pb, 1))
                step(dve.tensor_copy(key[:], bank(3)[:, 0:TT]))
                dve.tensor_tensor(selm[:], K("count").unsqueeze(1).to_broadcast([P, TT, KEEP]),
                                  key[:].unsqueeze(2).to_broadcast([P, TT, KEEP]), ALU.is_equal)\
                    .then_inc(sel_ready.sem, 1)

            def selT_out(pb):
                dve.wait_ge(pe_selT.sem, pe_selT.at(pb, 1))
                dve.tensor_copy(selT[:], bank(3)[:, 0:KEEP].unsqueeze(1).to_broadcast([P, HPG, KEEP]))\
                    .then_inc(selT_ready.sem, 1)

            def rope_heads(S, t):
                dve.wait_ge(act_k.sem, act_k.at(S, t + 1))
                if t > 0:
                    dve.wait_ge(rope_sum.sem, rope_sum.at(S, t))
                cs = table("ropeC")[:, t:t + 1].to_broadcast([P, 2 * HPG, ROPE])
                sn = table("ropeS")[:, t:t + 1].to_broadcast([P, 2 * HPG, ROPE])
                rope(qk[:, t % 2, :, KVL:KVL + ROPE], cs, sn, ra[:], rb[:]).then_inc(rope_ab.sem, 1)

            def vsd_out(S):
                dve.wait_ge(act_sel.sem, act_sel.at(S, 1))
                dve.scalar_tensor_tensor(vsd[:], side[:, HPG * KD:], gate[:, 1:2], K("diag"), ALU.mult, ALU.mult)\
                    .then_inc(vsd_ready.sem, 1)

            def rope_selected(S):
                dve.wait_ge(act_sel.sem, act_sel.at(S, 1))
                dve.wait_ge(rope_sum.sem, rope_sum.at(S, TT))
                cs = table("ropeC")[0:KEEP, 0:1].to_broadcast([KEEP, HPG, ROPE])
                sn = table("ropeS")[0:KEEP, 0:1].to_broadcast([KEEP, HPG, ROPE])
                rope(ksraw[:, :, 0:ROPE], cs, sn, ra[0:KEEP, 0:HPG], rb[0:KEEP, 0:HPG]).then_inc(ks_ab.sem, 1)

            def selected_shift(step, S):
                dve.wait_ge(pe_s2.sem, pe_s2.at(S, 1))
                s2 = side.rearrange("p (n k) -> p n k", k=KEEP)
                step(dve.tensor_reduce(n2[:, 0], s2, AX.X, ALU.max, negate=True))
                dve.tensor_tensor(p2[:], s2, n2[:, 0].unsqueeze(2).to_broadcast([P, TT * HPG, KEEP]), ALU.add)\
                    .then_inc(s2_shift.sem, 1)

            def selected_sum(step, S):
                dve.wait_ge(act_e2.sem, act_e2.at(S, 1))
                step(dve.tensor_reduce(n2[:, 1], p2[:], AX.X, ALU.add))
                dve.reciprocal(n2[:, 2], n2[:, 1]).then_inc(n2_ready.sem, 1)

            def row_max(it, u, first):
                dve.wait_ge(scored.sem, scored.at(it, u + 1))
                if u >= 2:
                    dve.wait_ge(weighed.sem, weighed.at(it, u - 1))
                elif not first:
                    dve.wait_ge(weighed.sem, weighed.at(it - 1, NU + u - 1))
                dve.tensor_reduce(nmax[:, u % 2], score_tiles(u), AX.X, ALU.max,
                                  negate=True).then_inc(maxed.sem, 1)

            def one_over(it, u, first=False):
                dve.wait_ge(weighed.sem, weighed.at(it, u + 1))
                if u >= 2:
                    dve.wait_ge(normed.sem, normed.at(it, u - 1))
                elif not first:
                    dve.wait_ge(normed.sem, normed.at(it - 1, NU + u - 1))
                dve.reciprocal(rec[:, u % 2], den[:, u % 2]).then_inc(rec_ready.sem, 1)

            def turned_out(it, u, first=False):
                qt, h = divmod(u, HPG)
                dve.wait_ge(turned.sem, turned.at(it, u + 1))
                if h == 0:
                    if qt >= 2:
                        dve.wait_ge(summed.sem, summed.at(it, qt - 1))
                    elif not first:
                        dve.wait_ge(summed.sem, summed.at(it - 1, qt + 3))
                dve.tensor_copy(turned_tile(qt)[:, h, :, 0:span(u)], turn_tiles(u))\
                    .then_inc(pT_ready.sem, 1)

            def add_share(it, batch):
                rows = rows_of(batch).rearrange("p t c -> p (t c)")
                dve.wait_ge(pe_y.sem, pe_y.at(it, 1))
                if not (isinstance(it, int) and it == 0):
                    dve.wait_ge(x_done.sem, x_done.at(it, 0))
                dve.tensor_tensor(rows, rows, bank(3), ALU.add).then_inc(x_done.sem, 1)

            lg, le = (sq[:, 2 * i:2 * i + 2].rearrange("p a (b e) -> p (a b) e", e=EXPERTS) for i in range(2))

            def router_logits(step, tb):
                dve.wait_ge(pe_lg.sem, pe_lg.at(tb, 1))
                dve.tensor_tensor(lg, side[:, 0:TT * EXPERTS].rearrange("p (t e) -> p t e", t=TT),
                                  brb[:].unsqueeze(1).to_broadcast([P, TT, EXPERTS]), ALU.add).then_inc(lg_read.sem, 1)
                dve.wait_ge(lg_read.sem, lg_read.at(tb, 1))
                step(dve.tensor_reduce(st[:, 44:48], lg, AX.X, ALU.max))
                dve.tensor_tensor(lg, lg, st[:, 44:48].unsqueeze(2).to_broadcast([P, TT, EXPERTS]), ALU.subtract)\
                    .then_inc(lg_ready.sem, 1)

            def router_probs(step, tb):
                dve.wait_ge(act_lg.sem, act_lg.at(tb, 1))
                step(dve.tensor_reduce(st[:, 48:52], le, AX.X, ALU.add))
                step(dve.reciprocal(st[:, 52:56], st[:, 48:52]))
                dve.tensor_tensor(ptok[:], le,
                                  st[:, 52:56].unsqueeze(2).to_broadcast([P, TT, EXPERTS]), ALU.mult)\
                    .then_inc(probs_ready.sem, 1)

            def presort(tb, k):
                if k == 0:
                    dve.wait_ge(act_runs.sem, act_runs.at(tb, 1))
                else:
                    dve.wait_ge(presorted.sem, presorted.at(tb, k))
                tiles = parts if k < MERGE else runs
                if k == MERGE:
                    dve.wait_ge(runs_kept.sem, runs_kept.at(tb, 0))
                    for i in range(2):
                        ins = dve.tensor_copy(runs[0][:, i * T // 2:(i + 1) * T // 2],
                                              parts[0][i * EXPERTS:(i + 1) * EXPERTS, :])
                    ins.then_inc(joined.sem, 1)
                    dve.wait_ge(joined.sem, joined.at(tb, 1))
                compare(dve, tiles[k % 2][:], tiles[1 - k % 2][:], *PASSES[k]).then_inc(presorted.sem, 1)

            def group(b, g, first, last, chains):
                it = b * NG + g
                S = it + 1
                start = first and g == 0
                sides = not (last and g == NG - 1)
                if sides:
                    step_s = Chain(dve, dve_s, S)
                if g == 2 and not last:
                    chains["p"] = Chain(dve, dve_p, b + 1)
                if g == 0 and not first:
                    chains["t"] = Chain(dve, dve_t, b - 1)
                for u in range(NU):
                    if u > 0:
                        one_over(it, u - 1, start)
                    elif not start:
                        one_over(it - 1, NU - 1)
                    row_max(it, u, start)
                    if u >= 2:
                        turned_out(it, u - 2, start)
                    elif not start:
                        turned_out(it - 1, NU + u - 2)
                    if u == 5 and not start:
                        add_share(it - 1, b if g else b - 1)
                    if sides:
                        if u in ROPE_SLOT:
                            rope_heads(S, ROPE_SLOT.index(u))
                        if u == 8:
                            vsd_out(S)
                        if u == 9:
                            rope_selected(S)
                        if u == 12:
                            selected_shift(step_s, S)
                        if u == 14:
                            selected_sum(step_s, S)
                        if g == NG - 1:
                            if u == 0:
                                dve.wait_ge(imp_read.sem, imp_read.at(b + 1, 1))
                            for _ in range(u < 4):
                                top_round(chains["p"])
                            if u == 3:
                                ranks(chains["p"], b + 1)
                            if u == 6:
                                one_hot(chains["p"], b + 1)
                            if u == 7:
                                selT_out(b + 1)
                                chains["p"].close()
                    if g == 0 and not first:
                        step = chains["t"]
                        if u == 5:
                            dve.wait_ge(x_done.sem, x_done.at(it - 1, 1))
                        if 5 <= u < 11:
                            norm(step, rows_of(b - 1), u - 5, x2_ready)
                        if u == 14:
                            router_logits(step, b - 1)
                        if u == 15:
                            router_probs(step, b - 1)
                            step.close()
                    if g == 2 and not last:
                        step = chains["p"]
                        if u == 0 and not first:
                            dve.wait_ge(pe_x2T.sem, pe_x2T.at(b - 1, 1))
                        if u < 6:
                            norm(step, rows_of(b + 1), u, xn_ready)
                        if u == 8:
                            mean_of_batch(step, b + 1)
                        if u == 10:
                            squares(step, b + 1)
                        if u == 11:
                            rope_shared(b + 1)
                            roots(step, (0,))
                        if u == 12:
                            roots(step, (1,))
                            gate_logits(step, b + 1)
                        if u == 13:
                            gates(step, b + 1)
                    if not first and presorts(g, u):
                        for k in range(presorts(g, u)):
                            presort(b - 1, sum(presorts(i // NU, i % NU) for i in range(g * NU + u)) + k)
                if sides:
                    step_s.close()

            step = Chain(dve, dve_p, 0)
            for k in range(6):
                norm(step, rows_of(0), k, xn_ready)
            dve.wait_ge(ld_w.sem, 16 * len(loads))
            dve.tensor_copy(identb[:], ident).then_inc(cast_done.sem, 1)
            dve.tensor_copy(maskb[:], K("mask")).then_inc(cast_done.sem, 1)
            dve.tensor_scalar(gq[:, 1:2], gq[:, 0:1], float(KD) ** -0.5, None, ALU.mult).then_inc(gq_ready.sem, 1)
            mean_of_batch(step, 0)
            squares(step, 0)
            gate_logits(step, 0)
            rope_shared(0)
            roots(step)
            gates(step, 0)
            for t in range(TT):
                if t == 0:
                    dve.wait_ge(k1_ready.sem, k1_ready.at(0, 1))
                rope_heads(0, t)
            dve.wait_ge(imp_read.sem, imp_read.at(0, 1))
            for _ in range(KEEP // 8):
                top_round(step)
            ranks(step, 0)
            one_hot(step, 0)
            selT_out(0)
            step.close()
            vsd_out(0)
            rope_selected(0)
            step = Chain(dve, dve_s, 0)
            selected_shift(step, 0)
            selected_sum(step, 0)
            step.close()
            dve.wait_ge(ld_x_others.sem, 16)
            dve.wait_ge(ld_later.sem, 16 * len(loads_later))
            chains = {}
            for g in range(NG):
                group(0, g, True, False, chains)
            with dve.Fori(1, B - 1) as b:
                for g in range(NG):
                    group(b, g, False, False, chains)
            for g in range(NG):
                group(B - 1, g, False, True, chains)
            it = B * NG - 1
            one_over(it, NU - 1)
            turned_out(it, NU - 2)
            turned_out(it, NU - 1)
            add_share(it, B - 1)
            step = Chain(dve, dve_t, B - 1)
            dve.wait_ge(x_done.sem, x_done.at(it, 1))
            for k in range(6):
                norm(step, rows_of(B - 1), k, x2_ready)
            router_logits(step, B - 1)
            router_probs(step, B - 1)
            step.close()
            for k in range(len(PASSES)):
                presort(B - 1, k)
            dve.wait_ge(spilled.sem, 16 * B)

            step = Chain(dve, dve_r, 0)
            dve.wait_ge(ld_runs.sem, 4 * 16)
            dve.wait_ge(presorted.sem, presorted.at(B - 1, len(PASSES)))
            step(dve.tensor_copy(sortA[EXPERTS:P, (NBLK - 1) * T:], runs[1][:]))
            bufs = [sortA, sortB]
            src, dst = sortA, 1
            size = 2 * T
            while size <= HALF:
                step(compare(dve, src, bufs[dst], size, size // 2))
                src, dst = bufs[dst], 1 - dst
                src, dst = halvings(dve, step, src, dst, bufs, size // 2)
                size *= 2
            other = routed
            step(dve.tensor_copy(other[0:EXPERTS, :], src[EXPERTS:P, :]))
            step(dve.tensor_copy(other[EXPERTS:P, :], src[0:EXPERTS, :]))
            dve.tensor_tensor(bufs[dst][0:EXPERTS, :], src[0:EXPERTS, :], other[0:EXPERTS, ::-1], ALU.max)
            step(dve.tensor_tensor(bufs[dst][EXPERTS:P, :], src[EXPERTS:P, :], other[EXPERTS:P, ::-1], ALU.min))
            src, dst = bufs[dst], 1 - dst
            src, dst = halvings(dve, step, src, dst, bufs, HALF)
            srt = src.rearrange("p (g k) -> p g k", k=GROUP)
            step(dve.tensor_reduce(gsum[:], srt, AX.X, ALU.add))
            step(dve.tensor_copy(glast[:], srt[:, :, GROUP - 1]))
            step(dve.memset(found[:], 0.0))
            n = 0
            for r in range(len(SCORE_ROUNDS)):
                step(dve.tensor_tensor(cand[:].bitcast(I32), cbits[:, r * CAND:(r + 1) * CAND],
                                       found[:, CAND:CAND + 1].bitcast(I32).to_broadcast([P, CAND]), ALU.bitwise_or))
                step(dve.tensor_tensor(gcmp[:], gsum[:].unsqueeze(1).to_broadcast([P, CAND, NGR]),
                                       cand[:].unsqueeze(2).to_broadcast([P, CAND, NGR]), ALU.is_ge))
                dve.tensor_reduce(cnt[:], gcmp[:], AX.X, ALU.add).then_inc(cnt_ready.sem, 1)
                n += 1
                dve.wait_ge(pe_cnt.sem, n)
                step(dve.scalar_tensor_tensor(found[:, 0:CAND], bank(4)[:, 0:CAND], float(BUDGET), cand[:],
                                              ALU.is_ge, ALU.mult))
                step(dve.tensor_reduce(found[:, CAND:CAND + 1], found[:], AX.X, ALU.max))
            kth = rs[:, 0:1]
            step(dve.tensor_copy(kth, found[:, CAND:CAND + 1]))
            step(dve.tensor_scalar(gm[:, 0], gsum[:], kth, None, ALU.is_gt))
            step(dve.tensor_scalar(gm[:, 1], gsum[:], kth, None, ALU.is_equal))
            dve.tensor_reduce(cnt[:, 0:1], gm[:, 0], AX.X, ALU.add).then_inc(cnt_ready.sem, 1)
            n += 1
            dve.wait_ge(pe_cnt.sem, n)
            room = rs[:, 1:2]
            step(dve.tensor_scalar(room, bank(4)[:, 0:1], -1.0, float(BUDGET), ALU.mult, ALU.add))
            step(dve.tensor_scalar(gkey[:], gm[:, 1], -1e6, 1e6, ALU.mult, ALU.add))
            step(dve.tensor_tensor(gkey[:], gkey[:], K("gidx"), ALU.add))
            step(dve.memset(found[:], 0.0))
            for r in range(len(INDEX_ROUNDS)):
                a = CONST["irnd"][0] + r * CAND
                step(dve.tensor_scalar(cand[:], cst[:, a:a + CAND], found[:, CAND:CAND + 1], None, ALU.add))
                step(dve.tensor_tensor(gcmp[:], gkey[:].unsqueeze(1).to_broadcast([P, CAND, NGR]),
                                       cand[:].unsqueeze(2).to_broadcast([P, CAND, NGR]), ALU.is_lt))
                dve.tensor_reduce(cnt[:], gcmp[:], AX.X, ALU.add).then_inc(cnt_ready.sem, 1)
                n += 1
                dve.wait_ge(pe_cnt.sem, n)
                step(dve.scalar_tensor_tensor(found[:, 0:CAND], bank(4)[:, 0:CAND], room, cand[:],
                                              ALU.is_le, ALU.mult))
                step(dve.tensor_reduce(found[:, CAND:CAND + 1], found[:], AX.X, ALU.max))
            step(dve.tensor_scalar(gm[:, 2], gkey[:], found[:, CAND:CAND + 1], None, ALU.is_lt))
            step(dve.tensor_tensor(gm[:, 3], gm[:, 0], gm[:, 2], ALU.add))
            dve.tensor_reduce(cnt[:, 0:1], gm[:, 3], AX.X, ALU.add).then_inc(cnt_ready.sem, 1)
            step(dve.tensor_tensor(gm[:, 0], gm[:, 3], glast[:], ALU.mult))
            step(dve.tensor_scalar(gm[:, 1], gm[:, 3], -BIG, BIG, ALU.mult, ALU.add))
            step(dve.tensor_tensor(gm[:, 2], gm[:, 0], gm[:, 1], ALU.add))
            low = rs[:, 2:3]
            step(dve.tensor_reduce(low, gm[:, 2], AX.X, ALU.min))
            step(dve.tensor_copy(rs[0:EXPERTS, 3:4], rs[EXPERTS:P, 2:3]))
            step(dve.tensor_copy(rs[EXPERTS:P, 3:4], rs[0:EXPERTS, 2:3]))
            step(dve.tensor_tensor(rs[:, 4:5], low, rs[:, 3:4], ALU.min))
            low = rs[:, 4:5]
            n += 1
            dve.wait_ge(pe_cnt.sem, n)
            step(dve.tensor_scalar(rs[:, 5:6], bank(4)[:, 0:1], float(GROUP), None, ALU.mult))
            dve.tensor_scalar(above, score, low, None, ALU.is_gt).then_inc(above_ready.sem, 1)
            step(dve.tensor_scalar(equal, score, low, None, ALU.is_equal))
            dve.tensor_reduce(cnt[:, 1:2], equal, AX.X, ALU.add).then_inc(cnt_ready.sem, 1)
            n += 1
            higher = routed
            step(dve.scalar_tensor_tensor(higher, score, low, score, ALU.is_gt, ALU.mult))
            dve.wait_ge(pe_cnt.sem, n)
            step(dve.tensor_copy(rs[:, 7:8], bank(4)[:, 1:2]))
            step(dve.tensor_tensor_scan(sortA, equal, equal, rs[:, 7:8], ALU.add, ALU.max))
            dve.wait_ge(pe_cnt.sem, n + 1)
            step(dve.tensor_tensor(rs[:, 6:7], rs[:, 5:6], bank(5)[:, 0:1], ALU.subtract))
            for c in (slice(0, T), slice(T, HALF)):
                step(dve.scalar_tensor_tensor(sortB[:, c], sortA[:, c], rs[:, 6:7], equal[:, c], ALU.is_le, ALU.mult))
                dve.scalar_tensor_tensor(routed[:, c], sortB[:, c], low, higher[:, c], ALU.mult, ALU.add)\
                    .then_inc(routed_ready.sem, 1)

            def split(jj, half, k, rows_of_block=None):
                rows = slice(half * EXPERTS, (half + 1) * EXPERTS)
                f = rows_of_block if rows_of_block is not None else fblk[half][rows, :]
                r1, r2 = frest[0][rows], frest[1][rows]
                n = half * 4 + k
                if k == 0 and rows_of_block is None:
                    dve.wait_ge(fblk_ready.sem, fblk_ready.at(jj, half + 1))
                if k == 0:
                    dve.tensor_copy(fpart[rows, 0], f).then_inc(fsplit.sem, 1)
                if k == 1:
                    dve.wait_ge(fsplit.sem, fsplit.at(jj, n))
                    dve.tensor_tensor(r1, f, fpart[rows, 0], ALU.subtract).then_inc(fsplit.sem, 1)
                if k == 2:
                    dve.wait_ge(fsplit.sem, fsplit.at(jj, n))
                    dve.tensor_copy(fpart[rows, 1], r1).then_inc(fsplit.sem, 1)
                if k == 3:
                    dve.wait_ge(fsplit.sem, fsplit.at(jj, n))
                    dve.tensor_tensor(r2, r1, fpart[rows, 1], ALU.subtract).then_inc(fsplit.sem, 1)
                if k == 4:
                    dve.wait_ge(fsplit.sem, fsplit.at(jj, n))
                    dve.tensor_copy(fpart[rows, 2], r2).then_inc(fpart_ready.sem, 1)

            def block_of(jj, last):
                step = Chain(dve, dve_e, jj)
                for n in range(2 * HT):
                    half, m = divmod(n, HT)
                    dve.wait_ge(pe_gt.sem, pe_gt.at(jj, n + 1))
                    dve.wait_ge(act_up.sem, act_up.at(jj, n + 1))
                    dve.scalar_tensor_tensor(gateT[:, n % 2], bank(2 + n % 2), bgt[:, m:m + 1], siluT[:, n % 2],
                                             ALU.add, ALU.mult).then_inc(gate_mul.sem, 1)
                    dve.wait_ge(pe_f.sem, pe_f.at(jj, n + 1))
                    dve.wait_ge(gate_mul.sem, gate_mul.at(jj, n + 1))
                    if n >= 2:
                        dve.wait_ge(pe_dn.sem, pe_dn.at(jj, n - 1))
                    else:
                        dve.wait_ge(pe_dn.sem, pe_dn.at(jj, 0))
                    dve.tensor_tensor(hT[:, n % 2], gateT[:, n % 2], bank(4 + n % 2), ALU.mult)\
                        .then_inc(h_ready.sem, 1)
                    if 2 <= m < 7 and half == 0:
                        split(jj, 1, m - 2)
                    if 2 <= m < 7 and half == 1 and not last:
                        split(jj + 1, 0, m - 2)
                    if m == HT - 1:
                        dve.wait_ge(pe_dn.sem, pe_dn.at(jj, n + 1))
                        dve.wait_ge(stored.sem, stored.at(jj, 0))
                        step(dve.tensor_scalar(yrec[:, 0], bank(7)[:, 0:TT], EPS_DEN, None, ALU.add))
                        step(dve.reciprocal(yrec[:, 1], yrec[:, 0]))
                        dve.tensor_tensor(yout[half][:], bank(6).rearrange("p (t c) -> p t c", t=TT),
                                          yrec[:, 1].unsqueeze(2).to_broadcast([P, TT, C]), ALU.mult)\
                            .then_inc(y_scaled.sem, 1)
                step.close()

            dve.wait_ge(routed_ready.sem, 1)
            for k in range(5):
                split(0, 0, k, routed[0:EXPERTS, 0:T])
            with dve.Fori(0, NBLK - 1) as jj:
                block_of(jj, False)
            block_of(NBLK - 1, True)


def presorts(g, u):
    return {0: [0] * NU,
            1: [0, 0, 1, 3, 3, 1, 3, 1, 1, 1, 1, 1, 1, 1, 1, 1],
            2: [1, 0, 0, 2, 2, 0, 3, 1, 1, 2, 0, 0, 0, 0, 0, 0],
            3: [1, 0, 0, 0, 2, 1, 2, 1, 1, 1, 1, 1, 1, 1, 0, 0]}[g][u]


def compare(dve, src, dst, size, d):
    k = size if 2 * d == size else 2 * d
    a = src.rearrange("p (n k) -> p n k", k=k)
    o = dst.rearrange("p (n k) -> p n k", k=k)
    lo, hi = a[:, :, 0:d], a[:, :, d:2 * d]
    if 2 * d == size:
        hi = hi[:, :, ::-1]
    dve.tensor_tensor(o[:, :, 0:d], lo, hi, ALU.max)
    return dve.tensor_tensor(o[:, :, d:2 * d], lo, hi, ALU.min)


def halvings(dve, step, src, dst, bufs, size):
    d = size // 2
    while d >= 1:
        step(compare(dve, src, bufs[dst], 0, d))
        src, dst = bufs[dst], 1 - dst
        d //= 2
    return src, dst


def constants():
    f = (np.float32(1.0) / np.float32(10000.0) ** (np.arange(0, ROPE, 2, dtype=np.float32) / np.float32(ROPE)))
    a = np.outer(np.arange(T, dtype=np.float32), f.astype(np.float32)).astype(np.float32)
    cos, sin = np.cos(a), np.sin(a)
    lane = np.arange(P)
    tiles = lambda m: m.reshape(TT, P, -1).transpose(1, 0, 2).reshape(P, -1)
    parts = {
        "ident": np.eye(P),
        "mask": np.where(lane[None, :] > lane[:, None], MASKED, 0.0),
        "ropeC": tiles(np.concatenate([cos, cos], 1)),
        "ropeS": tiles(np.concatenate([-sin, sin], 1)),
        "diag": (lane[:, None] // KEEP == lane[None, :] // VD) * 1.0,
        "count": np.tile(np.arange(1, KEEP + 1), (P, 1)),
        "pair": (lane[:, None] % EXPERTS == lane[None, :] % EXPERTS) * 1.0,
        "lower": (lane[None, :] == lane[:, None] + EXPERTS) * 1.0,
        "ones": np.ones((P, P)),
        "half": (lane[:, None] // EXPERTS == np.arange(2)[None, :]) * 1.0,
        "gidx": ((lane[:, None] // EXPERTS) * NGR + np.arange(NGR)[None, :]) * EXPERTS + lane[:, None] % EXPERTS,
        "irnd": np.tile(np.concatenate([np.arange(1, CAND + 1) << s for s in INDEX_ROUNDS]), (P, 1)),
    }
    cst = np.zeros((P, NCONST), np.float32)
    for name, (i, j) in CONST.items():
        cst[:, i:j] = parts[name]
    bits = np.tile(np.concatenate([np.arange(1, CAND + 1) << s for s in SCORE_ROUNDS]), (P, 1)).astype(np.int32)
    expert = np.arange(HT)[:, None] * EPT + lane[None, :] // HID
    sel = (np.arange(3 * SORT)[:, None, None] % SORT == expert[None] % SORT) * 1.0
    return cst, bits, sel


def kernel(**inputs):
    import ml_dtypes
    import concourse.bacc as _bacc
    from concourse.bass_utils import run_bass_kernel_spmd as _run

    w = {k: np.asarray(v) for k, v in inputs.items()}
    A = lambda n: w["L0_attn_" + n]
    F = lambda n: w["L0_ffn_" + n]
    cst, bits, sel = constants()

    def rope_first(m):
        m = m.reshape(C, NH, KD)
        return np.concatenate([m[:, :, NOPE:], m[:, :, :NOPE]], 2).reshape(C, NH * KD)

    arrays = {
        "x": A("x").reshape(NTOK, C),
        "w_cat": np.concatenate([A("w_cq"), A("w_ckv"), A("w_krope")], 1),
        "w_imp": A("w_imp"), "w_gate": A("w_gate"),
        "g_q": A("g_qnorm").reshape(QL, 1), "g_kv": A("g_kvnorm").reshape(KVL, 1),
        "w_q": np.concatenate([A("w_dq_rope").reshape(QL, NH, ROPE), A("w_dq_nope").reshape(QL, NH, NOPE)], 2),
        "dqn_t": A("w_dq_nope").reshape(QL, NH, NOPE).transpose(2, 1, 0).reshape(NOPE, NH * QL),
        "dkn_t": A("w_dk_nope").reshape(KVL, NH, NOPE).transpose(2, 1, 0).reshape(NOPE, NH * KVL),
        "w_dv": A("w_dv"), "w_wink": rope_first(A("w_wink")), "w_winv": A("w_winv"),
        "w_selk": rope_first(A("w_selk")), "w_selv": A("w_selv"), "w_proj": A("w_proj"),
        "w_r": F("Wr"), "b_r": F("br").reshape(EXPERTS),
        "w_up": F("Wup").transpose(1, 0, 2).reshape(C, EXPERTS * HID), "b_up": F("bup").reshape(HT, P).T,
        "w_gt": F("Wgate").transpose(1, 0, 2).reshape(C, EXPERTS * HID), "b_gt": F("bgate").reshape(HT, P).T,
        "w_dn": F("Wdown").reshape(EXPERTS * HID, C), "b_dn": F("bdown"),
        "consts": cst, "bits": bits, "select": sel.astype(ml_dtypes.bfloat16),
    }
    nc = _bacc.Bacc("TRN2", target_bir_lowering=False, num_devices=1)
    args, sent = [], {}
    for name, a in arrays.items():
        a = np.ascontiguousarray(a)
        sent["in_" + name] = a
        args.append(nc.dram_tensor("in_" + name, a.shape, mybir.dt.from_np(a.dtype), kind="ExternalInput").ap())
    out = nc.dram_tensor("out_x", (NTOK, C), F32, kind="ExternalOutput").ap()
    build(nc, *args, out)
    r = _run(nc, [sent], core_ids=[0])
    return r.results[0]["out_x"].reshape(B, T, C)
```
